# Optimizing a Trainium2 kernel written in Bass

```python
import numpy as np
import jax
import jax.numpy as jnp

def _softmax(x, axis=-1):
    return jax.nn.softmax(x, axis=axis)

def _gelu(x):
    return jax.nn.gelu(x, approximate=True)

def _silu(x):
    return jax.nn.silu(x)

def _sigmoid(x):
    return jax.nn.sigmoid(x)

def _layernorm(x, axis=-1, eps=1e-05):
    m = jnp.mean(x, axis=axis, keepdims=True)
    v = jnp.var(x, axis=axis, keepdims=True)
    return (x - m) / jnp.sqrt(v + eps)

def _scatter_add(tgt, idx, src, axis=0):
    return tgt.at[idx].add(src)

def _segment_sum(src, seg, n):
    return jax.ops.segment_sum(src, seg, n)
kernel_name = 'mk_adaln_ffn_d2_seqx_r8_b1fe20'

def setup_inputs(seed: int=0):
    np.random.seed(seed)
    _w = jnp.asarray

    def _rec_inputs():
        import jax
        import jax.numpy as jnp
        _rk = jax.random.key(seed)
        x = -0.000125 + 0.9999 * jax.random.normal(jax.random.fold_in(_rk, 1), (8, 128, 512), jnp.float32)
        _lenS = 128 - jax.random.randint(jax.random.fold_in(_rk, 7), (8,), 0, max(1, 128 // 4) + 1, jnp.int32)
        _lenS2 = 128 - jax.random.randint(jax.random.fold_in(_rk, 8), (8,), 0, max(1, 128 // 4) + 1, jnp.int32)
        itok_B_3_7 = jax.random.randint(jax.random.fold_in(_rk, 11), (8,), 3, 8, jnp.int32)
        itok_B_1_7 = jax.random.randint(jax.random.fold_in(_rk, 12), (8,), 1, 8, jnp.int32)
        return (x, itok_B_3_7, itok_B_1_7)
    x, itok_B_3_7, itok_B_1_7 = _rec_inputs()

    def _L0_cond_setup():
        import jax, jax.numpy as jnp
        import numpy as np
        MAX_LORAS, OUT, IN = (8, 512, 512)
        B, S = (4, 256)
        key = jax.random.key(seed)
        k1, k2, k3 = jax.random.split(key, 3)
        x = jax.random.normal(k1, (B, S, IN), dtype=jnp.float32)
        weight = jax.random.normal(k2, (MAX_LORAS, OUT, IN), dtype=jnp.float32) * 0.02
        adapter_ids = jax.random.randint(k3, (B,), 0, MAX_LORAS, dtype=jnp.int32)
        return {'x': x, 'weight': weight, 'adapter_ids': adapter_ids}
    _L0_cond_all = _L0_cond_setup()
    _L0_cond_in = {k: v for k, v in _L0_cond_all.items() if k in ('weight',)}
    del _L0_cond_all

    def _L0_ffn_setup():
        import jax, jax.numpy as jnp
        import numpy as np
        LORA_RANK = 16
        LORA_ALPHA = 16
        LORA_SCALE = LORA_ALPHA / LORA_RANK
        key = jax.random.key(seed)
        k1, k2, k3, k4, k5 = jax.random.split(key, 5)
        B, S, D_IN, D_OUT, N_LORA, R = (8, 256, 512, 512, 3, LORA_RANK)
        std = 1.0 / np.sqrt(D_IN)
        x = jax.random.normal(k1, (B, S, D_IN), dtype=jnp.float32)
        weight = jax.random.truncated_normal(k2, -3.0, 3.0, (D_OUT, D_IN), dtype=jnp.float32) * std
        bias = jax.random.normal(k3, (D_OUT,), dtype=jnp.float32) * 0.01
        lora_A = jax.random.normal(k4, (N_LORA, R, D_IN), dtype=jnp.float32) * std
        lora_B = jax.random.normal(k5, (N_LORA, D_OUT, R), dtype=jnp.float32) * 0.02
        lora_start_indices = jnp.arange(4, dtype=jnp.int64) * 2
        return {'x': x, 'weight': weight, 'bias': bias, 'lora_A': lora_A, 'lora_B': lora_B, 'lora_start_indices': lora_start_indices}
    _L0_ffn_all = _L0_ffn_setup()
    _L0_ffn_in = {k: v for k, v in _L0_ffn_all.items() if k in ('weight', 'bias', 'lora_A', 'lora_B', 'lora_start_indices')}
    del _L0_ffn_all

    def _L1_cond_setup():
        import jax, jax.numpy as jnp
        import numpy as np
        B, S, D_IN, D_OUT = (4, 256, 512, 512)
        N_ADAPTERS, MAX_RANK = (8, 16)
        key = jax.random.key(seed)
        ks = jax.random.split(key, 7)
        x = jax.random.normal(ks[0], (B, S, D_IN), dtype=jnp.float32)
        weight = jax.random.normal(ks[1], (D_OUT, D_IN), dtype=jnp.float32) * (1.0 / np.sqrt(D_IN))
        bias = jax.random.normal(ks[2], (D_OUT,), dtype=jnp.float32) * 0.01
        lora_a_weights = jax.random.normal(ks[3], (N_ADAPTERS, MAX_RANK, D_IN), dtype=jnp.float32) * (1.0 / np.sqrt(D_IN))
        lora_b_weights = jax.random.normal(ks[4], (N_ADAPTERS, D_OUT, MAX_RANK), dtype=jnp.float32) * 0.02
        scaling_factors = jax.random.uniform(ks[5], (N_ADAPTERS,), dtype=jnp.float32, minval=0.5, maxval=2.0)
        adapter_id = jax.random.randint(ks[6], (B,), 0, N_ADAPTERS, dtype=jnp.int64)
        return {'x': x, 'weight': weight, 'bias': bias, 'lora_a_weights': lora_a_weights, 'lora_b_weights': lora_b_weights, 'scaling_factors': scaling_factors, 'adapter_id': adapter_id}
    _L1_cond_all = _L1_cond_setup()
    _L1_cond_in = {k: v for k, v in _L1_cond_all.items() if k in ('weight', 'bias', 'lora_a_weights', 'lora_b_weights', 'scaling_factors')}
    del _L1_cond_all

    def _L1_ffn_setup():
        import jax, jax.numpy as jnp
        import numpy as np
        NUM_EXPERTS = 8
        RANK = 32
        ALPHA = 16.0
        TOP_K = 2
        TEMPERATURE = 1.0
        GAMMA = 0.5
        SOFT_TOPK_TEMP = 0.5
        N_GRAM = 2
        EPS = 1e-06
        key = jax.random.key(seed)
        ks = jax.random.split(key, 6)
        d_in, d_out = (512, 512)
        Bsz, T = (4, 256)
        x = jax.random.normal(ks[0], (Bsz, T, d_in), dtype=jnp.float32)
        W = jax.random.normal(ks[1], (d_out, d_in), dtype=jnp.float32) / np.sqrt(d_in)
        b = jax.random.normal(ks[2], (d_out,), dtype=jnp.float32) * 0.01
        A = jax.random.normal(ks[3], (d_in, RANK), dtype=jnp.float32) / np.sqrt(d_in)
        Bmat = jax.random.normal(ks[4], (RANK, d_out), dtype=jnp.float32) * 0.01
        LiMEs = jax.random.normal(ks[5], (NUM_EXPERTS, RANK), dtype=jnp.float32) * 0.1
        return {'x': x, 'W': W, 'b': b, 'A': A, 'Bmat': Bmat, 'LiMEs': LiMEs}
    _L1_ffn_all = _L1_ffn_setup()
    _L1_ffn_in = {k: v for k, v in _L1_ffn_all.items() if k in ('W', 'b', 'A', 'Bmat', 'LiMEs')}
    del _L1_ffn_all
    return {'x': x, 'itok_B_3_7': itok_B_3_7, 'itok_B_1_7': itok_B_1_7, 'L0_cond_weight': _L0_cond_in['weight'], 'L0_ffn_weight': _L0_ffn_in['weight'], 'L0_ffn_bias': _L0_ffn_in['bias'], 'L0_ffn_lora_A': _L0_ffn_in['lora_A'], 'L0_ffn_lora_B': _L0_ffn_in['lora_B'], 'L0_ffn_lora_start_indices': _L0_ffn_in['lora_start_indices'], 'L1_cond_weight': _L1_cond_in['weight'], 'L1_cond_bias': _L1_cond_in['bias'], 'L1_cond_lora_a_weights': _L1_cond_in['lora_a_weights'], 'L1_cond_lora_b_weights': _L1_cond_in['lora_b_weights'], 'L1_cond_scaling_factors': _L1_cond_in['scaling_factors'], 'L1_ffn_W': _L1_ffn_in['W'], 'L1_ffn_b': _L1_ffn_in['b'], 'L1_ffn_A': _L1_ffn_in['A'], 'L1_ffn_Bmat': _L1_ffn_in['Bmat'], 'L1_ffn_LiMEs': _L1_ffn_in['LiMEs']}

def reference(x, itok_B_3_7, itok_B_1_7, L0_cond_weight, L0_ffn_weight, L0_ffn_bias, L0_ffn_lora_A, L0_ffn_lora_B, L0_ffn_lora_start_indices, L1_cond_weight, L1_cond_bias, L1_cond_lora_a_weights, L1_cond_lora_b_weights, L1_cond_scaling_factors, L1_ffn_W, L1_ffn_b, L1_ffn_A, L1_ffn_Bmat, L1_ffn_LiMEs):
    import jax
    import jax.numpy as jnp

    def _L0_cond_ref(x, weight, adapter_ids):
        import jax, jax.numpy as jnp
        import numpy as np
        MAX_LORAS, OUT, IN = (8, 512, 512)
        B, S = (4, 256)
        w = weight[adapter_ids]
        return jnp.einsum('bsi,boi->bso', x, w)

    def _L0_ffn_ref(x, weight, bias, lora_A, lora_B, lora_start_indices):
        import jax, jax.numpy as jnp
        import numpy as np
        LORA_RANK = 16
        LORA_ALPHA = 16
        LORA_SCALE = LORA_ALPHA / LORA_RANK
        y = jnp.einsum('bsd,od->bso', x, weight) + bias
        B = x.shape[0]
        seg = jnp.searchsorted(lora_start_indices, jnp.arange(B), side='right') - 1
        adapter_idx = jnp.clip(seg - 1, 0, lora_A.shape[0] - 1)
        A = lora_A[adapter_idx]
        Bw = lora_B[adapter_idx]
        lo = jnp.einsum('bsr,bor->bso', jnp.einsum('bsd,brd->bsr', x, A), Bw) * LORA_SCALE
        use_lora = (seg > 0)[:, None, None]
        return y + jnp.where(use_lora, lo, jnp.zeros((), dtype=y.dtype))

    def _L1_cond_ref(x, weight, bias, lora_a_weights, lora_b_weights, scaling_factors, adapter_id):
        import jax, jax.numpy as jnp
        import numpy as np
        B, S, D_IN, D_OUT = (4, 256, 512, 512)
        N_ADAPTERS, MAX_RANK = (8, 16)
        base = jnp.einsum('bsi,oi->bso', x, weight) + bias
        a_sel = lora_a_weights[adapter_id]
        b_sel = lora_b_weights[adapter_id]
        scale = scaling_factors[adapter_id]
        low = jnp.einsum('bsi,bri->bsr', x, a_sel)
        delta = jnp.einsum('bsr,bor->bso', low, b_sel)
        return base + scale[:, None, None] * delta

    def _L1_ffn_ref(x, W, b, A, Bmat, LiMEs):
        import jax, jax.numpy as jnp
        import numpy as np
        NUM_EXPERTS = 8
        RANK = 32
        ALPHA = 16.0
        TOP_K = 2
        TEMPERATURE = 1.0
        GAMMA = 0.5
        SOFT_TOPK_TEMP = 0.5
        N_GRAM = 2
        EPS = 1e-06
        Bsz, T, d_in = x.shape
        E = LiMEs.shape[0]
        scaling = ALPHA / RANK
        H = jnp.einsum('btd,od->bto', x, W) + b
        z = jnp.einsum('btd,dr->btr', x, A)
        anchors = jnp.arange(N_GRAM - 1, T, N_GRAM)
        H_slice = H[:, anchors, :E]
        delta_slice = jnp.einsum('bar,er->bae', z[:, anchors], LiMEs)
        H_scale = jnp.maximum(jnp.max(jnp.abs(H_slice)), EPS)
        d_scale = jnp.maximum(jnp.max(jnp.abs(delta_slice)), EPS)
        logits = ((1.0 - GAMMA) * (H_slice / H_scale) + GAMMA * (delta_slice / d_scale)) / TEMPERATURE
        probs = jax.nn.softmax(logits, axis=-1)
        topk_vals, _ = jax.lax.top_k(probs, TOP_K)
        thresh = topk_vals[..., -1:]
        mask = jax.nn.sigmoid((probs - thresh) / SOFT_TOPK_TEMP)
        weights = probs * mask
        weights = weights / (jnp.sum(weights, axis=-1, keepdims=True) + 1e-09)
        weights_full = jnp.repeat(weights, N_GRAM, axis=1)
        p_mix = jnp.einsum('bte,er->btr', weights_full, LiMEs)
        delta = jnp.einsum('btr,ro->bto', z * p_mix, Bmat) * scaling
        return H + delta
    x = x + _L0_ffn_ref(_L0_cond_ref(x, L0_cond_weight, itok_B_3_7), L0_ffn_weight, L0_ffn_bias, L0_ffn_lora_A, L0_ffn_lora_B, L0_ffn_lora_start_indices)
    x = x + _L1_ffn_ref(_L1_cond_ref(x, L1_cond_weight, L1_cond_bias, L1_cond_lora_a_weights, L1_cond_lora_b_weights, L1_cond_scaling_factors, itok_B_1_7), L1_ffn_W, L1_ffn_b, L1_ffn_A, L1_ffn_Bmat, L1_ffn_LiMEs)
    return x

_drawn_inputs = setup_inputs


def setup_inputs(seed=0):
    import zlib

    import numpy as np

    out = dict(_drawn_inputs(seed))
    spreads = {}
    factors = {'L0_ffn_bias': 6.984,
     'L1_cond_bias': 8.0,
     'L1_cond_scaling_factors': 3.12,
     'L1_ffn_b': 8.0,
     'L1_ffn_A': 8.0,
     'L1_ffn_Bmat': 8.0,
     'L1_ffn_LiMEs': 8.0}
    for name, (base, spread) in spreads.items():
        noise = np.random.default_rng([zlib.crc32(name.encode()), seed]).standard_normal(out[name].shape)
        drawn = base * np.exp(spread * noise) if base else spread * noise
        out[name] = jnp.asarray(drawn.astype(out[name].dtype))
    for name, factor in factors.items():
        out[name] = (out[name] * factor).astype(out[name].dtype)
    return out
```

```python
from contextlib import ExitStack

import concourse.bass as bass
from concourse import mybir

F32 = mybir.dt.float32
F32R = mybir.dt.float32r
I32 = mybir.dt.int32
ALU = mybir.AluOpType
ACT = mybir.ActivationFunctionType
AX = mybir.AxisListType

P = 128
Q = 32
EPS = 1e-6
GAMMA = 0.5
SOFT_TOPK_TEMP = 0.5
ALPHA = 16.0


def build(nc, x, id0, id1, W0, W1, bias1, A0, B0, starts, W2, b2, a1, B1, s1, W3, b3, A, Bmat, L, out):
    NB, S, D = x.shape
    NW = W0.shape[0]
    C = D // P
    TB = D // Q
    NL0, R0, _ = A0.shape
    NL1, R1, _ = a1.shape
    K0 = NL0 * R0
    K1 = NL1 * R1
    R = A.shape[1]
    NE = L.shape[0]
    NS = R + 2 * NE
    NP = NB // 2
    SCALING = ALPHA / R
    assert S == P and K1 == P and 2 * K0 <= P and D == 512 and 4 * R == P and NB % 2 == 0

    ctx = ExitStack()
    with ctx, nc.allow_non_contiguous_dma(reason="three vectors of a few hundred values"):
        def sb(name, shape, dt=F32):
            return ctx.enter_context(nc.sbuf_tensor(name, shape, dt))

        def sem(name):
            return ctx.enter_context(nc.semaphore(name))

        RING = 2
        w_in = sb("w_in", [P, RING, C * D])
        w_t = sb("w_t", [P, C * D])
        w_hi = sb("w_hi", [P, 2, C, D], F32R)
        w_lo = sb("w_lo", [P, 2, C, D], F32R)
        w1_hi = sb("w1_hi", [P, C, D], F32R)
        w1_lo = sb("w1_lo", [P, C, D], F32R)
        x_in = sb("x_in", [P, 2 * D])
        x_t = sb("x_t", [P, 3, 2 * D])
        x_hi = sb("x_hi", [P, 2, C, 2 * S], F32R)
        x_lo = sb("x_lo", [P, 2, C, 2 * S], F32R)
        c0_row = sb("c0_row", [P, 2, D])
        c0_hi = sb("c0_hi", [P, 2, C, 2 * S], F32R)
        c0_lo = sb("c0_lo", [P, 2, C, 2 * S], F32R)
        x1_t = sb("x1_t", [P, C, 2 * S])
        x1_hi = sb("x1_hi", [P, NP, C, 2 * S], F32R)
        x1_lo = sb("x1_lo", [P, NP, C, 2 * S], F32R)
        low0_hi = sb("low0_hi", [2 * K0, 2 * S], F32R)
        low0_lo = sb("low0_lo", [2 * K0, 2 * S], F32R)
        low1_hi = sb("low1_hi", [P, NB, S], F32R)
        low1_lo = sb("low1_lo", [P, NB, S], F32R)
        a0_t = sb("a0_t", [P, C, 2 * K0], F32R)
        b0_hi = sb("b0_hi", [2 * K0, D], F32R)
        b0_lo = sb("b0_lo", [2 * K0, D], F32R)
        a1_hi = sb("a1_hi", [P, C, K1], F32R)
        a1_lo = sb("a1_lo", [P, C, K1], F32R)
        b1_row = sb("b1_row", [P, C, K1])
        b1_hi = sb("b1_hi", [P, C, K1], F32R)
        b1_lo = sb("b1_lo", [P, C, K1], F32R)
        be_hi = sb("be_hi", [K1, D], F32R)
        be_lo = sb("be_lo", [K1, D], F32R)
        small = sb("small", [P, C, NS])
        ae = sb("ae", [P, C, 2 * NS], F32R)
        bes = sb("bes", [K1, 2 * NS], F32R)
        l_t = sb("l_t", [R, NE])
        l_rep = sb("l_rep", [NB * NE, R])
        l_diag = sb("l_diag", [NB * NE, NB, R])
        bm_parts = sb("bm_parts", [P, D], F32R)
        bias_all = sb("bias_all", [P, D])
        bias_small = sb("bias_small", [P, NS])
        bias1_c = sb("bias1_c", [P, C])
        b2_c = sb("b2_c", [P, C])
        b2_hi = sb("b2_hi", [P, C], F32R)
        b2_lo = sb("b2_lo", [P, C], F32R)
        s_c = sb("s_c", [P, 1])
        ident = sb("ident", [P, P])
        ident_r = sb("ident_r", [P, P], F32R)
        ones2 = sb("ones2", [2, P])
        ids_i = sb("ids_i", [P, NB], I32)
        starts_i = sb("starts_i", [P, NL0 + 1], I32)
        iota_i = sb("iota_i", [P, 1 + NB], I32)
        part_f = sb("part_f", [P, 1])
        group_f = sb("group_f", [P, 3])
        ids_f = sb("ids_f", [P, NB])
        starts_f = sb("starts_f", [P, NL0 + 1])
        batch_f = sb("batch_f", [P, NB])
        seg_f = sb("seg_f", [P, NB])
        started = sb("started", [P, NB, NL0 + 1])
        mask0 = sb("mask0", [P, NB])
        mask1 = sb("mask1", [P, NB])
        top = sb("top", [P, 2])
        r2 = sb("r2", [2, 2])
        r2d = sb("r2d", [2, 2])
        r_b = sb("r_b", [P, 2])
        lg = sb("lg", [P, NB, NE])
        lgd = sb("lgd", [P, NB, NE])
        mx = sb("mx", [P, NB, 8])
        sub = sb("sub", [P, NB, NE + 1])
        ex = sb("ex", [P, NB, NE + 1])
        prob = sb("prob", [P, NB, NE + 1])
        gate = sb("gate", [P, NB, NE])
        wgt = sb("wgt", [P, NB, NE])
        tot = sb("tot", [P, 4, NB])
        zp_hi = sb("zp_hi", [P, NB, R], F32R)
        x1_flat = x1_t[:].rearrange("p c s -> p (c s)")
        a0_in, a0_row = x1_flat[0:K0, 0:D], c0_row[0:K0, 1]
        a1_in, a1_row = x1_flat[:, D:2 * D], x_t[:, 1, 0:D]
        b0_in = x_t[:, 1, D:D + C * K0].rearrange("p (c n r) -> p c n r", c=C, n=NL0)
        b0_row = c0_row[:, 0, 0:C * 2 * K0].rearrange("p (c g k) -> p c g k", c=C, g=2)
        a_t = x_t[0:R, 2, 0:D].rearrange("p (c k) -> p c k", k=P)
        bm4 = x_t[:, 2, D:2 * D]
        be_f = x_t[:, 1, 0:D + NS]
        ae_f = x_t[:, 1, D + NS:D + NS + C * NS].rearrange("p (c n) -> p c n", n=NS)
        small_parts = x_hi[:, 0, :, 0:2 * NS]
        zr = x_in[:, 0:NB * NS].rearrange("p (b n) -> p b n", n=NS)
        zp = x_in[:, NB * NS:NB * (NS + R)].rearrange("p (b r) -> p b r", r=R)
        w_tok = x_in[0:NB * NE, NB * (NS + R):NB * (NS + R) + S]
        m_hi, m_lo = w1_hi, w1_lo
        zs = w_t[:, 0:NB * P].rearrange("p (b g r) -> p b g r", b=NB, g=4)
        z_parts = c0_hi[:, 0].rearrange("p c s -> p (c s)").rearrange("p (b s) -> p b s", b=NB)
        out_sb = w_in[:, 1].rearrange("p (n d) -> p n d", d=D)

        bank = [ctx.enter_context(nc.psum_tensor(f"bank{n}", [P, D], F32)) for n in range(8)]

        ld = {n: sem("landed_" + n) for n in
              ("a0", "b0", "a1", "b1", "A", "l", "lr", "bm", "bias", "b1c", "b2c", "s", "ids", "starts")}
        w_landed = [sem(f"w_landed{n}") for n in range(RING)]
        x_landed = sem("x_landed")
        out_stored = [sem(f"out_stored{n}") for n in range(4)]
        ident_zero, ident_done, iota_done = sem("ident_zero"), sem("ident_done"), sem("iota_done")
        ones_done, ldiag_step = sem("ones_done"), sem("ldiag_step")
        rows_ready = sem("rows_ready")
        ident_r_done, bm_hi_done, bm_done = sem("ident_r_done"), sem("bm_hi_done"), sem("bm_done")
        mask_step, masks_done = sem("mask_step"), sem("masks_done")
        aux_ready, aux_hi, aux_lo = sem("aux_ready"), sem("aux_hi"), sem("aux_lo")
        b1_hi_done, b1_lo_done = sem("b1_hi_done"), sem("b1_lo_done")
        w_turned, w_hi_done, w_lo_done = sem("w_turned"), sem("w_hi_done"), sem("w_lo_done")
        w1_turned, w1_hi_done, w1_lo_done = sem("w1_turned"), sem("w1_hi_done"), sem("w1_lo_done")
        x_turned, x_hi_done, x_lo_done = sem("x_turned"), sem("x_hi_done"), sem("x_lo_done")
        c0_ready, c0_saved = sem("c0_ready"), sem("c0_saved")
        c0t_ready, c0t_hi_done, c0t_lo_done = sem("c0t_ready"), sem("c0t_hi_done"), sem("c0t_lo_done")
        low0_ready, low0_hi_done, low0_lo_done = sem("low0_ready"), sem("low0_hi_done"), sem("low0_lo_done")
        low1_ready, low1_hi_done, low1_lo_done = sem("low1_ready"), sem("low1_hi_done"), sem("low1_lo_done")
        y_ready, x1_summed = sem("y_ready"), sem("x1_summed")
        x1_hi_done, x1_lo_done = sem("x1_hi_done"), sem("x1_lo_done")
        small_done, w3_small_done = sem("small_done"), sem("w3_small_done")
        w3t_ready, w3_hi_done, w3_lo_done = sem("w3t_ready"), sem("w3_hi_done"), sem("w3_lo_done")
        bias_ready, be_ready, smalls_ready = sem("bias_ready"), sem("be_ready"), sem("smalls_ready")
        bias_done, be_scaled, be_done, ae_saved = sem("bias_done"), sem("be_scaled"), sem("be_done"), sem("ae_saved")
        w2_hi_done, w2_lo_done, ae_summed = sem("w2_hi_done"), sem("w2_lo_done"), sem("ae_summed")
        small_hi_done, small_lo_done = sem("small_hi_done"), sem("small_lo_done")
        ae_done, bsm_step = sem("ae_done"), sem("bsm_step")
        m_ready, m_hi_done, m_lo_done = sem("m_ready"), sem("m_hi_done"), sem("m_lo_done")
        zr_ready, zr_step, zr_done = sem("zr_ready"), sem("zr_step"), sem("zr_done")
        top_done, topt_ready, r_step, r_done = sem("top_done"), sem("topt_ready"), sem("r_step"), sem("r_done")
        rb_ready, lg_step, sub_done, ex_done = sem("rb_ready"), sem("lg_step"), sem("sub_done"), sem("ex_done")
        prob_step, gate_in, gate_exp, wgt_done = sem("prob_step"), sem("gate_in"), sem("gate_exp"), sem("wgt_done")
        wt_ready, wt_done, pm_ready, zp_done = sem("wt_ready"), sem("wt_done"), sem("pm_ready"), sem("zp_done")
        zp_hi_done, zs_hi_done, zs_lo_done = sem("zp_hi_done"), sem("zs_hi_done"), sem("zs_lo_done")
        zst_ready, zst_saved = sem("zst_ready"), sem("zst_saved")
        out_ready, out_done = sem("out_ready"), sem("out_done")

        def halves(ap, h):
            return ap.rearrange("p (t c q) -> p c t q", c=C, q=Q)[:, :, TB // 2 * h:TB // 2 * (h + 1), :]

        def rows(ap, h):
            return ap[:, :, D // 2 * h:D // 2 * (h + 1)].rearrange("p c (t q) -> p c t q", q=Q)

        def chunk(ap, c):
            return ap[:, P * c:P * (c + 1)]

        def tok(ap, b):
            return ap[..., S * (b % 2):S * (b % 2 + 1)]

        def f32(ap):
            return ap.bitcast(F32)

        def w1_in(e):
            return w_t[:].rearrange("p (e m c q) -> p e c m q", e=4, m=C, c=C)[:, e]

        def w1_out(ap, e):
            return ap[:].rearrange("p c (m e q) -> p e c m q", e=4, m=C)[:, e]

        def w2_in(c):
            return w_in[:, w_slot(W2_AT)[0], D * c:D * (c + 1)].rearrange("p (e m q) -> p m e q", e=4, m=C)

        def w2_out(ap, c):
            return ap[:, 1, c].rearrange("p (m e q) -> p m e q", e=4, m=C)

        def w_slot(b):
            n = 2 if b == "w1" else b if b < 2 else b + 1
            return n % RING, 64 * (n // RING) + (16 if b in (NB, NB + 1) else 64)

        W3_AT, W2_AT = NB, NB + 1

        loads = {}

        block = ctx.enter_context(nc.Block())

        @block.sync
        def _(sp):
            def load(name, dst, src):
                sp.dma_start(dst, src).then_inc(ld[name], 16)
                loads[name] = loads.get(name, 0) + 16

            def load_x(i):
                if i >= 1:
                    sp.wait_ge(x_turned, i)
                src = x[2 * i:2 * i + 2].rearrange("b (t q) (a j) -> a q (b t) j", q=Q, a=4)
                for a in range(4):
                    dst = x_in[Q * a:Q * (a + 1), :].rearrange("q (n j) -> q n j", j=P)
                    sp.dma_start(dst, src[a]).then_inc(x_landed, 16)

            def load_w(b):
                slot, landed = w_slot(b)
                if b == "w1":
                    sp.wait_ge(w_turned, 2)
                elif b == 3:
                    sp.wait_ge(w1_turned, 2)
                elif b >= 2:
                    sp.wait_ge(w_turned, 2 * (b - 1) + 2 if b == 2 else 2 * (b - 2) + 2)
                if b == W3_AT or b == W2_AT:
                    src = (W3 if b == W3_AT else W2).rearrange("(c p) d -> p c d", p=P)
                    dst = w_in[:, slot, :].rearrange("p (c d) -> p c d", d=D)
                    sp.dma_start(dst, src).then_inc(w_landed[slot], 16)
                    return
                if b == "w1":
                    src = W1.rearrange("(t q) (a j) -> a q t j", q=Q, a=4)
                else:
                    w = sp.value_load(id0[0:1, b:b + 1], min_val=0, max_val=NW - 1)
                    src = W0[bass.ds(w, 1)].rearrange("w (t q) (a j) -> a q (w t) j", q=Q, a=4)
                for a in range(4):
                    dst = w_in[Q * a:Q * (a + 1), slot, :].rearrange("q (t j) -> q t j", j=src.shape[-1])
                    sp.dma_start(dst, src[a]).then_inc(w_landed[slot], 16)

            load_x(0)
            load_w(0)
            load("a0", a0_in, A0.rearrange("n r d -> (n r) d"))
            for n in range(NL0):
                load("b0", b0_in[:, :, n], B0[n].rearrange("(c p) r -> p c r", p=P))
            load("a1", a1_in, a1.rearrange("n r d -> (n r) d"))
            load_w(1)
            load("A", small[:, :, 0:R], A.rearrange("(c p) r -> p c r", p=P))
            load("l", l_t[:], L.rearrange("e r -> r e"))
            load_w("w1")
            load_x(1)
            load("ids", ids_i[:], id1.partition_broadcast(P))
            load("starts", starts_i[:], starts.partition_broadcast(P))
            for a in range(4):
                at = slice(Q * a, Q * (a + 1))
                load("b1c", bias1_c[at, :], bias1.rearrange("(a c q) -> a q c", a=4, q=Q)[a])
            load_w(2)
            for a in range(4):
                load("bm", bm4[Q * a:Q * (a + 1), :], Bmat)
            load("b2c", b2_c[:], b2.rearrange("(c p) -> p c", p=P))
            for n in range(NL1):
                load("b1", b1_row[:, :, R1 * n:R1 * (n + 1)], B1[n].rearrange("(c p) r -> p c r", p=P))
                load("s", s_c[R1 * n:R1 * (n + 1), :], s1[n:n + 1].partition_broadcast(R1))
            load("bias", bias_all[:], b3.partition_broadcast(P))
            for b in range(NB):
                load("lr", l_rep[NE * b:NE * (b + 1), :], L)
            for i in range(1, NP):
                load_w(2 * i + 1)
                if i + 1 < NP:
                    load_x(i + 1)
                load_w(2 * i + 2)
            load_w(W2_AT)
            for b in range(NB):
                sp.wait_ge(out_done, b + 1)
                sp.dma_start(out[b], out_sb[:, b % 4]).then_inc(out_stored[b % 4], 16)
            for n in range(4):
                sp.wait_ge(out_stored[n], 16 * (NB // 4))

        @block.gpsimd
        def _(pool):
            nc.gpsimd.memset(ident[:], 0.0).then_inc(ident_zero, 1)
            pool.wait_ge(ident_zero, 1)
            nc.gpsimd.affine_select(out=ident[:], in_=ident[:], compare_op=ALU.not_equal, fill=1.0, base=0,
                                    pattern=[[-1, P]], channel_multiplier=1).then_inc(ident_done, 1)
            nc.gpsimd.memset(ones2[:], 1.0).then_inc(ones_done, 1)
            nc.gpsimd.iota(iota_i[:, 0:1], [[0, 1]], base=0, channel_multiplier=1)
            nc.gpsimd.iota(iota_i[:, 1:1 + NB], [[1, NB]], base=0, channel_multiplier=0).then_inc(iota_done, 1)

            def x_low(i):
                if i >= 2:
                    pool.wait_ge(c0_ready, 2 * (i - 1))
                pool.wait_ge(x_hi_done, i + 1)
                view = x_t[:, i % 3].rearrange("p (n c q) -> p c n q", c=C, q=Q)
                split = [t.rearrange("p c (n q) -> p c n q", q=Q) for t in (x_hi[:, i % 2], x_lo[:, i % 2])]
                nc.gpsimd.tensor_tensor(split[1], view, f32(split[0]), ALU.subtract).then_inc(x_lo_done, 1)

            def x1_low(i, h):
                pool.wait_ge(x1_hi_done, 2 * i + h + 1)
                c = slice(2 * h, 2 * h + 2)
                nc.gpsimd.tensor_tensor(x1_lo[:, i, c], x1_t[:, c], f32(x1_hi[:, i, c]),
                                        ALU.subtract).then_inc(x1_lo_done, 1)

            def in_order(ap):
                return ap.rearrange("k (e m q) -> k m e q", e=4, m=C)

            def ordered(ap):
                return ap.rearrange("k (m e q) -> k m e q", e=4, m=C)

            x_low(0)
            pool.wait_ge(ld["a0"], loads["a0"])
            nc.gpsimd.tensor_copy(ordered(a0_row), in_order(a0_in)).then_inc(rows_ready, 1)
            pool.wait_ge(ld["b0"], loads["b0"])
            for g in range(2):
                last = nc.gpsimd.tensor_copy(b0_row[:, :, g], b0_in.rearrange("p c n r -> p c (n r)"))
            last.then_inc(rows_ready, 1)
            pool.wait_ge(ld["a1"], loads["a1"])
            nc.gpsimd.tensor_copy(ordered(a1_row), in_order(a1_in)).then_inc(rows_ready, 1)
            for i in range(NP):
                if i + 1 < NP:
                    x_low(i + 1)
                if i == 0:
                    pool.wait_ge(ld["lr"], loads["lr"])
                    nc.gpsimd.affine_select(out=l_diag[:], in_=l_rep[:].unsqueeze(1).to_broadcast([NB * NE, NB, R]),
                                            compare_op=ALU.is_ge, fill=0.0, base=0, pattern=[[-NE, NB], [0, R]],
                                            channel_multiplier=1).then_inc(ldiag_step, 1)
                    pool.wait_ge(ldiag_step, 1)
                    nc.gpsimd.affine_select(out=l_diag[:], in_=l_diag[:], compare_op=ALU.is_ge, fill=0.0,
                                            base=NE - 1, pattern=[[NE, NB], [0, R]],
                                            channel_multiplier=-1).then_inc(ldiag_step, 1)
                if i >= 1:
                    x1_low(i - 1, 0)
                    x1_low(i - 1, 1)
            x1_low(NP - 1, 0)
            x1_low(NP - 1, 1)

        @block.scalar
        def _(act):
            def x_high(i):
                if i >= 2:
                    act.wait_ge(c0_ready, 2 * (i - 1))
                act.wait_ge(x_turned, i + 1)
                nc.scalar.copy(x_hi[:, i % 2].rearrange("p c (n q) -> p c n q", q=Q),
                               x_t[:, i % 3].rearrange("p (n c q) -> p c n q", c=C, q=Q)).then_inc(x_hi_done, 1)

            def w_high(b):
                for h in range(2):
                    if b >= 2 and h == 0:
                        act.wait_ge(c0_ready, b - 1)
                    act.wait_ge(w_turned, 2 * b + h + 1)
                    nc.scalar.copy(rows(w_hi[:, b % 2], h), halves(w_t[:], h)).then_inc(w_hi_done, 1)

            def w1_high():
                for e in range(4):
                    act.wait_ge(w1_turned, e // 2 + 1)
                    nc.scalar.copy(w1_out(w1_hi, e), w1_in(e)).then_inc(w1_hi_done, 1)

            def w3_high(c):
                if c == 0:
                    act.wait_ge(c0_ready, NB - 1)
                act.wait_ge(w3t_ready, c + 1)
                nc.scalar.copy(w_hi[:, 0, c], bank[c % 2][:]).then_inc(w3_hi_done, 1)

            def save_c0(b):
                if b == 1:
                    act.wait_ge(aux_ready, 1)
                if b >= 2:
                    act.wait_ge(c0t_ready, b - 1)
                act.wait_ge(c0_ready, b + 1)
                nc.scalar.copy(c0_row[:, b % 2].rearrange("p (c a q) -> p a c q", c=C, a=4),
                               bank[b % 2][:].rearrange("p (a c q) -> p a c q", c=C, a=4)).then_inc(c0_saved, 1)

            def c0_high(b):
                if b >= 4:
                    act.wait_ge(y_ready, 2 * (b // 2 - 1))
                act.wait_ge(c0t_ready, b + 1)
                nc.scalar.copy(tok(c0_hi[:, (b // 2) % 2], b),
                               bank[2 + b % 2][:].rearrange("p (c s) -> p c s", s=S)).then_inc(c0t_hi_done, 1)

            def x1_high(i, h):
                act.wait_ge(x1_summed, 2 * i + h + 1)
                c = slice(2 * h, 2 * h + 2)
                nc.scalar.copy(x1_hi[:, i, c], x1_t[:, c]).then_inc(x1_hi_done, 1)

            x_high(0)
            w_high(0)
            act.wait_ge(aux_ready, 1)
            nc.scalar.copy(a0_t[:, :, 0:K0], bank[7][:, 0:C * K0].rearrange("p (c k) -> p c k", k=K0)).then_inc(aux_hi, 1)
            act.wait_ge(aux_ready, 2)
            nc.scalar.copy(b0_hi[:].rearrange("k (m e q) -> k m e q", e=4, m=C),
                           bank[6][0:2 * K0, :].rearrange("k (e m q) -> k m e q", e=4, m=C)).then_inc(aux_hi, 1)
            for i in range(NP):
                w_high(2 * i + 1)
                save_c0(2 * i)
                if i == 0:
                    w1_high()
                if i + 1 < NP:
                    x_high(i + 1)
                if i >= 1:
                    x1_high(i - 1, 0)
                c0_high(2 * i)
                if i == 0:
                    act.wait_ge(aux_ready, 3)
                    nc.scalar.copy(a1_hi[:], bank[5][:].rearrange("p (c k) -> p c k", k=K1)).then_inc(aux_hi, 1)
                    act.wait_ge(aux_ready, 4)
                    nc.scalar.copy(a_t, bank[4][0:R, :].rearrange("p (c k) -> p c k", k=P)).then_inc(aux_hi, 1)
                    act.wait_ge(aux_ready, 5)
                    nc.scalar.copy(small[:, :, R + NE:NS],
                                   bank[4][:, 0:C * NE].rearrange("p (c e) -> p c e", e=NE)).then_inc(small_done, 1)
                    act.wait_ge(ident_done, 1)
                    nc.scalar.copy(ident_r[:], ident[:]).then_inc(ident_r_done, 1)
                    act.wait_ge(ld["b1"], loads["b1"])
                    nc.scalar.copy(b1_hi[:], b1_row[:]).then_inc(b1_hi_done, 1)
                    act.wait_ge(ld["b2c"], loads["b2c"])
                    nc.scalar.copy(b2_hi[:], b2_c[:]).then_inc(b1_hi_done, 1)
                    act.wait_ge(ld["bm"], loads["bm"])
                    nc.scalar.copy(bm_parts[:], bm4).then_inc(bm_hi_done, 1)
                if i + 1 < NP:
                    w_high(2 * i + 2)
                save_c0(2 * i + 1)
                if i >= 1:
                    x1_high(i - 1, 1)
                c0_high(2 * i + 1)
            for c in range(C):
                w3_high(c)
            slot, landed = w_slot(W2_AT)
            act.wait_ge(w_landed[slot], landed)
            act.wait_ge(c0_ready, NB)
            for c in range(C):
                nc.scalar.copy(w2_out(w_hi, c), w2_in(c)).then_inc(w2_hi_done, 1)
            act.wait_ge(w3_small_done, 1)
            act.wait_ge(ld["A"], loads["A"])
            nc.scalar.copy(small_parts[:, :, 0:NS], small[:]).then_inc(small_hi_done, 1)
            act.wait_ge(be_ready, 1)
            act.wait_ge(ld["s"], loads["s"])
            nc.scalar.activation(be_f[:, 0:D], bank[0][:], ACT.Copy, scale=s_c[:, 0:1]).then_inc(be_scaled, 1)
            act.wait_ge(be_scaled, 1)
            nc.scalar.copy(be_hi[:], be_f[:, 0:D]).then_inc(be_scaled, 1)
            act.wait_ge(smalls_ready, 1)
            nc.scalar.copy(ae_f, bank[1][:, 0:2 * C * NS].rearrange("p (c n) -> p c n", n=2 * NS)[:, :, 0:NS]
                           ).then_inc(ae_saved, 1)
            nc.scalar.activation(be_f[:, D:D + NS], bank[1][:, 2 * C * NS:(2 * C + 1) * NS], ACT.Copy,
                                 scale=s_c[:, 0:1]).then_inc(ae_saved, 1)
            act.wait_ge(ae_summed, 2)
            nc.scalar.copy(ae[:, :, 0:NS], ae_f).then_inc(ae_saved, 1)
            nc.scalar.copy(bes[:, 0:NS], be_f[:, D:D + NS]).then_inc(ae_saved, 1)
            x1_high(NP - 1, 0)
            x1_high(NP - 1, 1)

            def m_high(m):
                act.wait_ge(m_ready, m + 1)
                nc.scalar.copy(m_hi[:, m], bank[M_BANK[m]][:]).then_inc(m_hi_done, 1)

            m_high(0)
            m_high(1)
            m_high(2)
            m_high(3)
            act.wait_ge(sub_done, 1)
            nc.scalar.activation(ex[:], sub[:], ACT.Exp).then_inc(ex_done, 1)
            act.wait_ge(gate_in, 1)
            nc.scalar.activation(gate[:], gate[:], ACT.Exp, scale=-1.0 / SOFT_TOPK_TEMP).then_inc(gate_exp, 1)
            act.wait_ge(zp_hi_done, 1)
            hi2 = f32(zp_hi[:]).unsqueeze(2).to_broadcast([P, NB, 2, R])
            nc.scalar.copy(zs[:, :, 0:2, :], hi2).then_inc(zs_hi_done, 1)
            act.wait_ge(zst_ready, 1)
            nc.scalar.copy(z_parts[:, 0:4], bank[4][:].rearrange("p (b s) -> p b s", s=S)).then_inc(zst_saved, 1)
            act.wait_ge(zst_ready, 2)
            nc.scalar.copy(z_parts[:, 4:8], bank[5][:].rearrange("p (b s) -> p b s", s=S)).then_inc(zst_saved, 1)

        @block.vector
        def _(dve):
            def x_turn(i):
                dve.wait_ge(x_landed, 64 * (i + 1))
                if i == 1:
                    dve.wait_ge(rows_ready, 3)
                    dve.wait_ge(aux_ready, 3)
                if i == 2:
                    dve.wait_ge(bm_done, 2)
                    dve.wait_ge(aux_ready, 5)
                if i >= 3:
                    dve.wait_ge(x1_summed, 2 * (i - 2))
                nc.vector.transpose(x_t[:, i % 3], x_in[:]).then_inc(x_turned, 1)

            def w_turn(b):
                slot, landed = w_slot(b)
                dve.wait_ge(w_landed[slot], landed)
                for h in range(2):
                    if b == 2:
                        dve.wait_ge(w1_hi_done, 2 * h + 2)
                        dve.wait_ge(w1_lo_done, 2 * h + 2)
                    elif b >= 1:
                        dve.wait_ge(w_hi_done, 2 * (b - 1) + h + 1)
                        dve.wait_ge(w_lo_done, 2 * (b - 1) + h + 1)
                    half = slice(D * C // 2 * h, D * C // 2 * (h + 1))
                    nc.vector.transpose(w_t[:, half], w_in[:, slot, half]).then_inc(w_turned, 1)

            def w_low(b):
                for h in range(2):
                    if b >= 2 and h == 0:
                        dve.wait_ge(c0_ready, b - 1)
                    dve.wait_ge(w_hi_done, 2 * b + h + 1)
                    nc.vector.tensor_tensor(rows(w_lo[:, b % 2], h), halves(w_t[:], h),
                                            f32(rows(w_hi[:, b % 2], h)), ALU.subtract).then_inc(w_lo_done, 1)

            def w1_turn():
                slot, landed = w_slot("w1")
                dve.wait_ge(w_landed[slot], landed)
                for h in range(2):
                    dve.wait_ge(w_hi_done, 2 + h + 1)
                    dve.wait_ge(w_lo_done, 2 + h + 1)
                    half = slice(D * C // 2 * h, D * C // 2 * (h + 1))
                    nc.vector.transpose(w_t[:, half], w_in[:, slot, half]).then_inc(w1_turned, 1)

            def w1_low():
                for e in range(4):
                    dve.wait_ge(w1_hi_done, e + 1)
                    nc.vector.tensor_tensor(w1_out(w1_lo, e), w1_in(e), f32(w1_out(w1_hi, e)),
                                            ALU.subtract).then_inc(w1_lo_done, 1)

            def w3_low(c):
                dve.wait_ge(w3_hi_done, c + 1)
                nc.vector.tensor_tensor(w_lo[:, 0, c], bank[c % 2][:], f32(w_hi[:, 0, c]),
                                        ALU.subtract).then_inc(w3_lo_done, 1)

            def c0_low(b):
                if b >= 4:
                    dve.wait_ge(y_ready, 2 * (b // 2 - 1))
                dve.wait_ge(c0t_hi_done, b + 1)
                nc.vector.tensor_tensor(tok(c0_lo[:, (b // 2) % 2], b),
                                        bank[2 + b % 2][:].rearrange("p (c s) -> p c s", s=S),
                                        f32(tok(c0_hi[:, (b // 2) % 2], b)), ALU.subtract).then_inc(c0t_lo_done, 1)

            def low0_split(i):
                dve.wait_ge(low0_ready, i + 1)
                if i >= 1:
                    dve.wait_ge(y_ready, 2 * i)
                for j in range(2):
                    at = slice(S * j, S * (j + 1))
                    nc.vector.tensor_scalar(low0_hi[:, at], bank[6][0:2 * K0, at],
                                            mask0[0:2 * K0, 2 * i + j:2 * i + j + 1], None,
                                            ALU.mult).then_inc(low0_hi_done, 1)
                for j in range(2):
                    at = slice(S * j, S * (j + 1))
                    dve.wait_ge(low0_hi_done, 2 * i + j + 1)
                    last = nc.vector.scalar_tensor_tensor(low0_lo[:, at], bank[6][0:2 * K0, at],
                                                          mask0[0:2 * K0, 2 * i + j:2 * i + j + 1],
                                                          f32(low0_hi[:, at]), ALU.mult, ALU.subtract)
                last.then_inc(low0_lo_done, 1)

            def low1_split(i):
                dve.wait_ge(low1_ready, i + 1)
                for j in range(2):
                    b = 2 * i + j
                    nc.vector.tensor_scalar(low1_hi[:, b], bank[7][:, S * j:S * (j + 1)], mask1[:, b:b + 1], None,
                                            ALU.mult).then_inc(low1_hi_done, 1)
                for j in range(2):
                    b = 2 * i + j
                    dve.wait_ge(low1_hi_done, b + 1)
                    last = nc.vector.scalar_tensor_tensor(low1_lo[:, b], bank[7][:, S * j:S * (j + 1)],
                                                          mask1[:, b:b + 1], f32(low1_hi[:, b]),
                                                          ALU.mult, ALU.subtract)
                last.then_inc(low1_lo_done, 1)

            def x1_sum(i, h):
                dve.wait_ge(y_ready, 2 * i + h + 1)
                if i >= 1:
                    dve.wait_ge(x1_hi_done, 2 * (i - 1) + h + 1)
                    dve.wait_ge(x1_lo_done, 2 * (i - 1) + h + 1)
                for m in (2 * h, 2 * h + 1):
                    xt = x_t[:, i % 3].rearrange("p (n c q) -> p c n q", c=C, q=Q)[:, m]
                    y = bank[4 + h][:, 2 * S * (m % 2):2 * S * (m % 2 + 1)].rearrange("p (n q) -> p n q", q=Q)
                    last = nc.vector.scalar_tensor_tensor(x1_t[:, m].rearrange("p (n q) -> p n q", q=Q), y,
                                                          bias1_c[:, m:m + 1], xt, ALU.add, ALU.add)
                last.then_inc(x1_summed, 1)

            steps = [0]

            def masks():
                def step(ins):
                    steps[0] += 1
                    ins.then_inc(mask_step, 1)

                dve.wait_ge(iota_done, 1)
                step(nc.vector.tensor_copy(part_f[:], iota_i[:, 0:1]))
                step(nc.vector.tensor_copy(batch_f[:], iota_i[:, 1:1 + NB]))
                dve.wait_ge(ld["ids"], loads["ids"])
                step(nc.vector.tensor_copy(ids_f[:], ids_i[:]))
                dve.wait_ge(ld["starts"], loads["starts"])
                step(nc.vector.tensor_copy(starts_f[:], starts_i[:]))
                step(nc.vector.tensor_scalar(iota_i[:, 0:1], iota_i[:, 0:1], 4, None, ALU.logical_shift_right))
                dve.wait_ge(mask_step, steps[0])
                step(nc.vector.tensor_copy(group_f[:, 0:1], iota_i[:, 0:1]))
                step(nc.vector.tensor_scalar(group_f[:, 1:2], part_f[:], float(K0), float(-NL0), ALU.is_ge, ALU.mult))
                step(nc.vector.tensor_tensor(started[:], starts_f[:].unsqueeze(1).to_broadcast([P, NB, NL0 + 1]),
                                             batch_f[:].unsqueeze(2).to_broadcast([P, NB, NL0 + 1]), ALU.is_le))
                dve.wait_ge(mask_step, steps[0])
                step(nc.vector.tensor_reduce(seg_f[:], started[:], AX.X, ALU.add))
                step(nc.vector.scalar_tensor_tensor(group_f[:, 2:3], group_f[:, 0:1], 2.0, group_f[:, 1:2],
                                                    ALU.add, ALU.add))
                dve.wait_ge(mask_step, steps[0])
                nc.vector.tensor_scalar(mask0[:], seg_f[:], group_f[:, 2:3], None, ALU.is_equal)
                nc.vector.tensor_scalar(mask1[:], ids_f[:], group_f[:, 0:1], None,
                                        ALU.is_equal).then_inc(masks_done, 1)
                dve.wait_ge(masks_done, 1)

            x_turn(0)
            w_turn(0)
            w_low(0)
            dve.wait_ge(aux_hi, 1)
            nc.vector.tensor_tensor(a0_t[:, :, K0:2 * K0], bank[7][:, 0:C * K0].rearrange("p (c k) -> p c k", k=K0),
                                    f32(a0_t[:, :, 0:K0]), ALU.subtract).then_inc(aux_lo, 1)
            dve.wait_ge(aux_hi, 2)
            nc.vector.tensor_tensor(b0_lo[:].rearrange("k (m e q) -> k m e q", e=4, m=C),
                                    bank[6][0:2 * K0, :].rearrange("k (e m q) -> k m e q", e=4, m=C),
                                    f32(b0_hi[:]).rearrange("k (m e q) -> k m e q", e=4, m=C), ALU.subtract).then_inc(aux_lo, 1)
            for i in range(NP):
                w_turn(2 * i + 1)
                if i >= 2:
                    low1_split(i - 2)
                if i >= 1:
                    low0_split(i - 1)
                w_low(2 * i + 1)
                if i == 0:
                    w1_turn()
                    w1_low()
                    dve.wait_ge(ld["b1c"], loads["b1c"])
                if i + 1 < NP:
                    x_turn(i + 1)
                if i >= 1:
                    x1_sum(i - 1, 0)
                c0_low(2 * i)
                if i == 0:
                    masks()
                    dve.wait_ge(aux_hi, 3)
                    nc.vector.tensor_tensor(a1_lo[:], bank[5][:].rearrange("p (c k) -> p c k", k=K1), f32(a1_hi[:]),
                                            ALU.subtract).then_inc(aux_lo, 1)
                    dve.wait_ge(b1_hi_done, 2)
                    nc.vector.tensor_tensor(b1_lo[:], b1_row[:], f32(b1_hi[:]), ALU.subtract)
                    nc.vector.tensor_tensor(b2_lo[:], b2_c[:], f32(b2_hi[:]), ALU.subtract).then_inc(b1_lo_done, 1)
                    dve.wait_ge(bm_hi_done, 1)
                    for a in (1, 3):
                        at = slice(Q * a, Q * (a + 1))
                        nc.vector.tensor_tensor(bm_parts[at], bm4[at], f32(bm_parts[at]), ALU.subtract).then_inc(bm_done, 1)
                if i + 1 < NP:
                    w_turn(2 * i + 2)
                if i >= 1:
                    x1_sum(i - 1, 1)
                if i + 1 < NP:
                    w_low(2 * i + 2)
                c0_low(2 * i + 1)
            w3_low(0)
            w3_low(1)
            low1_split(NP - 2)
            low0_split(NP - 1)
            w3_low(2)
            w3_low(3)
            dve.wait_ge(w3_lo_done, 4)
            nc.vector.tensor_tensor(small[:, :, R:R + NE], f32(w_hi[:, 0, :, 0:NE]), f32(w_lo[:, 0, :, 0:NE]),
                                    ALU.add).then_inc(w3_small_done, 1)
            for c in range(C):
                dve.wait_ge(w2_hi_done, c + 1)
                nc.vector.tensor_tensor(w2_out(w_lo, c), w2_in(c), f32(w2_out(w_hi, c)), ALU.subtract).then_inc(w2_lo_done, 1)
            dve.wait_ge(small_hi_done, 1)
            nc.vector.tensor_tensor(small_parts[:, :, NS:2 * NS], small[:], f32(small_parts[:, :, 0:NS]),
                                    ALU.subtract).then_inc(small_lo_done, 1)
            dve.wait_ge(ld["bias"], loads["bias"])
            dve.wait_ge(smalls_ready, 1)
            dve.wait_ge(ae_saved, 2)
            nc.vector.tensor_tensor(ae_f, bank[1][:, 0:2 * C * NS].rearrange("p (c n) -> p c n", n=2 * NS)[:, :, NS:],
                                    ae_f, ALU.add).then_inc(ae_summed, 1)
            nc.vector.scalar_tensor_tensor(be_f[:, D:D + NS], bank[1][:, (2 * C + 1) * NS:(2 * C + 2) * NS],
                                           s_c[:, 0:1], be_f[:, D:D + NS], ALU.mult, ALU.add).then_inc(ae_summed, 1)
            nc.vector.tensor_copy(bias_small[:], bank[6][:, 0:NS]).then_inc(bsm_step, 1)
            dve.wait_ge(bsm_step, 1)
            nc.vector.tensor_tensor(bias_small[:, R:R + NE], bias_small[:, R:R + NE], bias_all[:, 0:NE],
                                    ALU.add).then_inc(bsm_step, 1)
            dve.wait_ge(bsm_step, 2)
            dve.wait_ge(bias_ready, 1)
            nc.vector.tensor_tensor(bias_all[:], bank[2][:], bias_all[:], ALU.add).then_inc(bias_done, 1)
            dve.wait_ge(be_scaled, 2)
            nc.vector.tensor_tensor(be_lo[:], be_f[:, 0:D], f32(be_hi[:]), ALU.subtract).then_inc(be_done, 1)
            dve.wait_ge(ae_saved, 4)
            nc.vector.tensor_tensor(ae[:, :, NS:2 * NS], ae_f, f32(ae[:, :, 0:NS]), ALU.subtract).then_inc(ae_done, 1)
            nc.vector.tensor_tensor(bes[:, NS:2 * NS], be_f[:, D:D + NS], f32(bes[:, 0:NS]),
                                    ALU.subtract).then_inc(ae_done, 1)
            x1_sum(NP - 1, 0)
            x1_sum(NP - 1, 1)

            def m_low(m):
                dve.wait_ge(m_hi_done, m + 1)
                nc.vector.tensor_tensor(m_lo[:, m], bank[M_BANK[m]][:], f32(m_hi[:, m]), ALU.subtract).then_inc(m_lo_done, 1)

            m_low(0)
            m_low(1)
            low1_split(NP - 1)
            for h in range(2):
                dve.wait_ge(zr_ready, h + 1)
                ps = bank[4 + h][:, 0:4 * 2 * NS].rearrange("p (b n) -> p b n", n=2 * NS)
                nc.vector.tensor_tensor(zr[:, 4 * h:4 * h + 4], ps[:, :, 0:NS],
                                        bias_small[:].unsqueeze(1).to_broadcast([P, 4, NS]),
                                        ALU.add).then_inc(zr_step, 1)
                dve.wait_ge(zr_step, h + 1)
                nc.vector.tensor_tensor(zr[:, 4 * h:4 * h + 4], ps[:, :, NS:2 * NS], zr[:, 4 * h:4 * h + 4],
                                        ALU.add).then_inc(zr_done, 1)
            dve.wait_ge(zr_done, 2)
            nc.vector.tensor_reduce(top[:], zr[:, :, R:NS].rearrange("p b (g e) -> p g b e", g=2), AX.XY, ALU.max,
                                    apply_absolute_value=True).then_inc(top_done, 1)
            m_low(2)
            dve.wait_ge(topt_ready, 1)
            nc.vector.tensor_reduce(r2[:, 0:1], bank[6][0:2, 0:S].rearrange("p (n two) -> p n two", two=2)[:, :, 1],
                                    AX.X, ALU.max).then_inc(r_step, 1)
            dve.wait_ge(r_step, 1)
            nc.vector.tensor_scalar(r2[:, 1:2], r2[:, 0:1], EPS, None, ALU.max).then_inc(r_step, 1)
            dve.wait_ge(r_step, 2)
            nc.vector.reciprocal(r2[:, 0:1], r2[:, 1:2]).then_inc(r_step, 1)
            dve.wait_ge(r_step, 3)
            nc.vector.tensor_scalar(r2d[:], ident[0:2, 0:2], r2[:, 0:1], GAMMA, ALU.mult, ALU.mult).then_inc(r_done, 1)
            m_low(3)
            dve.wait_ge(rb_ready, 1)
            nc.vector.tensor_copy(r_b[:], bank[6][:, S:S + 2]).then_inc(lg_step, 1)
            dve.wait_ge(lg_step, 1)
            nc.vector.tensor_scalar(lgd[:], zr[:, :, R + NE:NS], r_b[:, 1:2], None, ALU.mult).then_inc(lg_step, 1)
            dve.wait_ge(lg_step, 2)
            nc.vector.scalar_tensor_tensor(lg[:], zr[:, :, R:R + NE], r_b[:, 0:1], lgd[:], ALU.mult,
                                           ALU.add).then_inc(lg_step, 1)
            dve.wait_ge(lg_step, 3)
            for b in range(NB):
                last = nc.vector.max(mx[:, b], lg[:, b])
            last.then_inc(lg_step, 1)
            dve.wait_ge(lg_step, 4)
            nc.vector.tensor_tensor(sub[:, :, 0:NE], lg[:], mx[:, :, 0:1].to_broadcast([P, NB, NE]), ALU.subtract)
            nc.vector.tensor_tensor(sub[:, :, NE:NE + 1], mx[:, :, 1:2], mx[:, :, 0:1], ALU.subtract).then_inc(sub_done, 1)
            dve.wait_ge(ex_done, 1)
            nc.vector.tensor_reduce(tot[:, 0], ex[:, :, 0:NE], AX.X, ALU.add).then_inc(prob_step, 1)
            dve.wait_ge(prob_step, 1)
            nc.vector.reciprocal(tot[:, 1], tot[:, 0]).then_inc(prob_step, 1)
            dve.wait_ge(prob_step, 2)
            nc.vector.tensor_tensor(prob[:], ex[:], tot[:, 1].unsqueeze(2).to_broadcast([P, NB, NE + 1]),
                                    ALU.mult).then_inc(prob_step, 1)
            dve.wait_ge(prob_step, 3)
            nc.vector.tensor_tensor(gate[:], prob[:, :, 0:NE], prob[:, :, NE:NE + 1].to_broadcast([P, NB, NE]),
                                    ALU.subtract).then_inc(gate_in, 1)
            dve.wait_ge(gate_exp, 1)
            nc.vector.tensor_scalar(gate[:], gate[:], 1.0, None, ALU.add).then_inc(prob_step, 1)
            dve.wait_ge(prob_step, 4)
            nc.vector.reciprocal(gate[:], gate[:]).then_inc(prob_step, 1)
            dve.wait_ge(prob_step, 5)
            nc.vector.tensor_tensor(gate[:], gate[:], prob[:, :, 0:NE], ALU.mult).then_inc(prob_step, 1)
            dve.wait_ge(prob_step, 6)
            nc.vector.tensor_reduce(tot[:, 2], gate[:], AX.X, ALU.add).then_inc(prob_step, 1)
            dve.wait_ge(prob_step, 7)
            nc.vector.tensor_scalar(tot[:, 3], tot[:, 2], 1e-9, None, ALU.add).then_inc(prob_step, 1)
            dve.wait_ge(prob_step, 8)
            nc.vector.reciprocal(tot[:, 0], tot[:, 3]).then_inc(prob_step, 1)
            dve.wait_ge(prob_step, 9)
            nc.vector.tensor_tensor(wgt[:], gate[:], tot[:, 0].unsqueeze(2).to_broadcast([P, NB, NE]),
                                    ALU.mult).then_inc(wgt_done, 1)
            dve.wait_ge(wt_ready, 1)
            nc.vector.tensor_copy(w_tok.rearrange("p (n two) -> p n two", two=2),
                                  bank[7][0:NB * NE, 0:S].rearrange("p (n two) -> p n two", two=2)[:, :, 1:2]
                                  .to_broadcast([NB * NE, S // 2, 2])).then_inc(wt_done, 1)
            dve.wait_ge(pm_ready, 1)
            nc.vector.scalar_tensor_tensor(zp, bank[6][:, 256:256 + NB * R].rearrange("p (b r) -> p b r", r=R),
                                           SCALING, zr[:, :, 0:R], ALU.mult, ALU.mult).then_inc(zp_done, 1)
            dve.wait_ge(zp_done, 1)
            nc.vector.tensor_copy(zp_hi[:], zp).then_inc(zp_hi_done, 1)
            dve.wait_ge(zp_hi_done, 1)
            nc.vector.tensor_tensor(zs[:, :, 2:4, :], zp.unsqueeze(2).to_broadcast([P, NB, 2, R]),
                                    f32(zp_hi[:]).unsqueeze(2).to_broadcast([P, NB, 2, R]),
                                    ALU.subtract).then_inc(zs_lo_done, 1)
            for b in range(NB):
                dve.wait_ge(out_ready, b + 1)
                if b >= 4:
                    dve.wait_ge(out_stored[b % 4], 16 * (b // 4))
                nc.vector.tensor_tensor(out_sb[:, b % 4], bank[M_BANK[b % 4]][:], bias_all[:],
                                        ALU.add).then_inc(out_done, 1)

        @block.tensor
        def _(pe):
            mm = nc.tensor.matmul

            def product(o, parts, rest=None, start=True, stop=True):
                for n, (st, mv) in enumerate(parts):
                    ins = mm(o, st, mv, start=start and n == 0, stop=stop and n == len(parts) - 1)
                return ins

            def three(hi, lo, mhi, mlo):
                return [(hi, mhi), (hi, mlo), (lo, mhi)]

            def wide(o, at, parts):
                for n, (st, mv) in enumerate(parts):
                    ins = mm(o[:, at:at + mv.shape[-1]], st, mv, start=n == 0, stop=n == len(parts) - 1)
                return ins

            def layer_a(b):
                i = b // 2
                if b >= 2:
                    pe.wait_ge(c0_saved, b - 1)
                pe.wait_ge(x_hi_done, i + 1)
                pe.wait_ge(x_lo_done, i + 1)
                pe.wait_ge(w_hi_done, 2 * b + 2)
                pe.wait_ge(w_lo_done, 2 * b + 2)
                parts = []
                for c in range(C):
                    parts += three(tok(x_hi[:, i % 2, c], b), tok(x_lo[:, i % 2, c], b),
                                   w_hi[:, b % 2, c], w_lo[:, b % 2, c])
                product(bank[b % 2][:], parts).then_inc(c0_ready, 1)

            def turn_c0(b):
                pe.wait_ge(c0_saved, b + 1)
                if b >= 2:
                    pe.wait_ge(c0t_lo_done, b - 1)
                for c in range(C):
                    last = nc.tensor.transpose(bank[2 + b % 2][:, S * c:S * (c + 1)], chunk(c0_row[:, b % 2], c),
                                               ident[:])
                last.then_inc(c0t_ready, 1)

            def low0(i):
                pe.wait_ge(c0t_lo_done, 2 * i + 2)
                if i >= 1:
                    pe.wait_ge(low0_lo_done, i)
                else:
                    pe.wait_ge(aux_lo, 2)
                parts = []
                for c in range(C):
                    parts += [(a0_t[:, c], c0_hi[:, i % 2, c]), (a0_t[:, c], c0_lo[:, i % 2, c])]
                product(bank[6][0:2 * K0, 0:2 * S], parts).then_inc(low0_ready, 1)

            def layer_b(i, h):
                if i >= 1:
                    pe.wait_ge(x1_summed, 2 * (i - 1) + h + 1)
                else:
                    pe.wait_ge(w1_hi_done, 4)
                    pe.wait_ge(w1_lo_done, 4)
                    pe.wait_ge(aux_lo, 3)
                    pe.wait_ge(small_done, 1)
                for m in (2 * h, 2 * h + 1):
                    o = bank[4 + h][:, 2 * S * (m % 2):2 * S * (m % 2 + 1)]
                    parts = []
                    for c in range(C):
                        parts += three(chunk(w1_hi[:, c], m), chunk(w1_lo[:, c], m),
                                       c0_hi[:, i % 2, c], c0_lo[:, i % 2, c])
                    product(o, parts, stop=False)
                    pe.wait_ge(low0_lo_done, i + 1)
                    last = product(o, three(chunk(b0_hi[:], m), chunk(b0_lo[:], m), low0_hi[:], low0_lo[:]),
                                   start=False)
                last.then_inc(y_ready, 1)

            def low1(i):
                pe.wait_ge(x1_lo_done, 2 * i + 2)
                if i >= 1:
                    pe.wait_ge(low1_lo_done, i)
                else:
                    pe.wait_ge(aux_lo, 3)
                parts = []
                for c in range(C):
                    parts += three(a1_hi[:, c], a1_lo[:, c], x1_hi[:, i, c], x1_lo[:, i, c])
                product(bank[7][:, 0:2 * S], parts).then_inc(low1_ready, 1)

            pe.wait_ge(ident_done, 1)
            pe.wait_ge(rows_ready, 1)
            for c in range(C):
                last = nc.tensor.transpose(bank[7][:, K0 * c:K0 * (c + 1)], chunk(a0_row, c), ident[0:K0, 0:K0])
            last.then_inc(aux_ready, 1)
            pe.wait_ge(rows_ready, 2)
            for c in range(C):
                last = nc.tensor.transpose(bank[6][0:2 * K0, P * c:P * (c + 1)], b0_row[:, c].rearrange("p g k -> p (g k)"), ident[:])
            last.then_inc(aux_ready, 1)
            layer_a(0)
            pe.wait_ge(rows_ready, 3)
            for c in range(C):
                last = nc.tensor.transpose(bank[5][:, K1 * c:K1 * (c + 1)], chunk(a1_row, c), ident[:])
            last.then_inc(aux_ready, 1)
            pe.wait_ge(ld["A"], loads["A"])
            for c in range(C):
                last = nc.tensor.transpose(bank[4][0:R, P * c:P * (c + 1)], small[:, c, 0:R], ident[:])
            last.then_inc(aux_ready, 1)
            turn_c0(0)
            layer_a(1)
            pe.wait_ge(aux_hi, 4)
            pe.wait_ge(ld["l"], loads["l"])
            for c in range(C):
                last = mm(bank[4][:, NE * c:NE * (c + 1)], a_t[:, c], l_t[:], start=True, stop=True)
            last.then_inc(aux_ready, 1)
            turn_c0(1)

            for i in range(1, NP):
                layer_a(2 * i)
                if i >= 2:
                    low1(i - 2)
                low0(i - 1)
                layer_b(i - 1, 0)
                turn_c0(2 * i)
                layer_a(2 * i + 1)
                layer_b(i - 1, 1)
                turn_c0(2 * i + 1)
            def turn_w3(c):
                if c == 0:
                    slot, landed = w_slot(W3_AT)
                    pe.wait_ge(w_landed[slot], landed)
                if c < 2:
                    pe.wait_ge(c0_saved, NB - 1 + c)
                else:
                    pe.wait_ge(w3_lo_done, c - 1)
                for t in range(C):
                    at = D * t + P * c
                    last = nc.tensor.transpose(bank[c % 2][:, P * t:P * (t + 1)],
                                               w_in[:, w_slot(W3_AT)[0], at:at + P], ident[:])
                last.then_inc(w3t_ready, 1)

            turn_w3(0)
            turn_w3(1)
            low1(NP - 2)
            low0(NP - 1)
            turn_w3(2)
            turn_w3(3)
            layer_b(NP - 1, 0)
            layer_b(NP - 1, 1)
            pe.wait_ge(c0t_lo_done, NB - 1)
            pe.wait_ge(w3_lo_done, 4)
            pe.wait_ge(b1_lo_done, 1)
            parts = []
            for c in range(C):
                hi, lo = (b[:, c:c + 1].to_broadcast([P, P]) for b in (b2_hi, b2_lo))
                parts += three(hi, lo, w_hi[:, 0, c], w_lo[:, 0, c])
            product(bank[2][:], parts).then_inc(bias_ready, 1)
            parts = []
            for c in range(C):
                parts += three(b1_hi[:, c], b1_lo[:, c], w_hi[:, 0, c], w_lo[:, 0, c])
            product(bank[0][:], parts).then_inc(be_ready, 1)
            pe.wait_ge(w2_lo_done, C)
            pe.wait_ge(small_lo_done, 1)
            for m in range(C + 1):
                parts = []
                for c in range(C):
                    hi, lo = ((chunk(w_hi[:, 1, c], m), chunk(w_lo[:, 1, c], m)) if m < C
                              else (b1_hi[:, c], b1_lo[:, c]))
                    parts += [(hi, small_parts[:, c]), (lo, small_parts[:, c, 0:NS])]
                wide(bank[1], 2 * NS * m, parts)
            pe.wait_ge(low0_lo_done, NP)
            product(bank[6][:, 0:NS], [(b2_c[:, c:c + 1].to_broadcast([P, P]), small[:, c])
                                       for c in range(C)]).then_inc(smalls_ready, 1)

            def weights_product(m):
                if m == 0:
                    pe.wait_ge(c0t_lo_done, NB)
                    pe.wait_ge(w2_lo_done, C)
                    pe.wait_ge(ident_r_done, 1)
                elif m == 1:
                    pe.wait_ge(bias_done, 1)
                elif m == 2:
                    pe.wait_ge(be_scaled, 1)
                else:
                    pe.wait_ge(ae_summed, 2)
                parts = []
                for c in range(C):
                    parts += three(chunk(w_hi[:, 1, c], m), chunk(w_lo[:, 1, c], m), w_hi[:, 0, c], w_lo[:, 0, c])
                o = bank[M_BANK[m]]
                product(o[:], parts, stop=False)
                for a in range(4):
                    at = P * a + Q * m
                    last = mm(o[:, at:at + Q], ident_r[:], ident_r[:, Q * a:Q * (a + 1)], start=False, stop=a == 3)
                last.then_inc(m_ready, 1)

            weights_product(0)
            weights_product(1)
            low1(NP - 1)
            pe.wait_ge(x1_summed, 2 * NP)
            pe.wait_ge(ae_done, 2)
            for b in range(NB):
                i, o = b // 2, bank[4 + b // 4]
                at = 2 * NS * (b % 4)
                parts = []
                for c in range(C):
                    parts += [(tok(x1_hi[:, i, c], b), ae[:, c]), (tok(x1_lo[:, i, c], b), ae[:, c, 0:NS])]
                parts += [(low1_hi[:, b], bes[:]), (low1_lo[:, b], bes[:, 0:NS])]
                pe.wait_ge(low1_lo_done, i + 1)
                last = wide(o, at, parts)
                if b % 4 == 3:
                    last.then_inc(zr_ready, 1)
            weights_product(2)
            pe.wait_ge(top_done, 1)
            pe.wait_ge(bsm_step, 1)
            nc.tensor.transpose(bank[6][0:2, 0:S], top[:], ident[:]).then_inc(topt_ready, 1)
            weights_product(3)
            pe.wait_ge(r_done, 1)
            pe.wait_ge(ones_done, 1)
            mm(bank[6][:, S:S + 2], ones2[:], r2d[:], start=True, stop=True).then_inc(rb_ready, 1)

            def second_layer(b):
                i = b // 2
                if b >= 4:
                    pe.wait_ge(out_done, b - 3)
                parts = []
                for c in range(C):
                    if b == 0:
                        pe.wait_ge(m_lo_done, c + 1)
                        if c == 0:
                            pe.wait_ge(be_done, 1)
                    parts += three(tok(x1_hi[:, i, c], b), tok(x1_lo[:, i, c], b), m_hi[:, c], m_lo[:, c])
                parts += three(low1_hi[:, b], low1_lo[:, b], be_hi[:], be_lo[:])
                if b < 4:
                    pe.wait_ge(m_lo_done, b + 1)
                product(bank[M_BANK[b % 4]][:], parts, stop=False)

            def routed(b):
                product(bank[M_BANK[b % 4]][:], [(z_parts[:, b], bm_parts[:])], start=False).then_inc(out_ready, 1)

            second_layer(0)
            pe.wait_ge(wgt_done, 1)
            nc.tensor.transpose(bank[7][0:NB * NE, 0:S], wgt[:].rearrange("p b e -> p (b e)"),
                                ident[:]).then_inc(wt_ready, 1)
            second_layer(1)
            pe.wait_ge(wt_done, 1)
            pe.wait_ge(ldiag_step, 2)
            mm(bank[6][:, 256:256 + NB * R], w_tok, l_diag[:].rearrange("k b r -> k (b r)"), start=True, stop=True).then_inc(pm_ready, 1)
            second_layer(2)
            pe.wait_ge(zs_hi_done, 1)
            pe.wait_ge(zs_lo_done, 1)
            for b in range(NB):
                last = nc.tensor.transpose(bank[4 + b // 4][:, S * (b % 4):S * (b % 4 + 1)],
                                           zs[:, b].rearrange("p g r -> p (g r)"), ident[:])
                if b % 4 == 3:
                    last.then_inc(zst_ready, 1)
            second_layer(3)
            pe.wait_ge(zst_saved, 2)
            pe.wait_ge(bm_done, 2)
            for b in range(4):
                routed(b)
            for b in range(4, NB):
                second_layer(b)
                routed(b)


M_BANK = [3, 2, 0, 1]

_INS = ["x", "itok_B_3_7", "itok_B_1_7", "L0_cond_weight", "L0_ffn_weight", "L0_ffn_bias", "L0_ffn_lora_A",
        "L0_ffn_lora_B", "L0_ffn_lora_start_indices", "L1_cond_weight", "L1_cond_bias", "L1_cond_lora_a_weights",
        "L1_cond_lora_b_weights", "L1_cond_scaling_factors", "L1_ffn_W", "L1_ffn_b", "L1_ffn_A", "L1_ffn_Bmat",
        "L1_ffn_LiMEs"]


def kernel(**inputs):
    import numpy as np
    from concourse import bacc
    from concourse.bass_utils import run_bass_kernel_spmd

    nc = bacc.Bacc("TRN2", target_bir_lowering=False, num_devices=1)
    arrays, args = {}, []
    for name in _INS:
        a = np.ascontiguousarray(inputs[name])
        if name == "itok_B_3_7":
            a = a.reshape(1, -1)
        arrays["in_" + name] = a
        args.append(nc.dram_tensor("in_" + name, a.shape, mybir.dt.from_np(a.dtype), kind="ExternalInput").ap())
    shape = inputs["x"].shape
    args.append(nc.dram_tensor("out_dram", shape, F32, kind="ExternalOutput").ap())
    build(nc, *args)
    r = run_bass_kernel_spmd(nc, [arrays], core_ids=[0])
    return r.results[0]["out_dram"]
```

```python
from contextlib import ExitStack

import concourse.bass as bass
from concourse import mybir

F32 = mybir.dt.float32
F32R = mybir.dt.float32r
I32 = mybir.dt.int32
ALU = mybir.AluOpType
ACT = mybir.ActivationFunctionType
AX = mybir.AxisListType

P = 128
Q = 32
EPS = 1e-6
GAMMA = 0.5
SOFT_TOPK_TEMP = 0.5
ALPHA = 16.0


def build(nc, x, id0, id1, W0, W1, bias1, A0, B0, starts, W2, b2, a1, B1, s1, W3, b3, A, Bmat, L, out):
    NB, S, D = x.shape
    NW = W0.shape[0]
    C = D // P
    TB = D // Q
    NL0, R0, _ = A0.shape
    NL1, R1, _ = a1.shape
    K0 = NL0 * R0
    K1 = NL1 * R1
    R = A.shape[1]
    NE = L.shape[0]
    NS = R + 2 * NE
    NP = NB // 2
    SCALING = ALPHA / R
    assert S == P and K1 == P and 2 * K0 <= P and D == 512 and 4 * R == P and NB % 2 == 0

    ctx = ExitStack()
    with ctx, nc.allow_non_contiguous_dma(reason="three vectors of a few hundred values"):
        def sb(name, shape, dt=F32):
            return ctx.enter_context(nc.sbuf_tensor(name, shape, dt))

        def sem(name):
            return ctx.enter_context(nc.semaphore(name))

        RING = 2
        w_in = sb("w_in", [P, RING, C * D])
        w_t = sb("w_t", [P, C * D])
        w_hi = sb("w_hi", [P, 2, C, D], F32R)
        w_lo = sb("w_lo", [P, 2, C, D], F32R)
        w1_hi = sb("w1_hi", [P, C, D], F32R)
        w1_lo = sb("w1_lo", [P, C, D], F32R)
        m_hi = sb("m_hi", [P, C, D], F32R)
        m_lo = sb("m_lo", [P, C, D], F32R)
        x_in = sb("x_in", [P, 2 * D])
        x_t = sb("x_t", [P, 3, 2 * D])
        x_hi = sb("x_hi", [P, 2, C, 2 * S], F32R)
        x_lo = sb("x_lo", [P, 2, C, 2 * S], F32R)
        c0_row = sb("c0_row", [P, 2, D])
        c0_hi = sb("c0_hi", [P, 2, C, 2 * S], F32R)
        c0_lo = sb("c0_lo", [P, 2, C, 2 * S], F32R)
        x1_t = sb("x1_t", [P, C, 2 * S])
        with nc.sbuf_tensor("early", [P, (NP - 1) * 2 * C * 2 * S], F32) as early:
            pass
        x1_parts = sb("x1_parts", [P, NP - 1, 2, C, 2 * S], F32R)
        x1_hi = [x1_parts[:, i, 0] for i in range(NP - 1)]
        x1_lo = [x1_parts[:, i, 1] for i in range(NP - 1)]
        x1_hi.append(w_hi[:, 0, :, 0:2 * S])
        x1_lo.append(w_lo[:, 0, :, 0:2 * S])
        low0_hi = sb("low0_hi", [2 * K0, 2 * S], F32R)
        low0_lo = sb("low0_lo", [2 * K0, 2 * S], F32R)
        low1_hi = sb("low1_hi", [P, NB, S], F32R)
        low1_lo = sb("low1_lo", [P, NB, S], F32R)
        a0_t = sb("a0_t", [P, C, 2 * K0], F32R)
        b0_hi = sb("b0_hi", [2 * K0, D], F32R)
        b0_lo = sb("b0_lo", [2 * K0, D], F32R)
        a1_hi = sb("a1_hi", [P, C, K1], F32R)
        a1_lo = sb("a1_lo", [P, C, K1], F32R)
        be_hi = sb("be_hi", [K1, D], F32R)
        be_lo = sb("be_lo", [K1, D], F32R)
        ae = sb("ae", [P, C, 2 * NS], F32R)
        bes = sb("bes", [K1, 2 * NS], F32R)
        l_t = sb("l_t", [R, NE])
        l_rep = sb("l_rep", [NB * NE, R])
        l_diag = sb("l_diag", [NB * NE, NB, R])
        bm_parts = sb("bm_parts", [P, D], F32R)
        bias_all = sb("bias_all", [P, D])
        bias_small = sb("bias_small", [P, NS])
        bias1_c = sb("bias1_c", [P, C])
        b2_c = sb("b2_c", [P, C])
        b2_hi = sb("b2_hi", [P, C], F32R)
        b2_lo = sb("b2_lo", [P, C], F32R)
        s_c = sb("s_c", [P, 1])
        ident = sb("ident", [P, P])
        ident_r = sb("ident_r", [P, P], F32R)
        ones2 = sb("ones2", [2, P])
        ids_i = sb("ids_i", [P, NB], I32)
        starts_i = sb("starts_i", [P, NL0 + 1], I32)
        iota_i = sb("iota_i", [P, 1 + NB], I32)
        part_f = sb("part_f", [P, 1])
        group_f = sb("group_f", [P, 3])
        ids_f = sb("ids_f", [P, NB])
        starts_f = sb("starts_f", [P, NL0 + 1])
        batch_f = sb("batch_f", [P, NB])
        seg_f = sb("seg_f", [P, NB])
        started = sb("started", [P, NB, NL0 + 1])
        mask0 = sb("mask0", [P, NB])
        mask1 = sb("mask1", [P, NB])
        top = sb("top", [P, 2])
        r2 = sb("r2", [2, 2])
        r2d = sb("r2d", [2, 2])
        r_b = sb("r_b", [P, 2])
        lg = sb("lg", [P, NB, NE])
        lgd = sb("lgd", [P, NB, NE])
        mx = sb("mx", [P, NB, 8])
        sub = sb("sub", [P, NB, NE + 1])
        ex = sb("ex", [P, NB, NE + 1])
        prob = sb("prob", [P, NB, NE + 1])
        gate = sb("gate", [P, NB, NE])
        wgt = sb("wgt", [P, NB, NE])
        tot = sb("tot", [P, 4, NB])
        zp_hi = sb("zp_hi", [P, NB, R], F32R)
        used = [0]

        def early_part(n):
            used[0] += n
            return early[:, used[0] - n:used[0]]

        b1_row = early_part(C * K1).rearrange("p (c k) -> p c k", k=K1)
        a1_row = early_part(D)
        b0_in = early_part(C * K0).rearrange("p (c n r) -> p c n r", c=C, n=NL0)
        small = early_part(C * NS).rearrange("p (c n) -> p c n", n=NS)
        be_f, bes_f = early_part(D), early_part(NS)
        ae_f = early_part(C * NS).rearrange("p (c n) -> p c n", n=NS)
        a_t = early_part(C * P)[0:R].rearrange("p (c k) -> p c k", k=P)
        bm4 = early_part(D)
        w1_t = early_part(C * D)
        x1_flat = x1_t[:].rearrange("p c s -> p (c s)")
        a0_in, a0_row = x1_flat[0:K0, 0:D], c0_row[0:K0, 1]
        a1_in = x1_flat[:, D:2 * D]
        b0_row = c0_row[:, 0, 0:C * 2 * K0].rearrange("p (c g k) -> p c g k", c=C, g=2)
        b1_hi = c0_hi[:, 1, 0:2].rearrange("p c s -> p (c s)").rearrange("p (c k) -> p c k", k=K1)
        b1_lo = c0_hi[:, 1, 2:4].rearrange("p c s -> p (c s)").rearrange("p (c k) -> p c k", k=K1)
        small_parts = c0_hi[:, 0, :, 0:2 * NS]
        zr = x_in[:, 0:NB * NS].rearrange("p (b n) -> p b n", n=NS)
        zp = x_in[:, NB * NS:NB * (NS + R)].rearrange("p (b r) -> p b r", r=R)
        w_tok = x_in[0:NB * NE, NB * (NS + R):NB * (NS + R) + S]
        zs = w_t[:, 0:NB * P].rearrange("p (b g r) -> p b g r", b=NB, g=4)
        z_parts = c0_hi[:, 0].rearrange("p c s -> p (c s)").rearrange("p (b s) -> p b s", b=NB)
        out_sb = w_in[:, 1].rearrange("p (n d) -> p n d", d=D)

        bank = [ctx.enter_context(nc.psum_tensor(f"bank{n}", [P, D], F32)) for n in range(8)]

        ld = {n: sem("landed_" + n) for n in
              ("a0", "b0", "a1", "b1", "A", "l", "lr", "bm", "bias", "b1c", "b2c", "s", "ids", "starts")}
        w_landed = [sem(f"w_landed{n}") for n in range(RING)]
        x_landed = sem("x_landed")
        out_stored = [sem(f"out_stored{n}") for n in range(4)]
        ident_zero, ident_done, iota_done = sem("ident_zero"), sem("ident_done"), sem("iota_done")
        ones_done, ldiag_step = sem("ones_done"), sem("ldiag_step")
        rows_ready = sem("rows_ready")
        ident_r_done, bm_hi_done, bm_done = sem("ident_r_done"), sem("bm_hi_done"), sem("bm_done")
        mask_step, masks_done = sem("mask_step"), sem("masks_done")
        aux_ready, aux_hi, aux_lo = sem("aux_ready"), sem("aux_hi"), sem("aux_lo")
        b1_hi_done, b1_lo_done = sem("b1_hi_done"), sem("b1_lo_done")
        w_turned, w_hi_done, w_lo_done = sem("w_turned"), sem("w_hi_done"), sem("w_lo_done")
        w1_turned, w1_hi_done, w1_lo_done = sem("w1_turned"), sem("w1_hi_done"), sem("w1_lo_done")
        w1_lo_pool = sem("w1_lo_pool")
        x_turned, x_hi_done, x_lo_done = sem("x_turned"), sem("x_hi_done"), sem("x_lo_done")
        c0_ready, c0_saved = sem("c0_ready"), sem("c0_saved")
        c0t_ready, c0t_hi_done, c0t_lo_done = sem("c0t_ready"), sem("c0t_hi_done"), sem("c0t_lo_done")
        low0_ready, low0_hi_done, low0_lo_done = sem("low0_ready"), sem("low0_hi_done"), sem("low0_lo_done")
        low1_ready, low1_hi_done, low1_lo_done = sem("low1_ready"), sem("low1_hi_done"), sem("low1_lo_done")
        y_ready, x1_summed = sem("y_ready"), sem("x1_summed")
        x1_hi_done, x1_lo_done = sem("x1_hi_done"), sem("x1_lo_done")
        at_ready, at_saved, al_ready = sem("at_ready"), sem("at_saved"), sem("al_ready")
        small_done, w3_small_done = sem("small_done"), sem("w3_small_done")
        w3t_ready, w3_hi_done, w3_lo_done = sem("w3t_ready"), sem("w3_hi_done"), sem("w3_lo_done")
        bias_ready, be_ready, smalls_ready = sem("bias_ready"), sem("be_ready"), sem("smalls_ready")
        bias_done, be_scaled, be_done, ae_saved = sem("bias_done"), sem("be_scaled"), sem("be_done"), sem("ae_saved")
        w2_hi_done, w2_lo_done, ae_summed = sem("w2_hi_done"), sem("w2_lo_done"), sem("ae_summed")
        small_hi_done, small_lo_done = sem("small_hi_done"), sem("small_lo_done")
        ae_done, bsm_step = sem("ae_done"), sem("bsm_step")
        m_ready, m_hi_done, m_lo_done = sem("m_ready"), sem("m_hi_done"), sem("m_lo_done")
        zr_ready, zr_step, zr_done = sem("zr_ready"), sem("zr_step"), sem("zr_done")
        top_done, topt_ready, r_step, r_done = sem("top_done"), sem("topt_ready"), sem("r_step"), sem("r_done")
        rb_ready, lg_step, sub_done, ex_done = sem("rb_ready"), sem("lg_step"), sem("sub_done"), sem("ex_done")
        prob_step, gate_in, gate_exp, wgt_done = sem("prob_step"), sem("gate_in"), sem("gate_exp"), sem("wgt_done")
        wt_ready, wt_done, pm_ready, zp_done = sem("wt_ready"), sem("wt_done"), sem("pm_ready"), sem("zp_done")
        zp_hi_done, zs_hi_done, zs_lo_done = sem("zp_hi_done"), sem("zs_hi_done"), sem("zs_lo_done")
        zst_ready, zst_saved = sem("zst_ready"), sem("zst_saved")
        out_ready, out_done = sem("out_ready"), sem("out_done")

        def halves(ap, h):
            return ap.rearrange("p (t c q) -> p c t q", c=C, q=Q)[:, :, TB // 2 * h:TB // 2 * (h + 1), :]

        def rows(ap, h):
            return ap[:, :, D // 2 * h:D // 2 * (h + 1)].rearrange("p c (t q) -> p c t q", q=Q)

        def chunk(ap, c):
            return ap[:, P * c:P * (c + 1)]

        def tok(ap, b):
            return ap[..., S * (b % 2):S * (b % 2 + 1)]

        def f32(ap):
            return ap.bitcast(F32)

        def w1_in(e):
            return w1_t.rearrange("p (e m c q) -> p e c m q", e=4, m=C, c=C)[:, e]

        def w1_out(ap, e):
            return ap[:].rearrange("p c (m e q) -> p e c m q", e=4, m=C)[:, e]

        def w2_in(c):
            return w_in[:, w_slot("w2")[0], D * c:D * (c + 1)].rearrange("p (e m q) -> p m e q", e=4, m=C)

        def w2_out(ap, c):
            return ap[:, 1, c].rearrange("p (m e q) -> p m e q", e=4, m=C)

        order = ["w3", "w2", 0, 1, "w1"] + list(range(2, NB))

        def w_slot(b):
            n = order.index(b)
            return n % RING, 64 * (n // RING) + 16

        loads = {}

        block = ctx.enter_context(nc.Block())

        @block.sync
        def _(sp):
            def load(name, dst, src):
                sp.dma_start(dst, src).then_inc(ld[name], 16)
                loads[name] = loads.get(name, 0) + 16

            def load_x(i):
                if i >= 1:
                    sp.wait_ge(x_turned, i)
                src = x[2 * i:2 * i + 2].rearrange("b (t q) (a j) -> a q (b t) j", q=Q, a=4)
                for a in range(4):
                    dst = x_in[Q * a:Q * (a + 1), :].rearrange("q (n j) -> q n j", j=P)
                    sp.dma_start(dst, src[a]).then_inc(x_landed, 16)

            def load_w(b):
                slot, landed = w_slot(b)
                if b == 0:
                    sp.wait_ge(w3t_ready, C)
                elif b == 1:
                    sp.wait_ge(w2_hi_done, C)
                    sp.wait_ge(w2_lo_done, C)
                elif b == "w1":
                    sp.wait_ge(w_turned, 2)
                elif b == 2:
                    sp.wait_ge(w_turned, 4)
                elif b == 3:
                    sp.wait_ge(w1_turned, 2)
                elif b not in ("w3", "w2"):
                    sp.wait_ge(w_turned, 2 * (b - 2) + 2)
                if b in ("w3", "w2"):
                    src = (W3 if b == "w3" else W2).rearrange("(c p) d -> p c d", p=P)
                    dst = w_in[:, slot, :].rearrange("p (c d) -> p c d", d=D)
                    sp.dma_start(dst, src).then_inc(w_landed[slot], 16)
                    return
                if b == "w1":
                    src = W1.rearrange("(t q) (a j) -> a q t j", q=Q, a=4)
                else:
                    w = sp.value_load(id0[0:1, b:b + 1], min_val=0, max_val=NW - 1)
                    src = W0[bass.ds(w, 1)].rearrange("w (t q) (a j) -> a q (w t) j", q=Q, a=4)
                for a in range(4):
                    dst = w_in[Q * a:Q * (a + 1), slot, :].rearrange("q (t j) -> q t j", j=src.shape[-1])
                    sp.dma_start(dst, src[a]).then_inc(w_landed[slot], 16)

            load_w("w3")
            for c in range(C):
                load("b1", b1_row[:, c].rearrange("p (n r) -> p n r", r=R1),
                     B1[:, P * c:P * (c + 1), :].rearrange("n p r -> p n r"))
            load_w("w2")
            load("A", small[:, :, 0:R], A.rearrange("(c p) r -> p c r", p=P))
            load("l", l_t[:], L.rearrange("e r -> r e"))
            load("b2c", b2_c[:], b2.rearrange("(c p) -> p c", p=P))
            load_x(0)
            load_w(0)
            for n in range(NL1):
                load("s", s_c[R1 * n:R1 * (n + 1), :], s1[n:n + 1].partition_broadcast(R1))
            load_w(1)
            load_x(1)
            load("bias", bias_all[:], b3.partition_broadcast(P))
            load("ids", ids_i[:], id1.partition_broadcast(P))
            load("starts", starts_i[:], starts.partition_broadcast(P))
            load_w("w1")
            for a in range(4):
                at = slice(Q * a, Q * (a + 1))
                load("b1c", bias1_c[at, :], bias1.rearrange("(a c q) -> a q c", a=4, q=Q)[a])
            for a in range(4):
                load("bm", bm4[Q * a:Q * (a + 1), :], Bmat)
            load_w(2)
            for b in range(NB):
                load("lr", l_rep[NE * b:NE * (b + 1), :], L)
            for i in range(1, NP):
                load_w(2 * i + 1)
                if i + 1 < NP:
                    load_x(i + 1)
                    load_w(2 * i + 2)
            for b in range(NB):
                sp.wait_ge(out_done, b + 1)
                sp.dma_start(out[b], out_sb[:, b % 4]).then_inc(out_stored[b % 4], 16)
            for n in range(4):
                sp.wait_ge(out_stored[n], 16 * (NB // 4))

        @block.gpsimd
        def _(pool):
            nc.gpsimd.memset(ident[:], 0.0).then_inc(ident_zero, 1)
            pool.wait_ge(ident_zero, 1)
            nc.gpsimd.affine_select(out=ident[:], in_=ident[:], compare_op=ALU.not_equal, fill=1.0, base=0,
                                    pattern=[[-1, P]], channel_multiplier=1).then_inc(ident_done, 1)
            nc.gpsimd.memset(ones2[:], 1.0).then_inc(ones_done, 1)
            nc.gpsimd.iota(iota_i[:, 0:1], [[0, 1]], base=0, channel_multiplier=1)
            nc.gpsimd.iota(iota_i[:, 1:1 + NB], [[1, NB]], base=0, channel_multiplier=0).then_inc(iota_done, 1)

            def x_low(i):
                if i >= 2:
                    pool.wait_ge(c0_ready, 2 * (i - 1))
                pool.wait_ge(x_hi_done, i + 1)
                view = x_t[:, i % 3].rearrange("p (n c q) -> p c n q", c=C, q=Q)
                split = [t.rearrange("p c (n q) -> p c n q", q=Q) for t in (x_hi[:, i % 2], x_lo[:, i % 2])]
                nc.gpsimd.tensor_tensor(split[1], view, f32(split[0]), ALU.subtract).then_inc(x_lo_done, 1)

            def x1_low(i, h):
                pool.wait_ge(x1_hi_done, 2 * i + h + 1)
                c = slice(2 * h, 2 * h + 2)
                nc.gpsimd.tensor_tensor(x1_lo[i][:, c], x1_t[:, c], f32(x1_hi[i][:, c]),
                                        ALU.subtract).then_inc(x1_lo_done, 1)

            def in_order(ap):
                return ap.rearrange("k (e m q) -> k m e q", e=4, m=C)

            def ordered(ap):
                return ap.rearrange("k (m e q) -> k m e q", e=4, m=C)

            def load(name, dst, src):
                nc.gpsimd.dma_start(dst, src).then_inc(ld[name], 16)
                loads[name] = loads.get(name, 0) + 16

            load("a0", a0_in, A0.rearrange("n r d -> (n r) d"))
            for n in range(NL0):
                load("b0", b0_in[:, :, n], B0[n].rearrange("(c p) r -> p c r", p=P))
            load("a1", a1_in, a1.rearrange("n r d -> (n r) d"))
            x_low(0)
            pool.wait_ge(ld["a0"], loads["a0"])
            nc.gpsimd.tensor_copy(ordered(a0_row), in_order(a0_in)).then_inc(rows_ready, 1)
            pool.wait_ge(ld["b0"], loads["b0"])
            for g in range(2):
                last = nc.gpsimd.tensor_copy(b0_row[:, :, g], b0_in.rearrange("p c n r -> p c (n r)"))
            last.then_inc(rows_ready, 1)
            pool.wait_ge(ld["a1"], loads["a1"])
            nc.gpsimd.tensor_copy(ordered(a1_row), in_order(a1_in)).then_inc(rows_ready, 1)
            x_low(1)
            pool.wait_ge(bias_ready, 1)
            pool.wait_ge(w1_hi_done, 1)
            nc.gpsimd.tensor_tensor(w1_out(w1_lo, 0), w1_in(0), f32(w1_out(w1_hi, 0)),
                                    ALU.subtract).then_inc(w1_lo_pool, 1)
            for i in range(NP):
                if 1 <= i < NP - 1:
                    x_low(i + 1)
                if i == 0:
                    pool.wait_ge(ld["lr"], loads["lr"])
                    nc.gpsimd.affine_select(out=l_diag[:], in_=l_rep[:].unsqueeze(1).to_broadcast([NB * NE, NB, R]),
                                            compare_op=ALU.is_ge, fill=0.0, base=0, pattern=[[-NE, NB], [0, R]],
                                            channel_multiplier=1).then_inc(ldiag_step, 1)
                    pool.wait_ge(ldiag_step, 1)
                    nc.gpsimd.affine_select(out=l_diag[:], in_=l_diag[:], compare_op=ALU.is_ge, fill=0.0,
                                            base=NE - 1, pattern=[[NE, NB], [0, R]],
                                            channel_multiplier=-1).then_inc(ldiag_step, 1)
                if i >= 1:
                    x1_low(i - 1, 0)
                    x1_low(i - 1, 1)
            x1_low(NP - 1, 0)
            x1_low(NP - 1, 1)

        @block.scalar
        def _(act):
            def x_high(i):
                if i >= 2:
                    act.wait_ge(c0_ready, 2 * (i - 1))
                act.wait_ge(x_turned, i + 1)
                nc.scalar.copy(x_hi[:, i % 2].rearrange("p c (n q) -> p c n q", q=Q),
                               x_t[:, i % 3].rearrange("p (n c q) -> p c n q", c=C, q=Q)).then_inc(x_hi_done, 1)

            def w_high(b):
                for h in range(2):
                    if b >= 2 and h == 0:
                        act.wait_ge(c0_ready, b - 1)
                    elif b == 1 and h == 0:
                        act.wait_ge(m_ready, C)
                        act.wait_ge(smalls_ready, 1)
                    act.wait_ge(w_turned, 2 * b + h + 1)
                    nc.scalar.copy(rows(w_hi[:, b % 2], h), halves(w_t[:], h)).then_inc(w_hi_done, 1)

            def w1_high():
                act.wait_ge(bias_ready, 1)
                for e in range(4):
                    act.wait_ge(w1_turned, e // 2 + 1)
                    nc.scalar.copy(w1_out(w1_hi, e), w1_in(e)).then_inc(w1_hi_done, 1)

            def w3_high(c):
                act.wait_ge(w3t_ready, c + 1)
                nc.scalar.copy(w1_hi[:, c], bank[c][:]).then_inc(w3_hi_done, 1)

            def m_high(m):
                act.wait_ge(m_ready, m + 1)
                nc.scalar.copy(m_hi[:, m], bank[M_BANK[m]][:]).then_inc(m_hi_done, 1)

            def low0_high(i):
                act.wait_ge(masks_done, 1)
                act.wait_ge(low0_ready, i + 1)
                if i >= 1:
                    act.wait_ge(y_ready, 2 * i)
                for j in range(2):
                    at = slice(S * j, S * (j + 1))
                    last = nc.scalar.activation(low0_hi[:, at], bank[6][0:2 * K0, at], ACT.Copy,
                                                scale=mask0[0:2 * K0, 2 * i + j:2 * i + j + 1])
                last.then_inc(low0_hi_done, 1)

            def low1_high(i):
                act.wait_ge(low1_ready, i + 1)
                for j in range(2):
                    b = 2 * i + j
                    last = nc.scalar.activation(low1_hi[:, b], bank[7][:, S * j:S * (j + 1)], ACT.Copy,
                                                scale=mask1[:, b:b + 1])
                last.then_inc(low1_hi_done, 1)

            def save_c0(b):
                if b < 2:
                    act.wait_ge(aux_ready, 2)
                if b >= 2:
                    act.wait_ge(c0t_ready, b - 1)
                act.wait_ge(c0_ready, b + 1)
                nc.scalar.copy(c0_row[:, b % 2].rearrange("p (c a q) -> p a c q", c=C, a=4),
                               bank[b % 2][:].rearrange("p (a c q) -> p a c q", c=C, a=4)).then_inc(c0_saved, 1)

            def c0_high(b):
                if b >= 4:
                    act.wait_ge(y_ready, 2 * (b // 2 - 1))
                act.wait_ge(c0t_ready, b + 1)
                nc.scalar.copy(tok(c0_hi[:, (b // 2) % 2], b),
                               bank[2 + b % 2][:].rearrange("p (c s) -> p c s", s=S)).then_inc(c0t_hi_done, 1)

            def x1_high(i, h):
                act.wait_ge(x1_summed, 2 * i + h + 1)
                c = slice(2 * h, 2 * h + 2)
                nc.scalar.copy(x1_hi[i][:, c], x1_t[:, c]).then_inc(x1_hi_done, 1)

            act.wait_ge(ident_done, 1)
            nc.scalar.copy(ident_r[:], ident[:]).then_inc(ident_r_done, 1)
            for c in range(C):
                w3_high(c)
            act.wait_ge(ld["b1"], loads["b1"])
            nc.scalar.copy(b1_hi, b1_row).then_inc(b1_hi_done, 1)
            slot, landed = w_slot("w2")
            act.wait_ge(w_landed[slot], landed)
            for c in range(C):
                nc.scalar.copy(w2_out(w_hi, c), w2_in(c)).then_inc(w2_hi_done, 1)
            act.wait_ge(at_ready, 1)
            nc.scalar.copy(a_t, bank[4][0:R, :].rearrange("p (c k) -> p c k", k=P)).then_inc(at_saved, 1)
            act.wait_ge(ld["b2c"], loads["b2c"])
            nc.scalar.copy(b2_hi[:], b2_c[:]).then_inc(b1_hi_done, 1)
            x_high(0)
            act.wait_ge(al_ready, 1)
            nc.scalar.copy(small[:, :, R + NE:NS],
                           bank[4][:, 0:C * NE].rearrange("p (c e) -> p c e", e=NE)).then_inc(small_done, 1)
            act.wait_ge(w3_small_done, 1)
            act.wait_ge(ld["A"], loads["A"])
            act.wait_ge(small_done, 1)
            nc.scalar.copy(small_parts[:, :, 0:NS], small).then_inc(small_hi_done, 1)
            act.wait_ge(be_ready, 1)
            act.wait_ge(ld["s"], loads["s"])
            nc.scalar.activation(be_f, bank[7][:], ACT.Copy, scale=s_c[:, 0:1]).then_inc(be_scaled, 1)
            act.wait_ge(be_scaled, 1)
            nc.scalar.copy(be_hi[:], be_f).then_inc(be_scaled, 1)
            m_high(0)
            w_high(0)
            m_high(1)
            m_high(2)
            m_high(3)
            x_high(1)
            act.wait_ge(smalls_ready, 1)
            nc.scalar.copy(ae_f, bank[5][:, 0:2 * C * NS].rearrange("p (c n) -> p c n", n=2 * NS)[:, :, 0:NS]
                           ).then_inc(ae_saved, 1)
            nc.scalar.activation(bes_f, bank[5][:, 2 * C * NS:(2 * C + 1) * NS], ACT.Copy,
                                 scale=s_c[:, 0:1]).then_inc(ae_saved, 1)
            for i in range(NP):
                w_high(2 * i + 1)
                if i == 0:
                    act.wait_ge(ae_summed, 2)
                    nc.scalar.copy(ae[:, :, 0:NS], ae_f).then_inc(ae_saved, 1)
                    nc.scalar.copy(bes[:, 0:NS], bes_f).then_inc(ae_saved, 1)
                    w1_high()
                save_c0(2 * i)
                if i >= 1:
                    low0_high(i - 1)
                if i >= 2:
                    low1_high(i - 2)
                if i == 0:
                    act.wait_ge(aux_ready, 1)
                    nc.scalar.copy(a0_t[:, :, 0:K0], bank[7][:, 0:C * K0].rearrange("p (c k) -> p c k", k=K0)
                                   ).then_inc(aux_hi, 1)
                    act.wait_ge(aux_ready, 2)
                    nc.scalar.copy(b0_hi[:].rearrange("k (m e q) -> k m e q", e=4, m=C),
                                   bank[6][0:2 * K0, :].rearrange("k (e m q) -> k m e q", e=4, m=C)
                                   ).then_inc(aux_hi, 1)
                if 1 <= i < NP - 1:
                    x_high(i + 1)
                if i == 0:
                    save_c0(1)
                c0_high(2 * i)
                if i >= 1:
                    x1_high(i - 1, 0)
                if i == 0:
                    act.wait_ge(aux_ready, 3)
                    nc.scalar.copy(a1_hi[:], bank[5][:].rearrange("p (c k) -> p c k", k=K1)).then_inc(aux_hi, 1)
                if i >= 1:
                    save_c0(2 * i + 1)
                if i + 1 < NP:
                    w_high(2 * i + 2)
                c0_high(2 * i + 1)
                if i >= 1:
                    x1_high(i - 1, 1)
                if i == 0:
                    act.wait_ge(ld["bm"], loads["bm"])
                    nc.scalar.copy(bm_parts[:], bm4).then_inc(bm_hi_done, 1)
            low0_high(NP - 1)
            low1_high(NP - 2)
            x1_high(NP - 1, 0)
            x1_high(NP - 1, 1)
            low1_high(NP - 1)
            act.wait_ge(sub_done, 1)
            nc.scalar.activation(ex[:], sub[:], ACT.Exp).then_inc(ex_done, 1)
            act.wait_ge(gate_in, 1)
            nc.scalar.activation(gate[:], gate[:], ACT.Exp, scale=-1.0 / SOFT_TOPK_TEMP).then_inc(gate_exp, 1)
            act.wait_ge(zp_hi_done, 1)
            hi2 = f32(zp_hi[:]).unsqueeze(2).to_broadcast([P, NB, 2, R])
            nc.scalar.copy(zs[:, :, 0:2, :], hi2).then_inc(zs_hi_done, 1)
            act.wait_ge(zst_ready, 1)
            nc.scalar.copy(z_parts[:, 0:4], bank[4][:].rearrange("p (b s) -> p b s", s=S)).then_inc(zst_saved, 1)
            act.wait_ge(zst_ready, 2)
            nc.scalar.copy(z_parts[:, 4:8], bank[5][:].rearrange("p (b s) -> p b s", s=S)).then_inc(zst_saved, 1)

        @block.vector
        def _(dve):
            def x_turn(i):
                dve.wait_ge(x_landed, 64 * (i + 1))
                if i >= 3:
                    dve.wait_ge(x1_summed, 2 * (i - 2))
                nc.vector.transpose(x_t[:, i % 3], x_in[:]).then_inc(x_turned, 1)

            def w_turn(b):
                slot, landed = w_slot(b)
                dve.wait_ge(w_landed[slot], landed)
                for h in range(2):
                    if b >= 1:
                        dve.wait_ge(w_hi_done, 2 * (b - 1) + h + 1)
                        dve.wait_ge(w_lo_done, 2 * (b - 1) + h + 1)
                    half = slice(D * C // 2 * h, D * C // 2 * (h + 1))
                    nc.vector.transpose(w_t[:, half], w_in[:, slot, half]).then_inc(w_turned, 1)

            def w_low(b):
                for h in range(2):
                    if b >= 2 and h == 0:
                        dve.wait_ge(c0_ready, b - 1)
                    elif b == 1 and h == 0:
                        dve.wait_ge(m_ready, C)
                        dve.wait_ge(smalls_ready, 1)
                    dve.wait_ge(w_hi_done, 2 * b + h + 1)
                    nc.vector.tensor_tensor(rows(w_lo[:, b % 2], h), halves(w_t[:], h),
                                            f32(rows(w_hi[:, b % 2], h)), ALU.subtract).then_inc(w_lo_done, 1)

            def w1_turn():
                slot, landed = w_slot("w1")
                dve.wait_ge(w_landed[slot], landed)
                for h in range(2):
                    half = slice(D * C // 2 * h, D * C // 2 * (h + 1))
                    nc.vector.transpose(w1_t[:, half], w_in[:, slot, half]).then_inc(w1_turned, 1)

            def w1_low():
                dve.wait_ge(bias_ready, 1)
                for e in range(1, 4):
                    dve.wait_ge(w1_hi_done, e + 1)
                    nc.vector.tensor_tensor(w1_out(w1_lo, e), w1_in(e), f32(w1_out(w1_hi, e)),
                                            ALU.subtract).then_inc(w1_lo_done, 1)

            def w3_low(c):
                dve.wait_ge(w3_hi_done, c + 1)
                nc.vector.tensor_tensor(w1_lo[:, c], bank[c][:], f32(w1_hi[:, c]),
                                        ALU.subtract).then_inc(w3_lo_done, 1)

            def c0_low(b):
                if b >= 4:
                    dve.wait_ge(y_ready, 2 * (b // 2 - 1))
                dve.wait_ge(c0t_hi_done, b + 1)
                nc.vector.tensor_tensor(tok(c0_lo[:, (b // 2) % 2], b),
                                        bank[2 + b % 2][:].rearrange("p (c s) -> p c s", s=S),
                                        f32(tok(c0_hi[:, (b // 2) % 2], b)), ALU.subtract).then_inc(c0t_lo_done, 1)

            def low0_low(i):
                if i >= 1:
                    dve.wait_ge(y_ready, 2 * i)
                dve.wait_ge(low0_hi_done, i + 1)
                for j in range(2):
                    at = slice(S * j, S * (j + 1))
                    last = nc.vector.scalar_tensor_tensor(low0_lo[:, at], bank[6][0:2 * K0, at],
                                                          mask0[0:2 * K0, 2 * i + j:2 * i + j + 1],
                                                          f32(low0_hi[:, at]), ALU.mult, ALU.subtract)
                last.then_inc(low0_lo_done, 1)

            def low1_low(i):
                dve.wait_ge(low1_hi_done, i + 1)
                for j in range(2):
                    b = 2 * i + j
                    last = nc.vector.scalar_tensor_tensor(low1_lo[:, b], bank[7][:, S * j:S * (j + 1)],
                                                          mask1[:, b:b + 1], f32(low1_hi[:, b]),
                                                          ALU.mult, ALU.subtract)
                last.then_inc(low1_lo_done, 1)

            def m_low(m):
                dve.wait_ge(m_hi_done, m + 1)
                nc.vector.tensor_tensor(m_lo[:, m], bank[M_BANK[m]][:], f32(m_hi[:, m]),
                                        ALU.subtract).then_inc(m_lo_done, 1)

            def x1_sum(i, h):
                dve.wait_ge(y_ready, 2 * i + h + 1)
                if i >= 1:
                    dve.wait_ge(x1_hi_done, 2 * (i - 1) + h + 1)
                    dve.wait_ge(x1_lo_done, 2 * (i - 1) + h + 1)
                for m in (2 * h, 2 * h + 1):
                    xt = x_t[:, i % 3].rearrange("p (n c q) -> p c n q", c=C, q=Q)[:, m]
                    y = bank[4 + h][:, 2 * S * (m % 2):2 * S * (m % 2 + 1)].rearrange("p (n q) -> p n q", q=Q)
                    last = nc.vector.scalar_tensor_tensor(x1_t[:, m].rearrange("p (n q) -> p n q", q=Q), y,
                                                          bias1_c[:, m:m + 1], xt, ALU.add, ALU.add)
                last.then_inc(x1_summed, 1)

            steps = [0]

            def masks():
                def step(ins):
                    steps[0] += 1
                    ins.then_inc(mask_step, 1)

                dve.wait_ge(iota_done, 1)
                step(nc.vector.tensor_copy(part_f[:], iota_i[:, 0:1]))
                step(nc.vector.tensor_copy(batch_f[:], iota_i[:, 1:1 + NB]))
                dve.wait_ge(ld["ids"], loads["ids"])
                step(nc.vector.tensor_copy(ids_f[:], ids_i[:]))
                dve.wait_ge(ld["starts"], loads["starts"])
                step(nc.vector.tensor_copy(starts_f[:], starts_i[:]))
                step(nc.vector.tensor_scalar(iota_i[:, 0:1], iota_i[:, 0:1], 4, None, ALU.logical_shift_right))
                dve.wait_ge(mask_step, steps[0])
                step(nc.vector.tensor_copy(group_f[:, 0:1], iota_i[:, 0:1]))
                step(nc.vector.tensor_scalar(group_f[:, 1:2], part_f[:], float(K0), float(-NL0), ALU.is_ge, ALU.mult))
                step(nc.vector.tensor_tensor(started[:], starts_f[:].unsqueeze(1).to_broadcast([P, NB, NL0 + 1]),
                                             batch_f[:].unsqueeze(2).to_broadcast([P, NB, NL0 + 1]), ALU.is_le))
                dve.wait_ge(mask_step, steps[0])
                step(nc.vector.tensor_reduce(seg_f[:], started[:], AX.X, ALU.add))
                step(nc.vector.scalar_tensor_tensor(group_f[:, 2:3], group_f[:, 0:1], 2.0, group_f[:, 1:2],
                                                    ALU.add, ALU.add))
                dve.wait_ge(mask_step, steps[0])
                nc.vector.tensor_scalar(mask0[:], seg_f[:], group_f[:, 2:3], None, ALU.is_equal)
                nc.vector.tensor_scalar(mask1[:], ids_f[:], group_f[:, 0:1], None,
                                        ALU.is_equal).then_inc(masks_done, 1)
                dve.wait_ge(masks_done, 1)

            w3_low(0)
            w3_low(1)
            w3_low(2)
            w3_low(3)
            dve.wait_ge(w3_lo_done, C)
            nc.vector.tensor_tensor(small[:, :, R:R + NE], f32(w1_hi[:, :, 0:NE]), f32(w1_lo[:, :, 0:NE]),
                                    ALU.add).then_inc(w3_small_done, 1)
            dve.wait_ge(b1_hi_done, 1)
            nc.vector.tensor_tensor(b1_lo, b1_row, f32(b1_hi), ALU.subtract).then_inc(b1_lo_done, 1)
            for c in range(C):
                dve.wait_ge(w2_hi_done, c + 1)
                nc.vector.tensor_tensor(w2_out(w_lo, c), w2_in(c), f32(w2_out(w_hi, c)),
                                        ALU.subtract).then_inc(w2_lo_done, 1)
            x_turn(0)
            dve.wait_ge(b1_hi_done, 2)
            nc.vector.tensor_tensor(b2_lo[:], b2_c[:], f32(b2_hi[:]), ALU.subtract).then_inc(b1_lo_done, 1)
            dve.wait_ge(small_hi_done, 1)
            nc.vector.tensor_tensor(small_parts[:, :, NS:2 * NS], small, f32(small_parts[:, :, 0:NS]),
                                    ALU.subtract).then_inc(small_lo_done, 1)
            w_turn(0)
            m_low(0)
            w_low(0)
            m_low(1)
            dve.wait_ge(be_scaled, 2)
            nc.vector.tensor_tensor(be_lo[:], be_f, f32(be_hi[:]), ALU.subtract).then_inc(be_done, 1)
            m_low(2)
            w_turn(1)
            masks()
            m_low(3)
            x_turn(1)
            w1_turn()
            dve.wait_ge(smalls_ready, 1)
            dve.wait_ge(ae_saved, 2)
            nc.vector.tensor_tensor(ae_f, bank[5][:, 0:2 * C * NS].rearrange("p (c n) -> p c n", n=2 * NS)[:, :, NS:],
                                    ae_f, ALU.add).then_inc(ae_summed, 1)
            nc.vector.scalar_tensor_tensor(bes_f, bank[5][:, (2 * C + 1) * NS:(2 * C + 2) * NS],
                                           s_c[:, 0:1], bes_f, ALU.mult, ALU.add).then_inc(ae_summed, 1)
            nc.vector.tensor_copy(bias_small[:], bank[6][:, 0:NS]).then_inc(bsm_step, 1)
            for i in range(NP):
                if i >= 1:
                    w_turn(2 * i + 1)
                if i == 0:
                    w_low(1)
                    dve.wait_ge(ae_saved, 4)
                    nc.vector.tensor_tensor(ae[:, :, NS:2 * NS], ae_f, f32(ae[:, :, 0:NS]),
                                            ALU.subtract).then_inc(ae_done, 1)
                    nc.vector.tensor_tensor(bes[:, NS:2 * NS], bes_f, f32(bes[:, 0:NS]),
                                            ALU.subtract).then_inc(ae_done, 1)
                    dve.wait_ge(ld["bias"], loads["bias"])
                    dve.wait_ge(bsm_step, 1)
                    nc.vector.tensor_tensor(bias_small[:, R:R + NE], bias_small[:, R:R + NE], bias_all[:, 0:NE],
                                            ALU.add).then_inc(bsm_step, 1)
                    w1_low()
                    dve.wait_ge(aux_hi, 1)
                    nc.vector.tensor_tensor(a0_t[:, :, K0:2 * K0],
                                            bank[7][:, 0:C * K0].rearrange("p (c k) -> p c k", k=K0),
                                            f32(a0_t[:, :, 0:K0]), ALU.subtract).then_inc(aux_lo, 1)
                    dve.wait_ge(aux_hi, 2)
                    nc.vector.tensor_tensor(b0_lo[:].rearrange("k (m e q) -> k m e q", e=4, m=C),
                                            bank[6][0:2 * K0, :].rearrange("k (e m q) -> k m e q", e=4, m=C),
                                            f32(b0_hi[:]).rearrange("k (m e q) -> k m e q", e=4, m=C),
                                            ALU.subtract).then_inc(aux_lo, 1)
                    dve.wait_ge(ld["b1c"], loads["b1c"])
                if i >= 1:
                    low0_low(i - 1)
                    w_low(2 * i + 1)
                if i >= 2:
                    low1_low(i - 2)
                if 1 <= i < NP - 1:
                    x_turn(i + 1)
                if i == 0:
                    w_turn(2)
                if i >= 1:
                    x1_sum(i - 1, 0)
                c0_low(2 * i)
                if i == 0:
                    dve.wait_ge(aux_hi, 3)
                    nc.vector.tensor_tensor(a1_lo[:], bank[5][:].rearrange("p (c k) -> p c k", k=K1), f32(a1_hi[:]),
                                            ALU.subtract).then_inc(aux_lo, 1)
                    dve.wait_ge(bsm_step, 2)
                    nc.vector.tensor_tensor(bias_all[:], bank[4][:], bias_all[:], ALU.add).then_inc(bias_done, 1)
                if i >= 1 and i + 1 < NP:
                    w_turn(2 * i + 2)
                if i + 1 < NP:
                    w_low(2 * i + 2)
                if i >= 1:
                    x1_sum(i - 1, 1)
                c0_low(2 * i + 1)
                if i == 0:
                    dve.wait_ge(bm_hi_done, 1)
                    for a in (1, 3):
                        at = slice(Q * a, Q * (a + 1))
                        nc.vector.tensor_tensor(bm_parts[at], bm4[at], f32(bm_parts[at]),
                                                ALU.subtract).then_inc(bm_done, 1)
            low0_low(NP - 1)
            low1_low(NP - 2)
            x1_sum(NP - 1, 0)
            x1_sum(NP - 1, 1)
            low1_low(NP - 1)
            for h in range(2):
                dve.wait_ge(zr_ready, h + 1)
                ps = bank[4 + h][:, 0:4 * 2 * NS].rearrange("p (b n) -> p b n", n=2 * NS)
                nc.vector.tensor_tensor(zr[:, 4 * h:4 * h + 4], ps[:, :, 0:NS],
                                        bias_small[:].unsqueeze(1).to_broadcast([P, 4, NS]),
                                        ALU.add).then_inc(zr_step, 1)
                dve.wait_ge(zr_step, h + 1)
                nc.vector.tensor_tensor(zr[:, 4 * h:4 * h + 4], ps[:, :, NS:2 * NS], zr[:, 4 * h:4 * h + 4],
                                        ALU.add).then_inc(zr_done, 1)
            dve.wait_ge(zr_done, 2)
            nc.vector.tensor_reduce(top[:], zr[:, :, R:NS].rearrange("p b (g e) -> p g b e", g=2), AX.XY, ALU.max,
                                    apply_absolute_value=True).then_inc(top_done, 1)
            dve.wait_ge(topt_ready, 1)
            nc.vector.tensor_reduce(r2[:, 0:1], bank[6][0:2, 0:S].rearrange("p (n two) -> p n two", two=2)[:, :, 1],
                                    AX.X, ALU.max).then_inc(r_step, 1)
            dve.wait_ge(r_step, 1)
            nc.vector.tensor_scalar(r2[:, 1:2], r2[:, 0:1], EPS, None, ALU.max).then_inc(r_step, 1)
            dve.wait_ge(r_step, 2)
            nc.vector.reciprocal(r2[:, 0:1], r2[:, 1:2]).then_inc(r_step, 1)
            dve.wait_ge(r_step, 3)
            nc.vector.tensor_scalar(r2d[:], ident[0:2, 0:2], r2[:, 0:1], GAMMA, ALU.mult, ALU.mult).then_inc(r_done, 1)
            dve.wait_ge(rb_ready, 1)
            nc.vector.tensor_copy(r_b[:], bank[6][:, S:S + 2]).then_inc(lg_step, 1)
            dve.wait_ge(lg_step, 1)
            nc.vector.tensor_scalar(lgd[:], zr[:, :, R + NE:NS], r_b[:, 1:2], None, ALU.mult).then_inc(lg_step, 1)
            dve.wait_ge(lg_step, 2)
            nc.vector.scalar_tensor_tensor(lg[:], zr[:, :, R:R + NE], r_b[:, 0:1], lgd[:], ALU.mult,
                                           ALU.add).then_inc(lg_step, 1)
            dve.wait_ge(lg_step, 3)
            for b in range(NB):
                last = nc.vector.max(mx[:, b], lg[:, b])
            last.then_inc(lg_step, 1)
            dve.wait_ge(lg_step, 4)
            nc.vector.tensor_tensor(sub[:, :, 0:NE], lg[:], mx[:, :, 0:1].to_broadcast([P, NB, NE]), ALU.subtract)
            nc.vector.tensor_tensor(sub[:, :, NE:NE + 1], mx[:, :, 1:2], mx[:, :, 0:1], ALU.subtract).then_inc(sub_done, 1)
            dve.wait_ge(ex_done, 1)
            nc.vector.tensor_reduce(tot[:, 0], ex[:, :, 0:NE], AX.X, ALU.add).then_inc(prob_step, 1)
            dve.wait_ge(prob_step, 1)
            nc.vector.reciprocal(tot[:, 1], tot[:, 0]).then_inc(prob_step, 1)
            dve.wait_ge(prob_step, 2)
            nc.vector.tensor_tensor(prob[:], ex[:], tot[:, 1].unsqueeze(2).to_broadcast([P, NB, NE + 1]),
                                    ALU.mult).then_inc(prob_step, 1)
            dve.wait_ge(prob_step, 3)
            nc.vector.tensor_tensor(gate[:], prob[:, :, 0:NE], prob[:, :, NE:NE + 1].to_broadcast([P, NB, NE]),
                                    ALU.subtract).then_inc(gate_in, 1)
            dve.wait_ge(gate_exp, 1)
            nc.vector.tensor_scalar(gate[:], gate[:], 1.0, None, ALU.add).then_inc(prob_step, 1)
            dve.wait_ge(prob_step, 4)
            nc.vector.reciprocal(gate[:], gate[:]).then_inc(prob_step, 1)
            dve.wait_ge(prob_step, 5)
            nc.vector.tensor_tensor(gate[:], gate[:], prob[:, :, 0:NE], ALU.mult).then_inc(prob_step, 1)
            dve.wait_ge(prob_step, 6)
            nc.vector.tensor_reduce(tot[:, 2], gate[:], AX.X, ALU.add).then_inc(prob_step, 1)
            dve.wait_ge(prob_step, 7)
            nc.vector.tensor_scalar(tot[:, 3], tot[:, 2], 1e-9, None, ALU.add).then_inc(prob_step, 1)
            dve.wait_ge(prob_step, 8)
            nc.vector.reciprocal(tot[:, 0], tot[:, 3]).then_inc(prob_step, 1)
            dve.wait_ge(prob_step, 9)
            nc.vector.tensor_tensor(wgt[:], gate[:], tot[:, 0].unsqueeze(2).to_broadcast([P, NB, NE]),
                                    ALU.mult).then_inc(wgt_done, 1)
            dve.wait_ge(wt_ready, 1)
            nc.vector.tensor_copy(w_tok.rearrange("p (n two) -> p n two", two=2),
                                  bank[7][0:NB * NE, 0:S].rearrange("p (n two) -> p n two", two=2)[:, :, 1:2]
                                  .to_broadcast([NB * NE, S // 2, 2])).then_inc(wt_done, 1)
            dve.wait_ge(pm_ready, 1)
            nc.vector.scalar_tensor_tensor(zp, bank[6][:, 256:256 + NB * R].rearrange("p (b r) -> p b r", r=R),
                                           SCALING, zr[:, :, 0:R], ALU.mult, ALU.mult).then_inc(zp_done, 1)
            dve.wait_ge(zp_done, 1)
            nc.vector.tensor_copy(zp_hi[:], zp).then_inc(zp_hi_done, 1)
            dve.wait_ge(zp_hi_done, 1)
            nc.vector.tensor_tensor(zs[:, :, 2:4, :], zp.unsqueeze(2).to_broadcast([P, NB, 2, R]),
                                    f32(zp_hi[:]).unsqueeze(2).to_broadcast([P, NB, 2, R]),
                                    ALU.subtract).then_inc(zs_lo_done, 1)
            for b in range(NB):
                dve.wait_ge(out_ready, b + 1)
                if b >= 4:
                    dve.wait_ge(out_stored[b % 4], 16 * (b // 4))
                nc.vector.tensor_tensor(out_sb[:, b % 4], bank[OUT_BANK[b]][:], bias_all[:],
                                        ALU.add).then_inc(out_done, 1)

        @block.tensor
        def _(pe):
            mm = nc.tensor.matmul

            def product(o, parts, rest=None, start=True, stop=True):
                for n, (st, mv) in enumerate(parts):
                    ins = mm(o, st, mv, start=start and n == 0, stop=stop and n == len(parts) - 1)
                return ins

            def three(hi, lo, mhi, mlo):
                return [(hi, mhi), (hi, mlo), (lo, mhi)]

            def wide(o, at, parts):
                for n, (st, mv) in enumerate(parts):
                    ins = mm(o[:, at:at + mv.shape[-1]], st, mv, start=n == 0, stop=n == len(parts) - 1)
                return ins

            def layer_a(b):
                i = b // 2
                if b >= 2:
                    pe.wait_ge(c0_saved, b - 1)
                else:
                    pe.wait_ge(m_lo_done, b + 1)
                pe.wait_ge(x_hi_done, i + 1)
                pe.wait_ge(x_lo_done, i + 1)
                pe.wait_ge(w_hi_done, 2 * b + 2)
                pe.wait_ge(w_lo_done, 2 * b + 2)
                parts = []
                for c in range(C):
                    parts += three(tok(x_hi[:, i % 2, c], b), tok(x_lo[:, i % 2, c], b),
                                   w_hi[:, b % 2, c], w_lo[:, b % 2, c])
                product(bank[b % 2][:], parts).then_inc(c0_ready, 1)

            def turn_c0(b):
                pe.wait_ge(c0_saved, b + 1)
                if b >= 2:
                    pe.wait_ge(c0t_lo_done, b - 1)
                else:
                    pe.wait_ge(m_lo_done, b + 3)
                for c in range(C):
                    last = nc.tensor.transpose(bank[2 + b % 2][:, S * c:S * (c + 1)], chunk(c0_row[:, b % 2], c),
                                               ident[:])
                last.then_inc(c0t_ready, 1)

            def low0(i):
                pe.wait_ge(c0t_lo_done, 2 * i + 2)
                if i >= 1:
                    pe.wait_ge(low0_lo_done, i)
                else:
                    pe.wait_ge(aux_lo, 2)
                parts = []
                for c in range(C):
                    parts += [(a0_t[:, c], c0_hi[:, i % 2, c]), (a0_t[:, c], c0_lo[:, i % 2, c])]
                product(bank[6][0:2 * K0, 0:2 * S], parts).then_inc(low0_ready, 1)

            def layer_b(i, h):
                if i >= 1:
                    pe.wait_ge(x1_summed, 2 * (i - 1) + h + 1)
                else:
                    pe.wait_ge(w1_hi_done, 4)
                    pe.wait_ge(w1_lo_done, 3)
                    pe.wait_ge(w1_lo_pool, 1)
                    pe.wait_ge(bias_done, 1)
                    pe.wait_ge(aux_lo, 3)
                for m in (2 * h, 2 * h + 1):
                    o = bank[4 + h][:, 2 * S * (m % 2):2 * S * (m % 2 + 1)]
                    parts = []
                    for c in range(C):
                        parts += three(chunk(w1_hi[:, c], m), chunk(w1_lo[:, c], m),
                                       c0_hi[:, i % 2, c], c0_lo[:, i % 2, c])
                    product(o, parts, stop=False)
                    pe.wait_ge(low0_lo_done, i + 1)
                    last = product(o, three(chunk(b0_hi[:], m), chunk(b0_lo[:], m), low0_hi[:], low0_lo[:]),
                                   start=False)
                last.then_inc(y_ready, 1)

            def low1(i):
                pe.wait_ge(x1_lo_done, 2 * i + 2)
                if i >= 1:
                    pe.wait_ge(low1_lo_done, i)
                else:
                    pe.wait_ge(aux_lo, 3)
                parts = []
                for c in range(C):
                    parts += three(a1_hi[:, c], a1_lo[:, c], x1_hi[i][:, c], x1_lo[i][:, c])
                product(bank[7][:, 0:2 * S], parts).then_inc(low1_ready, 1)

            def turn_w3(c):
                for t in range(C):
                    at = D * t + P * c
                    last = nc.tensor.transpose(bank[c][:, P * t:P * (t + 1)],
                                               w_in[:, w_slot("w3")[0], at:at + P], ident[:])
                last.then_inc(w3t_ready, 1)

            pe.wait_ge(ident_done, 1)
            slot, landed = w_slot("w3")
            pe.wait_ge(w_landed[slot], landed)
            for c in range(C):
                turn_w3(c)
            pe.wait_ge(b1_lo_done, 1)
            parts = []
            for c in range(C):
                pe.wait_ge(w3_lo_done, c + 1)
                parts += three(b1_hi[:, c], b1_lo[:, c], w1_hi[:, c], w1_lo[:, c])
            product(bank[7][:], parts).then_inc(be_ready, 1)
            pe.wait_ge(ld["A"], loads["A"])
            for c in range(C):
                last = nc.tensor.transpose(bank[4][0:R, P * c:P * (c + 1)], small[:, c, 0:R], ident[:])
            last.then_inc(at_ready, 1)
            pe.wait_ge(at_saved, 1)
            pe.wait_ge(ld["l"], loads["l"])
            for c in range(C):
                last = mm(bank[4][:, NE * c:NE * (c + 1)], a_t[:, c], l_t[:], start=True, stop=True)
            last.then_inc(al_ready, 1)
            pe.wait_ge(w2_lo_done, C)
            pe.wait_ge(ident_r_done, 1)
            for m in range(C):
                parts = []
                for c in range(C):
                    parts += three(chunk(w_hi[:, 1, c], m), chunk(w_lo[:, 1, c], m), w1_hi[:, c], w1_lo[:, c])
                o = bank[M_BANK[m]]
                product(o[:], parts, stop=False)
                for a in range(4):
                    at = P * a + Q * m
                    last = mm(o[:, at:at + Q], ident_r[:], ident_r[:, Q * a:Q * (a + 1)], start=False, stop=a == 3)
                last.then_inc(m_ready, 1)
            pe.wait_ge(small_lo_done, 1)
            for m in range(C + 1):
                parts = []
                for c in range(C):
                    hi, lo = ((chunk(w_hi[:, 1, c], m), chunk(w_lo[:, 1, c], m)) if m < C
                              else (b1_hi[:, c], b1_lo[:, c]))
                    parts += [(hi, small_parts[:, c]), (lo, small_parts[:, c, 0:NS])]
                wide(bank[5], 2 * NS * m, parts)
            pe.wait_ge(b1_lo_done, 2)
            parts = []
            for c in range(C):
                hi, lo = (b[:, c:c + 1].to_broadcast([P, P]) for b in (b2_hi, b2_lo))
                parts += [(hi, small_parts[:, c, 0:NS]), (hi, small_parts[:, c, NS:]), (lo, small_parts[:, c, 0:NS])]
            product(bank[6][:, 0:NS], parts).then_inc(smalls_ready, 1)
            pe.wait_ge(small_done, 1)
            parts = []
            for c in range(C):
                hi, lo = (b[:, c:c + 1].to_broadcast([P, P]) for b in (b2_hi, b2_lo))
                parts += three(hi, lo, w1_hi[:, c], w1_lo[:, c])
            product(bank[4][:], parts).then_inc(bias_ready, 1)

            pe.wait_ge(rows_ready, 1)
            pe.wait_ge(be_scaled, 1)
            for c in range(C):
                last = nc.tensor.transpose(bank[7][:, K0 * c:K0 * (c + 1)], chunk(a0_row, c), ident[0:K0, 0:K0])
            last.then_inc(aux_ready, 1)
            pe.wait_ge(rows_ready, 2)
            pe.wait_ge(bsm_step, 1)
            for c in range(C):
                last = nc.tensor.transpose(bank[6][0:2 * K0, P * c:P * (c + 1)],
                                           b0_row[:, c].rearrange("p g k -> p (g k)"), ident[:])
            last.then_inc(aux_ready, 1)
            pe.wait_ge(rows_ready, 3)
            pe.wait_ge(ae_summed, 2)
            for c in range(C):
                last = nc.tensor.transpose(bank[5][:, K1 * c:K1 * (c + 1)], chunk(a1_row, c), ident[:])
            last.then_inc(aux_ready, 1)

            layer_a(0)
            layer_a(1)
            turn_c0(0)
            turn_c0(1)
            for i in range(1, NP):
                layer_a(2 * i)
                low0(i - 1)
                if i >= 2:
                    low1(i - 2)
                layer_b(i - 1, 0)
                turn_c0(2 * i)
                layer_a(2 * i + 1)
                layer_b(i - 1, 1)
                turn_c0(2 * i + 1)
            low0(NP - 1)
            low1(NP - 2)
            layer_b(NP - 1, 0)
            layer_b(NP - 1, 1)

            def small_outputs(b):
                i, o = b // 2, bank[4 + b // 4]
                at = 2 * NS * (b % 4)
                parts = []
                for c in range(C):
                    parts += [(tok(x1_hi[i][:, c], b), ae[:, c]), (tok(x1_lo[i][:, c], b), ae[:, c, 0:NS])]
                parts += [(low1_hi[:, b], bes[:]), (low1_lo[:, b], bes[:, 0:NS])]
                pe.wait_ge(low1_lo_done, i + 1)
                last = wide(o, at, parts)
                if b % 4 == 3:
                    last.then_inc(zr_ready, 1)

            def second_layer(b):
                i = b // 2
                parts = []
                for c in range(C):
                    parts += three(tok(x1_hi[i][:, c], b), tok(x1_lo[i][:, c], b), m_hi[:, c], m_lo[:, c])
                parts += three(low1_hi[:, b], low1_lo[:, b], be_hi[:], be_lo[:])
                product(bank[OUT_BANK[b]][:], parts, stop=False)

            def routed(b):
                product(bank[OUT_BANK[b]][:], [(z_parts[:, b], bm_parts[:])], start=False).then_inc(out_ready, 1)

            pe.wait_ge(x1_summed, 2 * NP - 1)
            pe.wait_ge(ae_done, 2)
            for b in range(4):
                small_outputs(b)
            low1(NP - 1)
            pe.wait_ge(x1_summed, 2 * NP)
            for b in range(4, NB):
                small_outputs(b)
            pe.wait_ge(be_done, 1)
            pe.wait_ge(c0_saved, NB)
            second_layer(0)
            pe.wait_ge(top_done, 1)
            nc.tensor.transpose(bank[6][0:2, 0:S], top[:], ident[:]).then_inc(topt_ready, 1)
            second_layer(1)
            pe.wait_ge(r_done, 1)
            pe.wait_ge(ones_done, 1)
            mm(bank[6][:, S:S + 2], ones2[:], r2d[:], start=True, stop=True).then_inc(rb_ready, 1)
            pe.wait_ge(c0t_lo_done, NB)
            second_layer(2)
            second_layer(3)
            pe.wait_ge(wgt_done, 1)
            nc.tensor.transpose(bank[7][0:NB * NE, 0:S], wgt[:].rearrange("p b e -> p (b e)"),
                                ident[:]).then_inc(wt_ready, 1)
            pe.wait_ge(wt_done, 1)
            pe.wait_ge(ldiag_step, 2)
            mm(bank[6][:, 256:256 + NB * R], w_tok, l_diag[:].rearrange("k b r -> k (b r)"), start=True, stop=True).then_inc(pm_ready, 1)
            second_layer(4)
            pe.wait_ge(zs_hi_done, 1)
            pe.wait_ge(zs_lo_done, 1)
            for b in range(NB):
                last = nc.tensor.transpose(bank[4 + b // 4][:, S * (b % 4):S * (b % 4 + 1)],
                                           zs[:, b].rearrange("p g r -> p (g r)"), ident[:])
                if b % 4 == 3:
                    last.then_inc(zst_ready, 1)
            second_layer(5)
            pe.wait_ge(zst_saved, 2)
            pe.wait_ge(bm_done, 2)
            for b in range(6):
                routed(b)
            for b in range(6, NB):
                pe.wait_ge(out_done, b - 5)
                second_layer(b)
                routed(b)


M_BANK = [0, 1, 2, 3]
OUT_BANK = [0, 1, 2, 3, 7, 6, 0, 1]

_INS = ["x", "itok_B_3_7", "itok_B_1_7", "L0_cond_weight", "L0_ffn_weight", "L0_ffn_bias", "L0_ffn_lora_A",
        "L0_ffn_lora_B", "L0_ffn_lora_start_indices", "L1_cond_weight", "L1_cond_bias", "L1_cond_lora_a_weights",
        "L1_cond_lora_b_weights", "L1_cond_scaling_factors", "L1_ffn_W", "L1_ffn_b", "L1_ffn_A", "L1_ffn_Bmat",
        "L1_ffn_LiMEs"]


def kernel(**inputs):
    import numpy as np
    from concourse import bacc
    from concourse.bass_utils import run_bass_kernel_spmd

    nc = bacc.Bacc("TRN2", target_bir_lowering=False, num_devices=1)
    arrays, args = {}, []
    for name in _INS:
        a = np.ascontiguousarray(inputs[name])
        if name == "itok_B_3_7":
            a = a.reshape(1, -1)
        arrays["in_" + name] = a
        args.append(nc.dram_tensor("in_" + name, a.shape, mybir.dt.from_np(a.dtype), kind="ExternalInput").ap())
    shape = inputs["x"].shape
    args.append(nc.dram_tensor("out_dram", shape, F32, kind="ExternalOutput").ap())
    build(nc, *args)
    r = run_bass_kernel_spmd(nc, [arrays], core_ids=[0])
    return r.results[0]["out_dram"]
```

```python
from contextlib import ExitStack

import concourse.bass as bass
from concourse import mybir

F32 = mybir.dt.float32
F32R = mybir.dt.float32r
I32 = mybir.dt.int32
ALU = mybir.AluOpType
ACT = mybir.ActivationFunctionType
AX = mybir.AxisListType

P = 128
Q = 32
EPS = 1e-6
GAMMA = 0.5
SOFT_TOPK_TEMP = 0.5
ALPHA = 16.0


def build(nc, x, id0, id1, W0, W1, bias1, A0, B0, starts, W2, b2, a1, B1, s1, W3, b3, A, Bmat, L, out):
    NB, S, D = x.shape
    NW = W0.shape[0]
    C = D // P
    TB = D // Q
    NL0, R0, _ = A0.shape
    NL1, R1, _ = a1.shape
    K0 = NL0 * R0
    K1 = NL1 * R1
    R = A.shape[1]
    NE = L.shape[0]
    NS = R + 2 * NE
    NP = NB // 2
    SCALING = ALPHA / R
    assert S == P and K1 == P and 2 * K0 <= P and D == 512 and 4 * R == P and NB % 2 == 0

    ctx = ExitStack()
    with ctx, nc.allow_non_contiguous_dma(reason="three vectors of a few hundred values"):
        def sb(name, shape, dt=F32):
            return ctx.enter_context(nc.sbuf_tensor(name, shape, dt))

        def sem(name):
            return ctx.enter_context(nc.semaphore(name))

        RING = 2
        w_in = sb("w_in", [P, RING, C * D])
        w_t = sb("w_t", [P, C * D])
        w_hi = sb("w_hi", [P, 2, C, D], F32R)
        w_lo = sb("w_lo", [P, 2, C, D], F32R)
        w1_hi = sb("w1_hi", [P, C, D], F32R)
        w1_lo = sb("w1_lo", [P, C, D], F32R)
        m_hi = sb("m_hi", [P, C, D], F32R)
        m_lo = sb("m_lo", [P, C, D], F32R)
        x_in = sb("x_in", [P, 2 * D])
        x_t = sb("x_t", [P, 3, 2 * D])
        x_hi = sb("x_hi", [P, 2, C, 2 * S], F32R)
        x_lo = sb("x_lo", [P, 2, C, 2 * S], F32R)
        c0_row = sb("c0_row", [P, 2, D])
        c0_hi = sb("c0_hi", [P, 2, C, 2 * S], F32R)
        c0_lo = sb("c0_lo", [P, 2, C, 2 * S], F32R)
        x1_t = sb("x1_t", [P, C, 2 * S])
        with nc.sbuf_tensor("early", [P, (NP - 1) * 2 * C * 2 * S], F32) as early:
            pass
        x1_parts = sb("x1_parts", [P, NP - 1, 2, C, 2 * S], F32R)
        x1_hi = [x1_parts[:, i, 0] for i in range(NP - 1)]
        x1_lo = [x1_parts[:, i, 1] for i in range(NP - 1)]
        x1_hi.append(w_hi[:, 0, :, 0:2 * S])
        x1_lo.append(w_lo[:, 0, :, 0:2 * S])
        low0_hi = sb("low0_hi", [2 * K0, 2 * S], F32R)
        low0_lo = sb("low0_lo", [2 * K0, 2 * S], F32R)
        low1_hi = sb("low1_hi", [P, NB, S], F32R)
        low1_lo = sb("low1_lo", [P, NB, S], F32R)
        a0_t = sb("a0_t", [P, C, 2 * K0], F32R)
        b0_hi = sb("b0_hi", [2 * K0, D], F32R)
        b0_lo = sb("b0_lo", [2 * K0, D], F32R)
        a1_hi = sb("a1_hi", [P, C, K1], F32R)
        a1_lo = sb("a1_lo", [P, C, K1], F32R)
        be_hi = sb("be_hi", [K1, D], F32R)
        be_lo = sb("be_lo", [K1, D], F32R)
        ae = sb("ae", [P, C, 2 * NS], F32R)
        bes = sb("bes", [K1, 2 * NS], F32R)
        l_t = sb("l_t", [R, NE])
        l_rep = sb("l_rep", [NB * NE, R])
        l_diag = sb("l_diag", [NB * NE, NB, R])
        bm_parts = sb("bm_parts", [P, D], F32R)
        bias_all = sb("bias_all", [P, D])
        bias_small = sb("bias_small", [2 * NS, 1])
        bias1_c = sb("bias1_c", [P, C])
        b3_c = sb("b3_c", [R + NE, 1])
        b2_c = sb("b2_c", [P, C])
        b2_parts = sb("b2_parts", [P, C, 2], F32R)
        s_c = sb("s_c", [P, 1])
        ident = sb("ident", [P, P])
        ident_r = sb("ident_r", [P, P], F32R)
        ones2 = sb("ones2", [2, P])
        ids_i = sb("ids_i", [P, NB], I32)
        starts_i = sb("starts_i", [P, NL0 + 1], I32)
        iota_i = sb("iota_i", [P, 1 + NB], I32)
        part_f = sb("part_f", [P, 1])
        group_f = sb("group_f", [P, 3])
        ids_f = sb("ids_f", [P, NB])
        starts_f = sb("starts_f", [P, NL0 + 1])
        batch_f = sb("batch_f", [P, NB])
        seg_f = sb("seg_f", [P, NB])
        started = sb("started", [P, NB, NL0 + 1])
        mask0 = sb("mask0", [P, NB])
        mask1 = sb("mask1", [P, NB])
        top = sb("top", [P, 2])
        r2 = sb("r2", [2, 2])
        r2d = sb("r2d", [2, 2])
        r_b = sb("r_b", [P, 2])
        lg = sb("lg", [P, NB, NE])
        lgd = sb("lgd", [P, NB, NE])
        mx = sb("mx", [P, NB, 8])
        sub = sb("sub", [P, NB, NE + 1])
        ex = sb("ex", [P, NB, NE + 1])
        prob = sb("prob", [P, NB, NE + 1])
        gate = sb("gate", [P, NB, NE])
        wgt = sb("wgt", [P, NB, NE])
        tot = sb("tot", [P, 4, NB])
        zp_hi = sb("zp_hi", [P, NB, R], F32R)
        used = [0]

        def early_part(n):
            used[0] += n
            return early[:, used[0] - n:used[0]]

        b1_row = early_part(C * K1).rearrange("p (n cr) -> p n cr", n=NL1)
        a1_row = early_part(D)
        b0_in = early_part(C * K0).rearrange("p (c n r) -> p c n r", c=C, n=NL0)
        small = early_part(C * NS).rearrange("p (c n) -> p c n", n=NS)
        be_f, bes_f = early_part(D), early_part(NS)
        ae_f = early_part(C * NS).rearrange("p (c n) -> p c n", n=NS)
        ae_rows = early_part(D)[0:2 * NS]
        a_t = early_part(C * P)[0:R].rearrange("p (c k) -> p c k", k=P)
        bm4 = early_part(D)
        w1_t = early_part(C * D)
        a0_row = c0_row[0:K0, 1]
        b0_row = c0_row[:, 0, 0:C * 2 * K0].rearrange("p (c g k) -> p c g k", c=C, g=2)
        b1_hi = c0_hi[:, 1, 0:2].rearrange("p c s -> p (c s)").rearrange("p (c k) -> p c k", k=K1)
        b1_lo = c0_hi[:, 1, 2:4].rearrange("p c s -> p (c s)").rearrange("p (c k) -> p c k", k=K1)
        small_parts = c0_hi[:, 0, :, 0:2 * NS]
        z_t = x_t[0:2 * NS, 1]
        zr = x_in[:, 0:NB * NS].rearrange("p (b n) -> p b n", n=NS)
        zp = x_in[:, NB * NS:NB * (NS + R)].rearrange("p (b r) -> p b r", r=R)
        w_tok = x_in[0:NB * NE, NB * (NS + R):NB * (NS + R) + S]
        zs = w_t[:, 0:NB * P].rearrange("p (b g r) -> p b g r", b=NB, g=4)
        z_parts = c0_hi[:, 0].rearrange("p c s -> p (c s)").rearrange("p (b s) -> p b s", b=NB)
        out_sb = w_in[:, 1].rearrange("p (n d) -> p n d", d=D)

        bank = [ctx.enter_context(nc.psum_tensor(f"bank{n}", [P, D], F32)) for n in range(8)]

        ld = {n: sem("landed_" + n) for n in
              ("a0", "b0", "a1", "b1", "A", "l", "lr", "bm", "bias", "b3", "b1c", "b2c", "s", "ids", "starts")}
        w_landed = [sem(f"w_landed{n}") for n in range(RING)]
        w3_landed = [sem(f"w3_landed{t}") for t in range(C)]
        w2_landed = [sem(f"w2_landed{h}") for h in range(2)]
        x_landed = sem("x_landed")
        out_stored = [sem(f"out_stored{n}") for n in range(4)]
        ident_zero, ident_done, iota_done = sem("ident_zero"), sem("ident_done"), sem("iota_done")
        ones_done, ldiag_step = sem("ones_done"), sem("ldiag_step")
        rows_ready = sem("rows_ready")
        ident_r_done, bm_hi_done, bm_done = sem("ident_r_done"), sem("bm_hi_done"), sem("bm_done")
        mask_step, masks_done = sem("mask_step"), sem("masks_done")
        aux_ready, aux_hi, aux_lo = sem("aux_ready"), sem("aux_hi"), sem("aux_lo")
        b1_hi_done, b1_lo_done = sem("b1_hi_done"), sem("b1_lo_done")
        w_turned, w_hi_done, w_lo0_done = sem("w_turned"), sem("w_hi_done"), sem("w_lo0_done")
        w1_turned, w1_hi_done, w1_lo_done = sem("w1_turned"), sem("w1_hi_done"), sem("w1_lo_done")
        w_lo1_done, w2_lo_pool = sem("w_lo1_done"), sem("w2_lo_pool")
        b2_hi_done, b2_lo_done = sem("b2_hi_done"), sem("b2_lo_done")
        x_turned, x_hi_done, x_lo_done = sem("x_turned"), sem("x_hi_done"), sem("x_lo_done")
        c0_ready, c0_saved = sem("c0_ready"), sem("c0_saved")
        c0t_ready, c0t_hi_done, c0t_lo_done = sem("c0t_ready"), sem("c0t_hi_done"), sem("c0t_lo_done")
        low0_ready, low0_hi_done, low0_lo_done = sem("low0_ready"), sem("low0_hi_done"), sem("low0_lo_done")
        low1_ready, low1_hi_done, low1_lo_done = sem("low1_ready"), sem("low1_hi_done"), sem("low1_lo_done")
        y_ready, x1_summed = sem("y_ready"), sem("x1_summed")
        x1_hi_done, x1_lo_done = sem("x1_hi_done"), sem("x1_lo_done")
        at_ready, at_saved, al_ready = sem("at_ready"), sem("at_saved"), sem("al_ready")
        small_done, w3_small_done = sem("small_done"), sem("w3_small_done")
        w3t_ready, w3_hi_done, w3_lo_done = sem("w3t_ready"), sem("w3_hi_done"), sem("w3_lo_done")
        bias_ready, be_ready, smalls_ready = sem("bias_ready"), sem("be_ready"), sem("smalls_ready")
        bias_done, be_scaled, be_done, ae_saved = sem("bias_done"), sem("be_scaled"), sem("be_done"), sem("ae_saved")
        w2_hi_done, w2_lo_done, ae_summed = sem("w2_hi_done"), sem("w2_lo_done"), sem("ae_summed")
        ae_ready, aet_ready, aet_saved = sem("ae_ready"), sem("aet_ready"), sem("aet_saved")
        bes_saved, bes_summed, bes_done = sem("bes_saved"), sem("bes_summed"), sem("bes_done")
        zt_ready, zt_saved = sem("zt_ready"), sem("zt_saved")
        small_hi_done, small_lo_done = sem("small_hi_done"), sem("small_lo_done")
        ae_done, bsm_step = sem("ae_done"), sem("bsm_step")
        m_ready, m_hi_done, m_lo_done = sem("m_ready"), sem("m_hi_done"), sem("m_lo_done")
        zr_ready, zr_step, zr_done = sem("zr_ready"), sem("zr_step"), sem("zr_done")
        top_done, topt_ready, r_step, r_done = sem("top_done"), sem("topt_ready"), sem("r_step"), sem("r_done")
        rb_ready, lg_step, sub_done, ex_done = sem("rb_ready"), sem("lg_step"), sem("sub_done"), sem("ex_done")
        prob_step, gate_in, gate_exp, wgt_done = sem("prob_step"), sem("gate_in"), sem("gate_exp"), sem("wgt_done")
        wt_ready, wt_done, pm_ready, zp_done = sem("wt_ready"), sem("wt_done"), sem("pm_ready"), sem("zp_done")
        zp_hi_done, zs_hi_done, zs_lo_done = sem("zp_hi_done"), sem("zs_hi_done"), sem("zs_lo_done")
        zst_ready, zst_saved = sem("zst_ready"), sem("zst_saved")
        out_ready, out_done = sem("out_ready"), sem("out_done")

        def halves(ap, h):
            return ap.rearrange("p (t c q) -> p c t q", c=C, q=Q)[:, :, TB // 2 * h:TB // 2 * (h + 1), :]

        def rows(ap, h):
            return ap[:, :, D // 2 * h:D // 2 * (h + 1)].rearrange("p c (t q) -> p c t q", q=Q)

        def chunk(ap, c):
            return ap[:, P * c:P * (c + 1)]

        def tok(ap, b):
            return ap[..., S * (b % 2):S * (b % 2 + 1)]

        def columns(step):
            return slice(0, D) if step < NB - 1 else slice(D // 2 * (step - NB + 1), D // 2 * (step - NB + 2))

        def w3_part(ap, n):
            h, g = divmod(n, 2)
            return ap[:, 2 * g:2 * g + 2, D // 2 * h:D // 2 * (h + 1)]

        def w3_bank(n):
            return bank[n][:].rearrange("p (c r) -> p c r", c=2)

        def f32(ap):
            return ap.bitcast(F32)

        def by_adapter(ap):
            return ap.rearrange("p c (n r) -> p c n r", n=NL1)

        def w1_in(e):
            return w1_t.rearrange("p (e m c q) -> p e c m q", e=4, m=C, c=C)[:, e]

        def w1_out(ap, e):
            return ap[:].rearrange("p c (m e q) -> p e c m q", e=4, m=C)[:, e]

        def w2_in(c):
            return w_in[:, w_slot("w2")[0], D * c:D * (c + 1)].rearrange("p (e m q) -> p m e q", e=4, m=C)

        def w2_out(ap, c):
            return ap[:, 1, c].rearrange("p (m e q) -> p m e q", e=4, m=C)

        order = ["w3", "w2", 0, 1, "w1"] + list(range(2, NB))

        def w_slot(b):
            n = order.index(b)
            return n % RING, 64 * (n // RING)

        loads = {}

        block = ctx.enter_context(nc.Block())

        @block.sync
        def _(sp):
            def load(name, dst, src):
                sp.dma_start(dst, src).then_inc(ld[name], 16)
                loads[name] = loads.get(name, 0) + 16

            def load_x(i):
                if i >= 1:
                    sp.wait_ge(x_turned, i)
                src = x[2 * i:2 * i + 2].rearrange("b (t q) (a j) -> a q (b t) j", q=Q, a=4)
                for a in range(4):
                    dst = x_in[Q * a:Q * (a + 1), :].rearrange("q (n j) -> q n j", j=P)
                    sp.dma_start(dst, src[a]).then_inc(x_landed, 16)

            which = {}

            def read_ids(batches):
                for b in batches:
                    which[b] = sp.value_load(id0[0:1, b:b + 1], min_val=0, max_val=NW - 1)

            def load_w(b):
                slot, landed = w_slot(b)
                if b == 0:
                    sp.wait_ge(w3t_ready, C)
                elif b == 1:
                    sp.wait_ge(w2_hi_done, C)
                    sp.wait_ge(w2_lo_done, 2)
                    sp.wait_ge(w2_lo_pool, 2)
                elif b == "w1":
                    sp.wait_ge(w_turned, 2)
                elif b == 2:
                    sp.wait_ge(w_turned, 4)
                elif b == 3:
                    sp.wait_ge(w1_turned, 2)
                elif b not in ("w3", "w2"):
                    sp.wait_ge(w_turned, 2 * (b - 2) + 2)
                if b == "w3":
                    for t in range(C):
                        sp.dma_start(w_in[:, slot, D * t:D * (t + 1)], W3[P * t:P * (t + 1), :]
                                     ).then_inc(w3_landed[t], 16)
                    return
                if b == "w2":
                    src = W2.rearrange("(p h c) d -> h p (c d)", p=P, h=2)
                    for h in range(2):
                        sp.dma_start(w_in[:, slot, 2 * D * h:2 * D * (h + 1)], src[h]).then_inc(w2_landed[h], 16)
                    return
                if b == "w1":
                    src = W1.rearrange("(t q) (a j) -> a q t j", q=Q, a=4)
                else:
                    src = W0[bass.ds(which[b], 1)].rearrange("w (t q) (a j) -> a q (w t) j", q=Q, a=4)
                for a in range(4):
                    dst = w_in[Q * a:Q * (a + 1), slot, :].rearrange("q (t j) -> q t j", j=src.shape[-1])
                    sp.dma_start(dst, src[a]).then_inc(w_landed[slot], 16)

            def load_ordered(name, dst, src):
                for a in range(4):
                    load(name, dst.rearrange("k (c a q) -> k a c q", a=4, c=C)[:, a],
                         src.rearrange("n r (a c q) -> (n r) a c q", a=4, c=C)[:, a])

            load_w("w3")
            load_w("w2")
            load("A", small[:, :, 0:R], A.rearrange("(p c) r -> p c r", c=C))
            load_x(0)
            load("b1", b1_row, B1.rearrange("n (p c) r -> p n (c r)", c=C))
            read_ids((0, 1))
            load_w(0)
            read_ids((2, 3))
            load_x(1)
            load("bias", bias_all[:], b3.partition_broadcast(P))
            load_w(1)
            load_w("w1")
            load_ordered("a0", a0_row, A0)
            read_ids((4, 5))
            load_w(2)
            load_ordered("a1", a1_row, a1)
            load("bm", bm4, Bmat.unsqueeze(0).to_broadcast([4, R, D]))
            for i in range(1, NP):
                load_w(2 * i + 1)
                if i == 1:
                    for a in range(4):
                        at = slice(Q * a, Q * (a + 1))
                        load("b1c", bias1_c[at, :], bias1.rearrange("(a c q) -> a q c", a=4, q=Q)[a])
                    load("lr", l_rep[:], L.unsqueeze(0).to_broadcast([NB, NE, R]))
                if i + 1 < NP:
                    load_x(i + 1)
                    load_w(2 * i + 2)
                if i == 1:
                    read_ids((6, 7))
            for step in range(NB + 1):
                b, at = min(step, NB - 1), columns(step)
                sp.wait_ge(out_done, step + 1)
                sp.dma_start(out[b][:, at], out_sb[:, b % 4, at]).then_inc(out_stored[b % 4], 16)
            for n in range(4):
                sp.wait_ge(out_stored[n], 32 if n < 3 else 48)

        @block.gpsimd
        def _(pool):
            nc.gpsimd.memset(ident[:], 0.0).then_inc(ident_zero, 1)
            pool.wait_ge(ident_zero, 1)
            nc.gpsimd.affine_select(out=ident[:], in_=ident[:], compare_op=ALU.not_equal, fill=1.0, base=0,
                                    pattern=[[-1, P]], channel_multiplier=1).then_inc(ident_done, 1)
            nc.gpsimd.memset(ones2[:], 1.0).then_inc(ones_done, 1)
            nc.gpsimd.iota(iota_i[:, 0:1], [[0, 1]], base=0, channel_multiplier=1)
            nc.gpsimd.iota(iota_i[:, 1:1 + NB], [[1, NB]], base=0, channel_multiplier=0).then_inc(iota_done, 1)

            def x_low(i):
                if i >= 2:
                    pool.wait_ge(c0_ready, 2 * (i - 1))
                pool.wait_ge(x_hi_done, i + 1)
                view = x_t[:, i % 3].rearrange("p (n c q) -> p c n q", c=C, q=Q)
                split = [t.rearrange("p c (n q) -> p c n q", q=Q) for t in (x_hi[:, i % 2], x_lo[:, i % 2])]
                nc.gpsimd.tensor_tensor(split[1], view, f32(split[0]), ALU.subtract).then_inc(x_lo_done, 1)

            def x1_low(i, h):
                pool.wait_ge(x1_hi_done, 2 * i + h + 1)
                c = slice(2 * h, 2 * h + 2)
                nc.gpsimd.tensor_tensor(x1_lo[i][:, c], x1_t[:, c], f32(x1_hi[i][:, c]),
                                        ALU.subtract).then_inc(x1_lo_done, 1)

            def load(name, dst, src):
                nc.gpsimd.dma_start(dst, src).then_inc(ld[name], 16)
                loads[name] = loads.get(name, 0) + 16

            load("b2c", b2_c[:], b2.rearrange("(p c) -> p c", c=C))
            load("l", l_t[:], L.rearrange("e r -> r e"))
            load("s", s_c[:], s1.rearrange("(n one) -> n one", one=1).unsqueeze(1).to_broadcast([NL1, R1, 1]))
            load("b3", b3_c[R:R + NE, :], b3[0:NE].rearrange("(n one) -> n one", one=1))
            load("ids", ids_i[:], id1.partition_broadcast(P))
            load("starts", starts_i[:], starts.partition_broadcast(P))
            for c in (1, 3):
                pool.wait_ge(w2_hi_done, c + 1)
                nc.gpsimd.tensor_tensor(w2_out(w_lo, c), w2_in(c), f32(w2_out(w_hi, c)),
                                        ALU.subtract).then_inc(w2_lo_pool, 1)
            for n in range(NL0):
                load("b0", b0_in[:, :, n], B0[n].rearrange("(c p) r -> p c r", p=P))
            x_low(0)
            pool.wait_ge(ld["b0"], loads["b0"])
            for g in range(2):
                last = nc.gpsimd.tensor_copy(b0_row[:, :, g], b0_in.rearrange("p c n r -> p c (n r)"))
            last.then_inc(rows_ready, 1)
            def w_low(b, h=1):
                if b >= 2:
                    pool.wait_ge(c0_ready, b - 1)
                elif b == 1:
                    pool.wait_ge(ae_ready, 1)
                pool.wait_ge(w_hi_done, 2 * b + h + 1)
                nc.gpsimd.tensor_tensor(rows(w_lo[:, b % 2], h), halves(w_t[:], h), f32(rows(w_hi[:, b % 2], h)),
                                        ALU.subtract).then_inc(w_lo1_done if h else w_lo0_done, 1)

            w_low(0)
            x_low(1)
            w_low(1)
            pool.wait_ge(be_ready, 1)
            for e in range(4):
                pool.wait_ge(w1_hi_done, e + 1)
                nc.gpsimd.tensor_tensor(w1_out(w1_lo, e), w1_in(e), f32(w1_out(w1_hi, e)),
                                        ALU.subtract).then_inc(w1_lo_done, 1)
            w_low(2)
            pool.wait_ge(ld["lr"], loads["lr"])
            nc.gpsimd.affine_select(out=l_diag[:], in_=l_rep[:].unsqueeze(1).to_broadcast([NB * NE, NB, R]),
                                    compare_op=ALU.is_ge, fill=0.0, base=0, pattern=[[-NE, NB], [0, R]],
                                    channel_multiplier=1).then_inc(ldiag_step, 1)
            pool.wait_ge(ldiag_step, 1)
            nc.gpsimd.affine_select(out=l_diag[:], in_=l_diag[:], compare_op=ALU.is_ge, fill=0.0,
                                    base=NE - 1, pattern=[[NE, NB], [0, R]],
                                    channel_multiplier=-1).then_inc(ldiag_step, 1)
            pool.wait_ge(be_scaled, 2)
            nc.gpsimd.tensor_tensor(be_lo[:], be_f, f32(be_hi[:]), ALU.subtract).then_inc(be_done, 1)
            for i in range(1, NP):
                w_low(2 * i + 1, 0 if i == 1 else 1)
                if i + 1 < NP:
                    x_low(i + 1)
                    w_low(2 * i + 2)
                x1_low(i - 1, 0)
                x1_low(i - 1, 1)

        @block.scalar
        def _(act):
            def x_high(i):
                if i >= 2:
                    act.wait_ge(c0_ready, 2 * (i - 1))
                act.wait_ge(x_turned, i + 1)
                nc.scalar.copy(x_hi[:, i % 2].rearrange("p c (n q) -> p c n q", q=Q),
                               x_t[:, i % 3].rearrange("p (n c q) -> p c n q", c=C, q=Q)).then_inc(x_hi_done, 1)

            def w_high(b, half=range(2)):
                for h in half:
                    if b >= 2 and h == 0:
                        act.wait_ge(c0_ready, b - 1)
                    elif b == 1 and h == 0:
                        act.wait_ge(ae_ready, 1)
                    act.wait_ge(w_turned, 2 * b + h + 1)
                    nc.scalar.copy(rows(w_hi[:, b % 2], h), halves(w_t[:], h)).then_inc(w_hi_done, 1)

            def w1_high():
                act.wait_ge(be_ready, 1)
                for e in range(4):
                    act.wait_ge(w1_turned, e // 2 + 1)
                    nc.scalar.copy(w1_out(w1_hi, e), w1_in(e)).then_inc(w1_hi_done, 1)

            def w3_high(n):
                act.wait_ge(w3t_ready, n + 1)
                nc.scalar.copy(w3_part(w1_hi, n), w3_bank(n)).then_inc(w3_hi_done, 1)

            def m_high(m):
                act.wait_ge(m_ready, m + 1)
                nc.scalar.copy(m_hi[:, m], bank[M_BANK[m]][:]).then_inc(m_hi_done, 1)

            def low0_high(i):
                act.wait_ge(masks_done, 1)
                act.wait_ge(low0_ready, i + 1)
                if i >= 1:
                    act.wait_ge(y_ready, 2 * i)
                for j in range(2):
                    at = slice(S * j, S * (j + 1))
                    last = nc.scalar.activation(low0_hi[:, at], bank[6][0:2 * K0, at], ACT.Copy,
                                                scale=mask0[0:2 * K0, 2 * i + j:2 * i + j + 1])
                last.then_inc(low0_hi_done, 1)

            def low1_high(i):
                act.wait_ge(low1_ready, i + 1)
                for j in range(2):
                    b = 2 * i + j
                    last = nc.scalar.activation(low1_hi[:, b], bank[7][:, S * j:S * (j + 1)], ACT.Copy,
                                                scale=mask1[:, b:b + 1])
                last.then_inc(low1_hi_done, 1)

            def save_c0(b):
                if b < 2:
                    act.wait_ge(aux_ready, 2)
                if b >= 2:
                    act.wait_ge(c0t_ready, b - 1)
                act.wait_ge(c0_ready, b + 1)
                nc.scalar.copy(c0_row[:, b % 2].rearrange("p (c a q) -> p a c q", c=C, a=4),
                               bank[b % 2][:].rearrange("p (a c q) -> p a c q", c=C, a=4)).then_inc(c0_saved, 1)

            def c0_high(b):
                if b >= 4:
                    act.wait_ge(y_ready, 2 * (b // 2 - 1))
                act.wait_ge(c0t_ready, b + 1)
                nc.scalar.copy(tok(c0_hi[:, (b // 2) % 2], b),
                               bank[2 + b % 2][:].rearrange("p (c s) -> p c s", s=S)).then_inc(c0t_hi_done, 1)

            def x1_high(i, h):
                act.wait_ge(x1_summed, 2 * i + h + 1)
                c = slice(2 * h, 2 * h + 2)
                nc.scalar.copy(x1_hi[i][:, c], x1_t[:, c]).then_inc(x1_hi_done, 1)

            act.wait_ge(ident_done, 1)
            nc.scalar.copy(ident_r[:], ident[:]).then_inc(ident_r_done, 1)
            for n in range(C):
                w3_high(n)
            for c in range(C):
                act.wait_ge(w2_landed[c // 2], 16)
                nc.scalar.copy(w2_out(w_hi, c), w2_in(c)).then_inc(w2_hi_done, 1)
            x_high(0)
            act.wait_ge(at_ready, 1)
            nc.scalar.copy(a_t, bank[4][0:R, :].rearrange("p (c k) -> p c k", k=P)).then_inc(at_saved, 1)
            m_high(0)
            act.wait_ge(ld["b1"], loads["b1"])
            nc.scalar.copy(by_adapter(b1_hi), b1_row.rearrange("p n (c r) -> p c n r", c=C)).then_inc(b1_hi_done, 1)
            act.wait_ge(al_ready, 1)
            nc.scalar.copy(small[:, :, R + NE:NS],
                           bank[4][:, 0:C * NE].rearrange("p (c e) -> p c e", e=NE)).then_inc(small_done, 1)
            act.wait_ge(w3_small_done, 1)
            act.wait_ge(ld["A"], loads["A"])
            act.wait_ge(small_done, 1)
            nc.scalar.copy(small_parts[:, :, 0:NS], small).then_inc(small_hi_done, 1)
            act.wait_ge(ld["s"], loads["s"])
            w_high(0)
            m_high(1)
            x_high(1)
            m_high(2)
            m_high(3)
            w_high(1, (0,))
            act.wait_ge(smalls_ready, 1)
            nc.scalar.activation(bes_f, bank[6][:, 0:NS], ACT.Copy, scale=s_c[:, 0:1]).then_inc(bes_saved, 1)
            w_high(1, (1,))
            nc.scalar.copy(ae_rows, bank[5][0:2 * NS, :]).then_inc(ae_saved, 1)
            act.wait_ge(be_ready, 1)
            nc.scalar.activation(be_f, bank[7][:], ACT.Copy, scale=s_c[:, 0:1]).then_inc(be_scaled, 1)
            w1_high()
            act.wait_ge(be_scaled, 1)
            nc.scalar.copy(be_hi[:], be_f).then_inc(be_scaled, 1)
            save_c0(0)
            w_high(2)
            save_c0(1)
            c0_high(0)
            act.wait_ge(aux_ready, 1)
            nc.scalar.copy(a0_t[:, :, 0:K0], bank[7][:, 0:C * K0].rearrange("p (c k) -> p c k",
                           k=K0)).then_inc(aux_hi, 1)
            act.wait_ge(aux_ready, 2)
            nc.scalar.copy(b0_hi[:].rearrange("k (m e q) -> k m e q", e=4, m=C),
                           bank[6][0:2 * K0, :].rearrange("k (e m q) -> k m e q", e=4, m=C)).then_inc(aux_hi, 1)
            c0_high(1)
            act.wait_ge(aux_ready, 3)
            nc.scalar.copy(a1_hi[:], bank[5][:].rearrange("p (c k) -> p c k", k=K1)).then_inc(aux_hi, 1)
            act.wait_ge(bes_summed, 1)
            nc.scalar.copy(bes[:, 0:NS], bes_f).then_inc(bes_saved, 1)
            act.wait_ge(ae_summed, 1)
            nc.scalar.copy(ae[:, :, 0:NS], ae_f).then_inc(ae_saved, 1)
            act.wait_ge(ld["bm"], loads["bm"])
            nc.scalar.copy(bm_parts[:], bm4).then_inc(bm_hi_done, 1)
            for i in range(1, NP):
                if i == 1:
                    low0_high(i - 1)
                w_high(2 * i + 1, (0,))
                save_c0(2 * i)
                if i >= 2:
                    low0_high(i - 1)
                w_high(2 * i + 1, (1,))
                if i >= 2:
                    low1_high(i - 2)
                if i + 1 < NP:
                    x_high(i + 1)
                    w_high(2 * i + 2)
                c0_high(2 * i)
                x1_high(i - 1, 0)
                save_c0(2 * i + 1)
                c0_high(2 * i + 1)
                x1_high(i - 1, 1)
            low0_high(NP - 1)
            low1_high(NP - 2)
            x1_high(NP - 1, 0)
            x1_high(NP - 1, 1)
            low1_high(NP - 1)
            act.wait_ge(sub_done, 1)
            nc.scalar.activation(ex[:], sub[:], ACT.Exp).then_inc(ex_done, 1)
            act.wait_ge(gate_in, 1)
            nc.scalar.activation(gate[:], gate[:], ACT.Exp, scale=-1.0 / SOFT_TOPK_TEMP).then_inc(gate_exp, 1)
            act.wait_ge(zp_hi_done, 1)
            hi2 = f32(zp_hi[:]).unsqueeze(2).to_broadcast([P, NB, 2, R])
            nc.scalar.copy(zs[:, :, 0:2, :], hi2).then_inc(zs_hi_done, 1)
            act.wait_ge(zst_ready, 1)
            nc.scalar.copy(z_parts[:, 0:4], bank[4][:].rearrange("p (b s) -> p b s", s=S)).then_inc(zst_saved, 1)
            act.wait_ge(zst_ready, 2)
            nc.scalar.copy(z_parts[:, 4:8], bank[5][:].rearrange("p (b s) -> p b s", s=S)).then_inc(zst_saved, 1)

        @block.vector
        def _(dve):
            def x_turn(i):
                dve.wait_ge(x_landed, 64 * (i + 1))
                if i >= 3:
                    dve.wait_ge(x1_summed, 2 * (i - 2))
                nc.vector.transpose(x_t[:, i % 3], x_in[:]).then_inc(x_turned, 1)

            def w_turn(b):
                slot, landed = w_slot(b)
                dve.wait_ge(w_landed[slot], landed)
                for h in range(2):
                    if b >= 1:
                        dve.wait_ge(w_hi_done, 2 * (b - 1) + h + 1)
                        dve.wait_ge(w_lo1_done if h == 1 else w_lo0_done, b)
                    at = slice(D * C // 2 * h, D * C // 2 * (h + 1))
                    nc.vector.transpose(w_t[:, at], w_in[:, slot, at]).then_inc(w_turned, 1)

            def w_low(b, h=0):
                if b >= 2:
                    dve.wait_ge(c0_ready, b - 1)
                elif b == 1:
                    dve.wait_ge(ae_ready, 1)
                dve.wait_ge(w_hi_done, 2 * b + h + 1)
                nc.vector.tensor_tensor(rows(w_lo[:, b % 2], h), halves(w_t[:], h), f32(rows(w_hi[:, b % 2], h)),
                                        ALU.subtract).then_inc(w_lo1_done if h else w_lo0_done, 1)

            def w1_turn():
                slot, landed = w_slot("w1")
                dve.wait_ge(w_landed[slot], landed)
                for h in range(2):
                    half = slice(D * C // 2 * h, D * C // 2 * (h + 1))
                    nc.vector.transpose(w1_t[:, half], w_in[:, slot, half]).then_inc(w1_turned, 1)

            def w3_low(n):
                dve.wait_ge(w3_hi_done, n + 1)
                nc.vector.tensor_tensor(w3_part(w1_lo, n), w3_bank(n), f32(w3_part(w1_hi, n)),
                                        ALU.subtract).then_inc(w3_lo_done, 1)

            def c0_low(b):
                if b >= 4:
                    dve.wait_ge(y_ready, 2 * (b // 2 - 1))
                dve.wait_ge(c0t_hi_done, b + 1)
                nc.vector.tensor_tensor(tok(c0_lo[:, (b // 2) % 2], b),
                                        bank[2 + b % 2][:].rearrange("p (c s) -> p c s", s=S),
                                        f32(tok(c0_hi[:, (b // 2) % 2], b)), ALU.subtract).then_inc(c0t_lo_done, 1)

            def low0_low(i):
                if i >= 1:
                    dve.wait_ge(y_ready, 2 * i)
                dve.wait_ge(low0_hi_done, i + 1)
                for j in range(2):
                    at = slice(S * j, S * (j + 1))
                    last = nc.vector.scalar_tensor_tensor(low0_lo[:, at], bank[6][0:2 * K0, at],
                                                          mask0[0:2 * K0, 2 * i + j:2 * i + j + 1],
                                                          f32(low0_hi[:, at]), ALU.mult, ALU.subtract)
                last.then_inc(low0_lo_done, 1)

            def low1_low(i):
                dve.wait_ge(low1_hi_done, i + 1)
                for j in range(2):
                    b = 2 * i + j
                    last = nc.vector.scalar_tensor_tensor(low1_lo[:, b], bank[7][:, S * j:S * (j + 1)],
                                                          mask1[:, b:b + 1], f32(low1_hi[:, b]),
                                                          ALU.mult, ALU.subtract)
                last.then_inc(low1_lo_done, 1)

            def small_saved(i):
                dve.wait_ge(zt_ready, i + 1)
                nc.vector.tensor_scalar(z_t[:, 2 * S * i:2 * S * (i + 1)],
                                        bank[ZT_BANK[i]][0:2 * NS, 0:2 * S],
                                        bias_small[:, 0:1], None, ALU.add).then_inc(zt_saved, 1)

            def m_low(m):
                dve.wait_ge(m_hi_done, m + 1)
                nc.vector.tensor_tensor(m_lo[:, m], bank[M_BANK[m]][:], f32(m_hi[:, m]),
                                        ALU.subtract).then_inc(m_lo_done, 1)

            def x1_low(i):
                for h in range(2):
                    dve.wait_ge(x1_hi_done, 2 * i + h + 1)
                    c = slice(2 * h, 2 * h + 2)
                    nc.vector.tensor_tensor(x1_lo[i][:, c], x1_t[:, c], f32(x1_hi[i][:, c]),
                                            ALU.subtract).then_inc(x1_lo_done, 1)

            def x1_sum(i, h):
                dve.wait_ge(y_ready, 2 * i + h + 1)
                if i >= 1:
                    dve.wait_ge(x1_hi_done, 2 * (i - 1) + h + 1)
                    dve.wait_ge(x1_lo_done, 2 * (i - 1) + h + 1)
                for m in (2 * h, 2 * h + 1):
                    xt = x_t[:, i % 3].rearrange("p (n c q) -> p c n q", c=C, q=Q)[:, m]
                    y = bank[4 + h][:, 2 * S * (m % 2):2 * S * (m % 2 + 1)].rearrange("p (n q) -> p n q", q=Q)
                    last = nc.vector.scalar_tensor_tensor(x1_t[:, m].rearrange("p (n q) -> p n q", q=Q), y,
                                                          bias1_c[:, m:m + 1], xt, ALU.add, ALU.add)
                last.then_inc(x1_summed, 1)

            steps = [0]

            def masks():
                def step(ins):
                    steps[0] += 1
                    ins.then_inc(mask_step, 1)

                dve.wait_ge(iota_done, 1)
                step(nc.vector.tensor_copy(part_f[:], iota_i[:, 0:1]))
                step(nc.vector.tensor_copy(batch_f[:], iota_i[:, 1:1 + NB]))
                dve.wait_ge(ld["ids"], loads["ids"])
                step(nc.vector.tensor_copy(ids_f[:], ids_i[:]))
                dve.wait_ge(ld["starts"], loads["starts"])
                step(nc.vector.tensor_copy(starts_f[:], starts_i[:]))
                step(nc.vector.tensor_scalar(iota_i[:, 0:1], iota_i[:, 0:1], 4, None, ALU.logical_shift_right))
                dve.wait_ge(mask_step, steps[0])
                step(nc.vector.tensor_copy(group_f[:, 0:1], iota_i[:, 0:1]))
                step(nc.vector.tensor_scalar(group_f[:, 1:2], part_f[:], float(K0), float(-NL0), ALU.is_ge, ALU.mult))
                step(nc.vector.tensor_tensor(started[:], starts_f[:].unsqueeze(1).to_broadcast([P, NB, NL0 + 1]),
                                             batch_f[:].unsqueeze(2).to_broadcast([P, NB, NL0 + 1]), ALU.is_le))
                dve.wait_ge(mask_step, steps[0])
                step(nc.vector.tensor_reduce(seg_f[:], started[:], AX.X, ALU.add))
                step(nc.vector.scalar_tensor_tensor(group_f[:, 2:3], group_f[:, 0:1], 2.0, group_f[:, 1:2],
                                                    ALU.add, ALU.add))
                dve.wait_ge(mask_step, steps[0])
                nc.vector.tensor_scalar(mask0[:], seg_f[:], group_f[:, 2:3], None, ALU.is_equal)
                nc.vector.tensor_scalar(mask1[:], ids_f[:], group_f[:, 0:1], None,
                                        ALU.is_equal).then_inc(masks_done, 1)
                dve.wait_ge(masks_done, 1)

            dve.wait_ge(ld["b2c"], loads["b2c"])
            nc.vector.tensor_copy(b2_parts[:, :, 0], b2_c[:]).then_inc(b2_hi_done, 1)
            dve.wait_ge(b2_hi_done, 1)
            nc.vector.tensor_tensor(b2_parts[:, :, 1], b2_c[:], f32(b2_parts[:, :, 0]),
                                    ALU.subtract).then_inc(b2_lo_done, 1)
            w3_low(0)
            w3_low(1)
            w3_low(2)
            w3_low(3)
            dve.wait_ge(w3_lo_done, C)
            nc.vector.tensor_tensor(small[:, :, R:R + NE], f32(w1_hi[:, :, 0:NE]), f32(w1_lo[:, :, 0:NE]),
                                    ALU.add).then_inc(w3_small_done, 1)
            for c in (0, 2):
                dve.wait_ge(w2_hi_done, c + 1)
                nc.vector.tensor_tensor(w2_out(w_lo, c), w2_in(c), f32(w2_out(w_hi, c)),
                                        ALU.subtract).then_inc(w2_lo_done, 1)
            x_turn(0)
            masks()
            m_low(0)
            dve.wait_ge(b1_hi_done, 1)
            nc.vector.tensor_tensor(by_adapter(b1_lo), b1_row.rearrange("p n (c r) -> p c n r", c=C),
                                    f32(by_adapter(b1_hi)), ALU.subtract).then_inc(b1_lo_done, 1)
            w_turn(0)
            dve.wait_ge(small_hi_done, 1)
            nc.vector.tensor_tensor(small_parts[:, :, NS:2 * NS], small, f32(small_parts[:, :, 0:NS]),
                                    ALU.subtract).then_inc(small_lo_done, 1)
            w_low(0)
            x_turn(1)
            m_low(1)
            dve.wait_ge(ld["bias"], loads["bias"])
            dve.wait_ge(bias_ready, 1)
            nc.vector.tensor_tensor(bias_all[:], bank[6][:], bias_all[:], ALU.add).then_inc(bias_done, 1)
            m_low(2)
            w_turn(1)
            m_low(3)
            w1_turn()
            w_low(1)
            dve.wait_ge(bes_saved, 1)
            nc.vector.scalar_tensor_tensor(bes_f, bank[6][:, NS:2 * NS], s_c[:, 0:1], bes_f, ALU.mult,
                                           ALU.add).then_inc(bes_summed, 1)
            nc.vector.tensor_reduce(bias_small[:], bank[6][0:2 * NS, 2 * NS:2 * NS + 2], AX.X,
                                    ALU.add).then_inc(bsm_step, 1)
            dve.wait_ge(ld["b3"], loads["b3"])
            dve.wait_ge(bsm_step, 1)
            nc.vector.tensor_tensor(bias_small[R:R + NE], bias_small[R:R + NE], b3_c[R:R + NE],
                                    ALU.add).then_inc(bsm_step, 1)
            w_turn(2)
            dve.wait_ge(aet_ready, 1)
            aet = bank[2][:, 0:2 * C * NS].rearrange("p (c n) -> p c n", n=2 * NS)
            nc.vector.tensor_copy(ae_f, aet[:, :, 0:NS]).then_inc(aet_saved, 1)
            dve.wait_ge(aet_saved, 1)
            nc.vector.tensor_tensor(ae_f, aet[:, :, NS:], ae_f, ALU.add).then_inc(ae_summed, 1)
            w_low(2)
            dve.wait_ge(aux_hi, 1)
            nc.vector.tensor_tensor(a0_t[:, :, K0:2 * K0], bank[7][:, 0:C * K0].rearrange("p (c k) -> p c k", k=K0),
                                    f32(a0_t[:, :, 0:K0]), ALU.subtract).then_inc(aux_lo, 1)
            c0_low(0)
            c0_low(1)
            dve.wait_ge(aux_hi, 2)
            nc.vector.tensor_tensor(b0_lo[:].rearrange("k (m e q) -> k m e q", e=4, m=C),
                                    bank[6][0:2 * K0, :].rearrange("k (e m q) -> k m e q", e=4, m=C),
                                    f32(b0_hi[:]).rearrange("k (m e q) -> k m e q", e=4, m=C),
                                    ALU.subtract).then_inc(aux_lo, 1)
            w_turn(3)
            dve.wait_ge(ld["b1c"], loads["b1c"])
            for i in range(1, NP):
                if i >= 2:
                    w_turn(2 * i + 1)
                if i >= 2:
                    w_low(2 * i + 1)
                low0_low(i - 1)
                if i >= 2 and i + 1 < NP:
                    x_turn(i + 1)
                if i == 1:
                    x_turn(i + 1)
                    w_low(2 * i + 1, 1)
                    dve.wait_ge(aux_hi, 3)
                    nc.vector.tensor_tensor(a1_lo[:], bank[5][:].rearrange("p (c k) -> p c k", k=K1), f32(a1_hi[:]),
                                            ALU.subtract).then_inc(aux_lo, 1)
                if i + 1 < NP:
                    w_turn(2 * i + 2)
                if i >= 2:
                    low1_low(i - 2)
                if i == 2:
                    dve.wait_ge(bm_hi_done, 1)
                    for a in (1, 3):
                        at = slice(Q * a, Q * (a + 1))
                        nc.vector.tensor_tensor(bm_parts[at], bm4[at], f32(bm_parts[at]),
                                                ALU.subtract).then_inc(bm_done, 1)
                x1_sum(i - 1, 0)
                if i + 1 < NP:
                    w_low(2 * i + 2)
                c0_low(2 * i)
                if i == 1:
                    dve.wait_ge(bes_saved, 2)
                    nc.vector.tensor_tensor(bes[:, NS:2 * NS], bes_f, f32(bes[:, 0:NS]),
                                            ALU.subtract).then_inc(bes_done, 1)
                    dve.wait_ge(ae_saved, 2)
                    nc.vector.tensor_tensor(ae[:, :, NS:2 * NS], ae_f, f32(ae[:, :, 0:NS]),
                                            ALU.subtract).then_inc(ae_done, 1)
                x1_sum(i - 1, 1)
                c0_low(2 * i + 1)
            dve.wait_ge(bsm_step, 2)
            small_saved(0)
            small_saved(1)
            low0_low(NP - 1)
            low1_low(NP - 2)
            x1_sum(NP - 1, 0)
            x1_sum(NP - 1, 1)

            def small_sum(h):
                dve.wait_ge(zr_ready, h + 1)
                ps = bank[ZR_BANK[h]][:, 0:4 * 2 * NS].rearrange("p (b n) -> p b n", n=2 * NS)
                nc.vector.tensor_copy(zr[:, 4 * h:4 * h + 4], ps[:, :, 0:NS]).then_inc(zr_step, 1)
                dve.wait_ge(zr_step, h + 1)
                nc.vector.tensor_tensor(zr[:, 4 * h:4 * h + 4], ps[:, :, NS:2 * NS], zr[:, 4 * h:4 * h + 4],
                                        ALU.add).then_inc(zr_done, 1)

            x1_low(NP - 1)
            small_saved(2)
            low1_low(NP - 1)
            small_sum(0)
            small_saved(3)
            small_sum(1)
            dve.wait_ge(zr_done, 2)
            nc.vector.tensor_reduce(top[:], zr[:, :, R:NS].rearrange("p b (g e) -> p g b e", g=2), AX.XY, ALU.max,
                                    apply_absolute_value=True).then_inc(top_done, 1)
            dve.wait_ge(topt_ready, 1)
            nc.vector.tensor_reduce(r2[:, 0:1], bank[4][0:2, 0:S].rearrange("p (n two) -> p n two", two=2)[:, :, 1],
                                    AX.X, ALU.max).then_inc(r_step, 1)
            dve.wait_ge(r_step, 1)
            nc.vector.tensor_scalar(r2[:, 1:2], r2[:, 0:1], EPS, None, ALU.max).then_inc(r_step, 1)
            dve.wait_ge(r_step, 2)
            nc.vector.reciprocal(r2[:, 0:1], r2[:, 1:2]).then_inc(r_step, 1)
            dve.wait_ge(r_step, 3)
            nc.vector.tensor_scalar(r2d[:], ident[0:2, 0:2], r2[:, 0:1], GAMMA, ALU.mult, ALU.mult).then_inc(r_done, 1)
            dve.wait_ge(rb_ready, 1)
            nc.vector.tensor_copy(r_b[:], bank[4][:, S:S + 2]).then_inc(lg_step, 1)
            dve.wait_ge(lg_step, 1)
            nc.vector.tensor_scalar(lgd[:], zr[:, :, R + NE:NS], r_b[:, 1:2], None, ALU.mult).then_inc(lg_step, 1)
            dve.wait_ge(lg_step, 2)
            nc.vector.scalar_tensor_tensor(lg[:], zr[:, :, R:R + NE], r_b[:, 0:1], lgd[:], ALU.mult,
                                           ALU.add).then_inc(lg_step, 1)
            dve.wait_ge(lg_step, 3)
            for b in range(NB):
                last = nc.vector.max(mx[:, b], lg[:, b])
            last.then_inc(lg_step, 1)
            dve.wait_ge(lg_step, 4)
            nc.vector.tensor_tensor(sub[:, :, 0:NE], lg[:], mx[:, :, 0:1].to_broadcast([P, NB, NE]), ALU.subtract)
            nc.vector.tensor_tensor(sub[:, :, NE:NE + 1], mx[:, :, 1:2], mx[:, :, 0:1],
                                    ALU.subtract).then_inc(sub_done, 1)
            dve.wait_ge(ex_done, 1)
            nc.vector.tensor_reduce(tot[:, 0], ex[:, :, 0:NE], AX.X, ALU.add).then_inc(prob_step, 1)
            dve.wait_ge(prob_step, 1)
            nc.vector.reciprocal(tot[:, 1], tot[:, 0]).then_inc(prob_step, 1)
            dve.wait_ge(prob_step, 2)
            nc.vector.tensor_tensor(prob[:], ex[:], tot[:, 1].unsqueeze(2).to_broadcast([P, NB, NE + 1]),
                                    ALU.mult).then_inc(prob_step, 1)
            dve.wait_ge(prob_step, 3)
            nc.vector.tensor_tensor(gate[:], prob[:, :, 0:NE], prob[:, :, NE:NE + 1].to_broadcast([P, NB, NE]),
                                    ALU.subtract).then_inc(gate_in, 1)
            dve.wait_ge(gate_exp, 1)
            nc.vector.tensor_scalar(gate[:], gate[:], 1.0, None, ALU.add).then_inc(prob_step, 1)
            dve.wait_ge(prob_step, 4)
            nc.vector.reciprocal(gate[:], gate[:]).then_inc(prob_step, 1)
            dve.wait_ge(prob_step, 5)
            nc.vector.tensor_tensor(gate[:], gate[:], prob[:, :, 0:NE], ALU.mult).then_inc(prob_step, 1)
            dve.wait_ge(prob_step, 6)
            nc.vector.tensor_reduce(tot[:, 2], gate[:], AX.X, ALU.add).then_inc(prob_step, 1)
            dve.wait_ge(prob_step, 7)
            nc.vector.tensor_scalar(tot[:, 3], tot[:, 2], 1e-9, None, ALU.add).then_inc(prob_step, 1)
            dve.wait_ge(prob_step, 8)
            nc.vector.reciprocal(tot[:, 0], tot[:, 3]).then_inc(prob_step, 1)
            dve.wait_ge(prob_step, 9)
            nc.vector.tensor_tensor(wgt[:], gate[:], tot[:, 0].unsqueeze(2).to_broadcast([P, NB, NE]),
                                    ALU.mult).then_inc(wgt_done, 1)
            dve.wait_ge(wt_ready, 1)
            nc.vector.tensor_copy(w_tok.rearrange("p (n two) -> p n two", two=2),
                                  bank[5][0:NB * NE, 0:S].rearrange("p (n two) -> p n two", two=2)[:, :, 1:2]
                                  .to_broadcast([NB * NE, S // 2, 2])).then_inc(wt_done, 1)
            dve.wait_ge(pm_ready, 1)
            nc.vector.scalar_tensor_tensor(zp, bank[4][:, 256:256 + NB * R].rearrange("p (b r) -> p b r", r=R),
                                           SCALING, zr[:, :, 0:R], ALU.mult, ALU.mult).then_inc(zp_done, 1)
            dve.wait_ge(zp_done, 1)
            nc.vector.tensor_copy(zp_hi[:], zp).then_inc(zp_hi_done, 1)
            dve.wait_ge(zp_hi_done, 1)
            nc.vector.tensor_tensor(zs[:, :, 2:4, :], zp.unsqueeze(2).to_broadcast([P, NB, 2, R]),
                                    f32(zp_hi[:]).unsqueeze(2).to_broadcast([P, NB, 2, R]),
                                    ALU.subtract).then_inc(zs_lo_done, 1)
            for step in range(NB + 1):
                b, at = min(step, NB - 1), columns(step)
                dve.wait_ge(out_ready, step + 1)
                if b >= 4:
                    dve.wait_ge(out_stored[b % 4], 16)
                nc.vector.tensor_tensor(out_sb[:, b % 4, at], bank[OUT_BANK[step]][:, at], bias_all[:, at],
                                        ALU.add).then_inc(out_done, 1)

        @block.tensor
        def _(pe):
            mm = nc.tensor.matmul

            def product(o, parts, start=True, stop=True):
                for n, (st, mv) in enumerate(parts):
                    ins = mm(o, st, mv, start=start and n == 0, stop=stop and n == len(parts) - 1)
                return ins

            def three(hi, lo, mhi, mlo):
                return [(hi, mhi), (hi, mlo), (lo, mhi)]

            def wide(o, at, parts):
                for n, (st, mv) in enumerate(parts):
                    ins = mm(o[:, at:at + mv.shape[-1]], st, mv, start=n == 0, stop=n == len(parts) - 1)
                return ins

            def layer_a(b):
                i = b // 2
                if b >= 2:
                    pe.wait_ge(c0_saved, b - 1)
                else:
                    pe.wait_ge(m_lo_done, b + 1)
                pe.wait_ge(x_hi_done, i + 1)
                pe.wait_ge(x_lo_done, i + 1)
                for rows_in in (range(0, 1), range(1, 2)) if b in (2, 3) else (range(0, 2),):
                    pe.wait_ge(w_hi_done, 2 * b + rows_in.stop)
                    for h in rows_in:
                        pe.wait_ge((w_lo0_done, w_lo1_done)[h], b + 1)
                    at = slice(D // 2 * rows_in.start, D // 2 * rows_in.stop)
                    parts = []
                    for c in range(C):
                        parts += three(tok(x_hi[:, i % 2, c], b), tok(x_lo[:, i % 2, c], b),
                                       w_hi[:, b % 2, c, at], w_lo[:, b % 2, c, at])
                    last = product(bank[b % 2][:, at], parts)
                last.then_inc(c0_ready, 1)

            def turn_c0(b):
                pe.wait_ge(c0_saved, b + 1)
                if b >= 2:
                    pe.wait_ge(c0t_lo_done, b - 1)
                elif b == 1:
                    pe.wait_ge(m_lo_done, C)
                else:
                    pe.wait_ge(ae_summed, 1)
                for c in range(C):
                    last = nc.tensor.transpose(bank[2 + b % 2][:, S * c:S * (c + 1)], chunk(c0_row[:, b % 2], c),
                                               ident[:])
                last.then_inc(c0t_ready, 1)

            def low0(i):
                pe.wait_ge(c0t_lo_done, 2 * i + 2)
                if i >= 1:
                    pe.wait_ge(low0_lo_done, i)
                else:
                    pe.wait_ge(aux_lo, 2)
                parts = []
                for c in range(C):
                    parts += [(a0_t[:, c], c0_hi[:, i % 2, c]), (a0_t[:, c], c0_lo[:, i % 2, c])]
                product(bank[6][0:2 * K0, 0:2 * S], parts).then_inc(low0_ready, 1)

            def layer_b(i, h):
                if i >= 1:
                    pe.wait_ge(x1_summed, 2 * (i - 1) + h + 1)
                else:
                    pe.wait_ge(w1_hi_done, 4)
                    pe.wait_ge(w1_lo_done, 4)
                    if h == 0:
                        pe.wait_ge(small_done, 1)
                    else:
                        pe.wait_ge(aux_lo, 3)
                for m in (2 * h, 2 * h + 1):
                    o = bank[4 + h][:, 2 * S * (m % 2):2 * S * (m % 2 + 1)]
                    parts = []
                    for c in range(C):
                        parts += three(chunk(w1_hi[:, c], m), chunk(w1_lo[:, c], m),
                                       c0_hi[:, i % 2, c], c0_lo[:, i % 2, c])
                    product(o, parts, stop=False)
                    pe.wait_ge(low0_lo_done, i + 1)
                    last = product(o, three(chunk(b0_hi[:], m), chunk(b0_lo[:], m), low0_hi[:], low0_lo[:]),
                                   start=False)
                last.then_inc(y_ready, 1)

            def low1(i):
                pe.wait_ge(x1_lo_done, 2 * i + 2)
                if i >= 1:
                    pe.wait_ge(low1_lo_done, i)
                else:
                    pe.wait_ge(aux_lo, 3)
                parts = []
                for c in range(C):
                    parts += three(a1_hi[:, c], a1_lo[:, c], x1_hi[i][:, c], x1_lo[i][:, c])
                product(bank[7][:, 0:2 * S], parts).then_inc(low1_ready, 1)

            pe.wait_ge(ident_done, 1)
            for t in range(C):
                pe.wait_ge(w3_landed[t], 16)
                for c in range(C):
                    o = bank[t // 2 * 2 + c // 2][:, 2 * P * (c % 2) + P * (t % 2):]
                    last = nc.tensor.transpose(o[:, 0:P], w_in[:, w_slot("w3")[0], D * t + c:D * (t + 1):C], ident[:])
                    if t % 2 == 1 and c % 2 == 1:
                        last.then_inc(w3t_ready, 1)
            pe.wait_ge(b2_lo_done, 1)
            for h in range(2):
                at = slice(D // 2 * h, D // 2 * (h + 1))
                for c in range(C):
                    pe.wait_ge(w3_lo_done, 2 * h + c // 2 + 1)
                    hi, lo = (b2_parts[:, c, k:k + 1].to_broadcast([P, P]) for k in (0, 1))
                    last = product(bank[6][:, at], three(hi, lo, w1_hi[:, c, at], w1_lo[:, c, at]), start=c == 0,
                                   stop=c == C - 1)
            last.then_inc(bias_ready, 1)
            pe.wait_ge(ident_r_done, 1)
            for m in range(C):
                o = bank[M_BANK[m]]
                for c in range(C):
                    pe.wait_ge(w2_lo_pool if c % 2 else w2_lo_done, c // 2 + 1)
                    product(o[:], three(chunk(w_hi[:, 1, c], m), chunk(w_lo[:, 1, c], m), w1_hi[:, c], w1_lo[:, c]),
                            start=c == 0, stop=False)
                mm(o[:].rearrange("p (a m q) -> p m a q", a=4, m=C)[:, m], ident_r[:],
                   ident_r[:].rearrange("p (a q) -> p a q", a=4), start=False, stop=True).then_inc(m_ready, 1)
                if m == 0:
                    pe.wait_ge(ld["A"], loads["A"])
                    for c in range(C):
                        last = nc.tensor.transpose(bank[4][0:R, P * c:P * (c + 1)], small[:, c, 0:R], ident[:])
                    last.then_inc(at_ready, 1)
                elif m == 1:
                    pe.wait_ge(at_saved, 1)
                    pe.wait_ge(ld["l"], loads["l"])
                    for c in range(C):
                        last = mm(bank[4][:, NE * c:NE * (c + 1)], a_t[:, c], l_t[:], start=True, stop=True)
                    last.then_inc(al_ready, 1)
            pe.wait_ge(small_lo_done, 1)
            parts = []
            for c in range(C):
                parts += [(small_parts[:, c], w_hi[:, 1, c]), (small_parts[:, c], w_lo[:, 1, c])]
            product(bank[5][0:2 * NS, :], parts).then_inc(ae_ready, 1)
            pe.wait_ge(bias_done, 1)
            pe.wait_ge(b1_lo_done, 1)
            parts = []
            for c in range(C):
                parts += [(b1_hi[:, c], small_parts[:, c]), (b1_lo[:, c], small_parts[:, c, 0:NS])]
            wide(bank[6], 0, parts)
            product(bank[6][0:2 * NS, 2 * NS:2 * NS + 2],
                    [(small_parts[:, c], b2_parts[:, c]) for c in range(C)]).then_inc(smalls_ready, 1)
            parts = []
            for c in range(C):
                parts += three(b1_hi[:, c], b1_lo[:, c], w1_hi[:, c], w1_lo[:, c])
            product(bank[7][:], parts).then_inc(be_ready, 1)
            layer_a(0)
            pe.wait_ge(ae_saved, 1)
            pe.wait_ge(m_lo_done, 3)
            for c in range(C):
                last = nc.tensor.transpose(bank[2][:, 2 * NS * c:2 * NS * (c + 1)], chunk(ae_rows, c),
                                           ident[0:2 * NS, 0:2 * NS])
            last.then_inc(aet_ready, 1)

            pe.wait_ge(ld["a0"], loads["a0"])
            pe.wait_ge(be_scaled, 1)
            for c in range(C):
                last = nc.tensor.transpose(bank[7][:, K0 * c:K0 * (c + 1)], chunk(a0_row, c), ident[0:K0, 0:K0])
            last.then_inc(aux_ready, 1)
            pe.wait_ge(rows_ready, 1)
            pe.wait_ge(bsm_step, 1)
            for c in range(C):
                last = nc.tensor.transpose(bank[6][0:2 * K0, P * c:P * (c + 1)],
                                           b0_row[:, c].rearrange("p g k -> p (g k)"), ident[:])
            last.then_inc(aux_ready, 1)
            layer_a(1)
            turn_c0(0)
            pe.wait_ge(ld["a1"], loads["a1"])
            for c in range(C):
                last = nc.tensor.transpose(bank[5][:, K1 * c:K1 * (c + 1)], chunk(a1_row, c), ident[:])
            last.then_inc(aux_ready, 1)
            turn_c0(1)
            for i in range(1, NP):
                layer_a(2 * i)
                low0(i - 1)
                if i >= 2:
                    low1(i - 2)
                layer_b(i - 1, 0)
                turn_c0(2 * i)
                layer_a(2 * i + 1)
                layer_b(i - 1, 1)
                turn_c0(2 * i + 1)
            def small_outputs(i):
                parts = []
                for c in range(C):
                    parts += [(ae[:, c], x1_hi[i][:, c]), (ae[:, c], x1_lo[i][:, c])]
                parts += [(bes[:], t[:, 2 * i:2 * i + 2].rearrange("p b s -> p (b s)")) for t in (low1_hi, low1_lo)]
                pe.wait_ge(low1_lo_done, i + 1)
                product(bank[ZT_BANK[i]][0:2 * NS, 0:2 * S], parts).then_inc(zt_ready, 1)

            def turn_small(i):
                pe.wait_ge(zt_saved, i + 1)
                for b in (2 * i, 2 * i + 1):
                    at = 2 * NS * (b % 4)
                    last = nc.tensor.transpose(bank[ZR_BANK[b // 4]][:, at:at + 2 * NS], z_t[:, S * b:S * (b + 1)],
                                               ident[0:2 * NS, 0:2 * NS])
                if i % 2 == 1:
                    last.then_inc(zr_ready, 1)

            def second_layer(b, chunks=range(C), step=None):
                i = b // 2
                o, at = OUT_BANK[b if step is None else step], columns(b if step is None else step)
                parts = []
                for c in chunks:
                    parts += three(tok(x1_hi[i][:, c], b), tok(x1_lo[i][:, c], b), m_hi[:, c, at], m_lo[:, c, at])
                if C - 1 in chunks:
                    parts += three(low1_hi[:, b], low1_lo[:, b], be_hi[:, at], be_lo[:, at])
                product(bank[o][:, at], parts, start=0 in chunks, stop=False)

            def routed(b, step=None):
                o, at = OUT_BANK[b if step is None else step], columns(b if step is None else step)
                product(bank[o][:, at], [(z_parts[:, b], bm_parts[:, at])], start=False).then_inc(out_ready, 1)

            pe.wait_ge(ae_done, 1)
            pe.wait_ge(bes_done, 1)
            pe.wait_ge(c0_saved, NB)
            small_outputs(0)
            small_outputs(1)
            low0(NP - 1)
            low1(NP - 2)
            layer_b(NP - 1, 0)
            layer_b(NP - 1, 1)
            pe.wait_ge(x1_summed, 2 * NP - 1)
            small_outputs(2)
            pe.wait_ge(low0_lo_done, NP)
            turn_small(0)
            turn_small(1)
            pe.wait_ge(be_done, 1)
            second_layer(0, range(0, 2))
            low1(NP - 1)
            second_layer(0, range(2, C))
            pe.wait_ge(x1_summed, 2 * NP)
            small_outputs(3)
            second_layer(1, range(0, 1))
            pe.wait_ge(c0t_lo_done, NB)
            turn_small(2)
            turn_small(3)
            second_layer(1, range(1, 3))
            pe.wait_ge(top_done, 1)
            nc.tensor.transpose(bank[4][0:2, 0:S], top[:], ident[:]).then_inc(topt_ready, 1)
            second_layer(1, range(3, C))
            pe.wait_ge(r_done, 1)
            pe.wait_ge(ones_done, 1)
            mm(bank[4][:, S:S + 2], ones2[:], r2d[:], start=True, stop=True).then_inc(rb_ready, 1)
            second_layer(2)
            second_layer(3)
            pe.wait_ge(wgt_done, 1)
            nc.tensor.transpose(bank[5][0:NB * NE, 0:S], wgt[:].rearrange("p b e -> p (b e)"),
                                ident[:]).then_inc(wt_ready, 1)
            second_layer(4, range(0, 1))
            pe.wait_ge(wt_done, 1)
            pe.wait_ge(ldiag_step, 2)
            mm(bank[4][:, 256:256 + NB * R], w_tok, l_diag[:].rearrange("k b r -> k (b r)"), start=True,
               stop=True).then_inc(pm_ready, 1)
            second_layer(4, range(1, C))
            pe.wait_ge(zs_hi_done, 1)
            pe.wait_ge(zs_lo_done, 1)
            for b in range(NB):
                last = nc.tensor.transpose(bank[4 + b // 4][:, S * (b % 4):S * (b % 4 + 1)],
                                           zs[:, b].rearrange("p g r -> p (g r)"), ident[:])
                if b % 4 == 3:
                    last.then_inc(zst_ready, 1)
            second_layer(5)
            pe.wait_ge(zst_saved, 2)
            pe.wait_ge(bm_done, 2)
            for b in range(6):
                routed(b)
            for step in range(6, NB + 1):
                pe.wait_ge(out_done, OUT_BANK.index(OUT_BANK[step]) + 1)
                second_layer(min(step, NB - 1), step=step)
                routed(min(step, NB - 1), step)


M_BANK = [0, 1, 2, 3]
ZT_BANK = [0, 1, 4, 5]
ZR_BANK = [6, 2]
OUT_BANK = [0, 1, 3, 2, 7, 6, 0, 1, 3]

_INS = ["x", "itok_B_3_7", "itok_B_1_7", "L0_cond_weight", "L0_ffn_weight", "L0_ffn_bias", "L0_ffn_lora_A",
        "L0_ffn_lora_B", "L0_ffn_lora_start_indices", "L1_cond_weight", "L1_cond_bias", "L1_cond_lora_a_weights",
        "L1_cond_lora_b_weights", "L1_cond_scaling_factors", "L1_ffn_W", "L1_ffn_b", "L1_ffn_A", "L1_ffn_Bmat",
        "L1_ffn_LiMEs"]


def kernel(**inputs):
    import numpy as np
    from concourse import bacc
    from concourse.bass_utils import run_bass_kernel_spmd

    nc = bacc.Bacc("TRN2", target_bir_lowering=False, num_devices=1)
    arrays, args = {}, []
    for name in _INS:
        a = np.ascontiguousarray(inputs[name])
        if name == "itok_B_3_7":
            a = a.reshape(1, -1)
        arrays["in_" + name] = a
        args.append(nc.dram_tensor("in_" + name, a.shape, mybir.dt.from_np(a.dtype), kind="ExternalInput").ap())
    shape = inputs["x"].shape
    args.append(nc.dram_tensor("out_dram", shape, F32, kind="ExternalOutput").ap())
    build(nc, *args)
    r = run_bass_kernel_spmd(nc, [arrays], core_ids=[0])
    return r.results[0]["out_dram"]
```
